# Optimizing a Trainium2 kernel written in Bass

```python
import numpy as np
import jax
import jax.numpy as jnp

def _softmax(x, axis=-1):
    return jax.nn.softmax(x, axis=axis)

def _gelu(x):
    return jax.nn.gelu(x, approximate=True)

def _silu(x):
    return jax.nn.silu(x)

def _sigmoid(x):
    return jax.nn.sigmoid(x)

def _layernorm(x, axis=-1, eps=1e-05):
    m = jnp.mean(x, axis=axis, keepdims=True)
    v = jnp.var(x, axis=axis, keepdims=True)
    return (x - m) / jnp.sqrt(v + eps)

def _scatter_add(tgt, idx, src, axis=0):
    return tgt.at[idx].add(src)

def _segment_sum(src, seg, n):
    return jax.ops.segment_sum(src, seg, n)
kernel_name = 'mk_gps_d2_gnn_r32_5d79d9'

def setup_inputs(seed: int=0):
    np.random.seed(seed)
    _w = jnp.asarray

    def _rec_inputs():
        import jax
        import jax.numpy as jnp
        _gk = jax.random.key(seed)
        x = -0.0003713 + 1 * jax.random.normal(jax.random.fold_in(_gk, 1), (3125, 256), jnp.float32)
        src = jax.random.randint(jax.random.fold_in(_gk, 2), (50000,), 0, 3125, jnp.int32)
        dst = jnp.minimum((3125 * jax.random.uniform(jax.random.fold_in(_gk, 3), (50000,)) ** 2.0).astype(jnp.int32), 99999)
        _o = jnp.argsort(dst, stable=True)
        src = src[_o]
        dst = dst[_o]
        return (x, src, dst)
    x, src, dst = _rec_inputs()

    def _L0_gnn_setup():
        import jax, jax.numpy as jnp
        import numpy as np
        N_NODES = 50000
        N_EDGES = 50000
        H_SIZE = 256
        HEADS = 8
        HEAD_DIM = H_SIZE // HEADS
        NEG_SLOPE = 0.2
        key = jax.random.key(seed)
        k_x, k_e, k_w, k_as, k_ad, k_b = jax.random.split(key, 6)
        x = jax.random.normal(k_x, (N_NODES, H_SIZE), dtype=jnp.float32)
        edge_index = jax.random.randint(k_e, (2, N_EDGES), 0, N_NODES, dtype=jnp.int64)
        scale = 1.0 / np.sqrt(H_SIZE)
        W = jax.random.normal(k_w, (H_SIZE, HEADS, HEAD_DIM), dtype=jnp.float32) * scale
        att_src = jax.random.normal(k_as, (HEADS, HEAD_DIM), dtype=jnp.float32) * scale
        att_dst = jax.random.normal(k_ad, (HEADS, HEAD_DIM), dtype=jnp.float32) * scale
        bias = jnp.zeros((H_SIZE,), dtype=jnp.float32)
        return {'x': x, 'edge_index': edge_index, 'W': W, 'att_src': att_src, 'att_dst': att_dst, 'bias': bias}
    _L0_gnn_all = _L0_gnn_setup()
    _L0_gnn_in = {k: v for k, v in _L0_gnn_all.items() if k in ('W', 'att_src', 'att_dst', 'bias')}
    del _L0_gnn_all

    def _L0_mix_setup():
        import jax, jax.numpy as jnp
        import numpy as np
        N, F, C, H = (32, 128, 256, 8)
        D = C // H
        EPS_ATTN = 1e-06
        EPS_LN = 1e-05

        def layer_norm(x, g, b):
            mu = jnp.mean(x, axis=-1, keepdims=True)
            var = jnp.var(x, axis=-1, keepdims=True)
            return (x - mu) * jax.lax.rsqrt(var + EPS_LN) * g + b
        key = jax.random.key(seed)
        ks = jax.random.split(key, 8)
        s = 1.0 / np.sqrt(C)
        return {'x': jax.random.normal(ks[0], (N, F, C), jnp.float32), 'Wqkv': jax.random.uniform(ks[1], (3 * C, C), jnp.float32, -s, s), 'ln1_g': jnp.ones((C,), jnp.float32), 'ln1_b': jnp.zeros((C,), jnp.float32), 'W1': jax.random.uniform(ks[2], (C, C), jnp.float32, -s, s), 'b1': jax.random.uniform(ks[3], (C,), jnp.float32, -s, s), 'W2': jax.random.uniform(ks[4], (C, C), jnp.float32, -s, s), 'b2': jax.random.uniform(ks[5], (C,), jnp.float32, -s, s), 'ln2_g': jnp.ones((C,), jnp.float32), 'ln2_b': jnp.zeros((C,), jnp.float32)}
    _L0_mix_all = _L0_mix_setup()
    _L0_mix_in = {k: v for k, v in _L0_mix_all.items() if k in ('Wqkv', 'ln1_g', 'ln1_b', 'W1', 'b1', 'W2', 'b2', 'ln2_g', 'ln2_b')}
    del _L0_mix_all

    def _L0_ffn_setup():
        import jax, jax.numpy as jnp
        import numpy as np
        B, S, D, H, E, K = (8, 256, 256, 1024, 8, 2)
        key = jax.random.key(seed)
        ks = jax.random.split(key, 7)
        s_in = 1.0 / np.sqrt(D)
        s_hid = 1.0 / np.sqrt(H)
        return {'x': jax.random.normal(ks[0], (B, S, D), dtype=jnp.float32), 'Wg': jax.random.uniform(ks[1], (E, D), jnp.float32, -s_in, s_in), 'bg': jax.random.uniform(ks[2], (E,), jnp.float32, -s_in, s_in), 'W1': jax.random.uniform(ks[3], (E, H, D), jnp.float32, -s_in, s_in), 'b1': jax.random.uniform(ks[4], (E, H), jnp.float32, -s_in, s_in), 'W2': jax.random.uniform(ks[5], (E, D, H), jnp.float32, -s_hid, s_hid), 'b2': jax.random.uniform(ks[6], (E, D), jnp.float32, -s_hid, s_hid)}
    _L0_ffn_all = _L0_ffn_setup()
    _L0_ffn_in = {k: v for k, v in _L0_ffn_all.items() if k in ('Wg', 'bg', 'W1', 'b1', 'W2', 'b2')}
    del _L0_ffn_all

    def _L1_gnn_setup():
        import jax, jax.numpy as jnp
        import numpy as np
        N, DIM, H, C, E = (50000, 256, 4, 64, 25000)
        NEG_SLOPE = 0.2
        LN_EPS = 1e-05
        key = jax.random.key(seed)
        ks = jax.random.split(key, 8)
        x = jax.random.normal(ks[0], (N, DIM), dtype=jnp.float32)
        edge_index = jax.random.randint(ks[1], (2, E), 0, N, dtype=jnp.int64)
        W = jax.random.normal(ks[2], (DIM, H * C), dtype=jnp.float32) * (1.0 / np.sqrt(DIM))
        a_src = jax.random.normal(ks[3], (H, C), dtype=jnp.float32) * (1.0 / np.sqrt(C))
        a_dst = jax.random.normal(ks[4], (H, C), dtype=jnp.float32) * (1.0 / np.sqrt(C))
        bias_gat = jnp.zeros((DIM,), dtype=jnp.float32)
        W_res = jax.random.normal(ks[5], (DIM, DIM), dtype=jnp.float32) * (1.0 / np.sqrt(DIM))
        b_res = jnp.zeros((DIM,), dtype=jnp.float32)
        gamma = jnp.ones((DIM,), dtype=jnp.float32)
        beta = jnp.zeros((DIM,), dtype=jnp.float32)
        return {'x': x, 'edge_index': edge_index, 'W': W, 'a_src': a_src, 'a_dst': a_dst, 'bias_gat': bias_gat, 'W_res': W_res, 'b_res': b_res, 'gamma': gamma, 'beta': beta}
    _L1_gnn_all = _L1_gnn_setup()
    _L1_gnn_in = {k: v for k, v in _L1_gnn_all.items() if k in ('W', 'a_src', 'a_dst', 'bias_gat', 'W_res', 'b_res', 'gamma', 'beta')}
    del _L1_gnn_all

    def _L1_mix_setup():
        import jax, jax.numpy as jnp
        import numpy as np
        NHEAD = 8
        ATT_EPS = 1e-06
        LN_EPS = 1e-05

        def _layernorm(x, g, b):
            mu = jnp.mean(x, axis=-1, keepdims=True)
            var = jnp.mean(jnp.square(x - mu), axis=-1, keepdims=True)
            return (x - mu) * jax.lax.rsqrt(var + LN_EPS) * g + b
        key = jax.random.key(seed)
        ks = jax.random.split(key, 7)
        N, L, C = (4, 512, 256)
        s = 1.0 / np.sqrt(C)
        return {'x': jax.random.normal(ks[0], (N, L, C), jnp.float32), 'Wq': jax.random.normal(ks[1], (C, C), jnp.float32) * s, 'Wk': jax.random.normal(ks[2], (C, C), jnp.float32) * s, 'Wv': jax.random.normal(ks[3], (C, C), jnp.float32) * s, 'Wm': jax.random.normal(ks[4], (C, C), jnp.float32) * s, 'W1': jax.random.normal(ks[5], (2 * C, 2 * C), jnp.float32) * (1.0 / np.sqrt(2 * C)), 'W2': jax.random.normal(ks[6], (2 * C, C), jnp.float32) * (1.0 / np.sqrt(2 * C)), 'g1': jnp.ones((C,), jnp.float32), 'b1': jnp.zeros((C,), jnp.float32), 'g2': jnp.ones((C,), jnp.float32), 'b2': jnp.zeros((C,), jnp.float32)}
    _L1_mix_all = _L1_mix_setup()
    _L1_mix_in = {k: v for k, v in _L1_mix_all.items() if k in ('Wq', 'Wk', 'Wv', 'Wm', 'W1', 'W2', 'g1', 'b1', 'g2', 'b2')}
    del _L1_mix_all

    def _L1_ffn_setup():
        import jax, jax.numpy as jnp
        import numpy as np
        B, K, D = (512, 16, 256)
        E = 32
        H = int(D * 0.25)
        key = jax.random.key(seed)
        ks = jax.random.split(key, 7)
        d_rs = D ** (-0.5)
        h_rs = H ** (-0.5)
        x = jax.random.normal(ks[0], (B, K, D), dtype=jnp.float32)
        router_w = jax.random.uniform(ks[1], (E, D), jnp.float32, -d_rs, d_rs)
        router_b = jax.random.uniform(ks[2], (E,), jnp.float32, -d_rs, d_rs)
        W1 = jax.random.uniform(ks[3], (E, D, H), jnp.float32, -h_rs, h_rs)
        b1 = jax.random.uniform(ks[4], (E, H), jnp.float32, -h_rs, h_rs)
        W2 = jax.random.uniform(ks[5], (E, H, D), jnp.float32, -d_rs, d_rs)
        b2 = jax.random.uniform(ks[6], (E, D), jnp.float32, -d_rs, d_rs)
        return {'x': x, 'router_w': router_w, 'router_b': router_b, 'W1': W1, 'b1': b1, 'W2': W2, 'b2': b2}
    _L1_ffn_all = _L1_ffn_setup()
    _L1_ffn_in = {k: v for k, v in _L1_ffn_all.items() if k in ('router_w', 'router_b', 'W1', 'b1', 'W2', 'b2')}
    del _L1_ffn_all
    return {'x': x, 'src': src, 'dst': dst, 'L0_gnn_W': _L0_gnn_in['W'], 'L0_gnn_att_src': _L0_gnn_in['att_src'], 'L0_gnn_att_dst': _L0_gnn_in['att_dst'], 'L0_gnn_bias': _L0_gnn_in['bias'], 'L0_mix_Wqkv': _L0_mix_in['Wqkv'], 'L0_mix_ln1_g': _L0_mix_in['ln1_g'], 'L0_mix_ln1_b': _L0_mix_in['ln1_b'], 'L0_mix_W1': _L0_mix_in['W1'], 'L0_mix_b1': _L0_mix_in['b1'], 'L0_mix_W2': _L0_mix_in['W2'], 'L0_mix_b2': _L0_mix_in['b2'], 'L0_mix_ln2_g': _L0_mix_in['ln2_g'], 'L0_mix_ln2_b': _L0_mix_in['ln2_b'], 'L0_ffn_Wg': _L0_ffn_in['Wg'], 'L0_ffn_bg': _L0_ffn_in['bg'], 'L0_ffn_W1': _L0_ffn_in['W1'], 'L0_ffn_b1': _L0_ffn_in['b1'], 'L0_ffn_W2': _L0_ffn_in['W2'], 'L0_ffn_b2': _L0_ffn_in['b2'], 'L1_gnn_W': _L1_gnn_in['W'], 'L1_gnn_a_src': _L1_gnn_in['a_src'], 'L1_gnn_a_dst': _L1_gnn_in['a_dst'], 'L1_gnn_bias_gat': _L1_gnn_in['bias_gat'], 'L1_gnn_W_res': _L1_gnn_in['W_res'], 'L1_gnn_b_res': _L1_gnn_in['b_res'], 'L1_gnn_gamma': _L1_gnn_in['gamma'], 'L1_gnn_beta': _L1_gnn_in['beta'], 'L1_mix_Wq': _L1_mix_in['Wq'], 'L1_mix_Wk': _L1_mix_in['Wk'], 'L1_mix_Wv': _L1_mix_in['Wv'], 'L1_mix_Wm': _L1_mix_in['Wm'], 'L1_mix_W1': _L1_mix_in['W1'], 'L1_mix_W2': _L1_mix_in['W2'], 'L1_mix_g1': _L1_mix_in['g1'], 'L1_mix_b1': _L1_mix_in['b1'], 'L1_mix_g2': _L1_mix_in['g2'], 'L1_mix_b2': _L1_mix_in['b2'], 'L1_ffn_router_w': _L1_ffn_in['router_w'], 'L1_ffn_router_b': _L1_ffn_in['router_b'], 'L1_ffn_W1': _L1_ffn_in['W1'], 'L1_ffn_b1': _L1_ffn_in['b1'], 'L1_ffn_W2': _L1_ffn_in['W2'], 'L1_ffn_b2': _L1_ffn_in['b2']}

def reference(x, src, dst, L0_gnn_W, L0_gnn_att_src, L0_gnn_att_dst, L0_gnn_bias, L0_mix_Wqkv, L0_mix_ln1_g, L0_mix_ln1_b, L0_mix_W1, L0_mix_b1, L0_mix_W2, L0_mix_b2, L0_mix_ln2_g, L0_mix_ln2_b, L0_ffn_Wg, L0_ffn_bg, L0_ffn_W1, L0_ffn_b1, L0_ffn_W2, L0_ffn_b2, L1_gnn_W, L1_gnn_a_src, L1_gnn_a_dst, L1_gnn_bias_gat, L1_gnn_W_res, L1_gnn_b_res, L1_gnn_gamma, L1_gnn_beta, L1_mix_Wq, L1_mix_Wk, L1_mix_Wv, L1_mix_Wm, L1_mix_W1, L1_mix_W2, L1_mix_g1, L1_mix_b1, L1_mix_g2, L1_mix_b2, L1_ffn_router_w, L1_ffn_router_b, L1_ffn_W1, L1_ffn_b1, L1_ffn_W2, L1_ffn_b2):
    import jax
    import jax.numpy as jnp

    def _L0_gnn_ref(x, edge_index, W, att_src, att_dst, bias):
        import jax, jax.numpy as jnp
        import numpy as np
        N_NODES = 50000
        N_EDGES = 50000
        H_SIZE = 256
        HEADS = 8
        HEAD_DIM = H_SIZE // HEADS
        NEG_SLOPE = 0.2
        'GATConv (concat heads) -> relu -> dropout(eval=identity).\n\n            x: [N, F]; edge_index: [2, E] with (src=row0, dst=row1) meaning message j->i.\n            '
        N = x.shape[0]
        h = jnp.einsum('nf,fhd->nhd', x, W)
        a_src = jnp.sum(h * att_src, axis=-1)
        a_dst = jnp.sum(h * att_dst, axis=-1)
        src = edge_index[0]
        dst = edge_index[1]
        e = jax.nn.leaky_relu(a_src[src] + a_dst[dst], NEG_SLOPE)
        e_max = jax.ops.segment_max(e, dst, num_segments=N)
        e_exp = jnp.exp(e - e_max[dst])
        denom = jax.ops.segment_sum(e_exp, dst, num_segments=N)
        alpha = e_exp / (denom[dst] + 1e-16)
        msg = h[src] * alpha[:, :, None]
        out = jax.ops.segment_sum(msg, dst, num_segments=N)
        out = out.reshape(N, -1) + bias
        return jax.nn.relu(out)

    def _L0_mix_ref(x, Wqkv, ln1_g, ln1_b, W1, b1, W2, b2, ln2_g, ln2_b):
        import jax, jax.numpy as jnp
        import numpy as np
        N, F, C, H = (32, 128, 256, 8)
        D = C // H
        EPS_ATTN = 1e-06
        EPS_LN = 1e-05

        def layer_norm(x, g, b):
            mu = jnp.mean(x, axis=-1, keepdims=True)
            var = jnp.var(x, axis=-1, keepdims=True)
            return (x - mu) * jax.lax.rsqrt(var + EPS_LN) * g + b
        n, f, c = x.shape
        qkv = jnp.einsum('nfc,oc->nfo', x, Wqkv)
        q, k, v = jnp.split(qkv, 3, axis=-1)
        q = q.reshape(n, f, H, D)
        k = k.reshape(n, f, H, D)
        v = v.reshape(n, f, H, D)
        q = jax.nn.elu(q) + 1.0
        k = jax.nn.elu(k) + 1.0
        kv = jnp.einsum('nshd,nshm->nhmd', k, v)
        ksum = jnp.sum(k, axis=1)
        z = 1.0 / (jnp.einsum('nlhd,nhd->nlh', q, ksum) + EPS_ATTN)
        t = jnp.einsum('nlhd,nhmd,nlh->nlhm', q, kv, z)
        t = t.reshape(n, f, c)
        x1 = layer_norm(t + x, ln1_g, ln1_b)
        h = jax.nn.gelu(jnp.einsum('nfc,oc->nfo', x1, W1) + b1, approximate=False)
        y = jnp.einsum('nfc,oc->nfo', h, W2) + b2
        return layer_norm(y + x1, ln2_g, ln2_b)

    def _L0_ffn_ref(x, Wg, bg, W1, b1, W2, b2):
        import jax, jax.numpy as jnp
        import numpy as np
        B, S, D, H, E, K = (8, 256, 256, 1024, 8, 2)
        gate_scores = jnp.einsum('bsd,ed->bse', x, Wg) + bg
        topk_scores, topk_idx = jax.lax.top_k(gate_scores, K)
        topk_probs = jax.nn.softmax(topk_scores, axis=-1)
        combine = jnp.sum(topk_probs[..., None] * jax.nn.one_hot(topk_idx, E, dtype=x.dtype), axis=-2)
        out = jnp.zeros_like(x)
        for e in range(E):
            h = jax.nn.relu(jnp.einsum('bsd,hd->bsh', x, W1[e]) + b1[e])
            y = jnp.einsum('bsh,dh->bsd', h, W2[e]) + b2[e]
            out = out + combine[..., e:e + 1] * y
        return out

    def _L1_gnn_ref(x, edge_index, W, a_src, a_dst, bias_gat, W_res, b_res, gamma, beta):
        import jax, jax.numpy as jnp
        import numpy as np
        N, DIM, H, C, E = (50000, 256, 4, 64, 25000)
        NEG_SLOPE = 0.2
        LN_EPS = 1e-05
        n = x.shape[0]
        loops = jnp.arange(n, dtype=edge_index.dtype)
        src = jnp.concatenate([edge_index[0], loops])
        dst = jnp.concatenate([edge_index[1], loops])
        h = (x @ W).reshape(n, H, C)
        al_src = jnp.einsum('nhc,hc->nh', h, a_src)
        al_dst = jnp.einsum('nhc,hc->nh', h, a_dst)
        e = jax.nn.leaky_relu(al_src[src] + al_dst[dst], NEG_SLOPE)
        emax = jax.ops.segment_max(e, dst, num_segments=n)
        ee = jnp.exp(e - emax[dst])
        denom = jax.ops.segment_sum(ee, dst, num_segments=n)
        alpha = ee / (denom[dst] + 1e-16)
        msg = h[src] * alpha[:, :, None]
        out = jax.ops.segment_sum(msg, dst, num_segments=n)
        out = out.reshape(n, H * C) + bias_gat
        y = out + x @ W_res + b_res
        mu = jnp.mean(y, axis=-1, keepdims=True)
        var = jnp.mean((y - mu) ** 2, axis=-1, keepdims=True)
        return gamma * (y - mu) * jax.lax.rsqrt(var + LN_EPS) + beta

    def _L1_mix_ref(x, Wq, Wk, Wv, Wm, W1, W2, g1, b1, g2, b2):
        import jax, jax.numpy as jnp
        import numpy as np
        NHEAD = 8
        ATT_EPS = 1e-06
        LN_EPS = 1e-05

        def _layernorm(x, g, b):
            mu = jnp.mean(x, axis=-1, keepdims=True)
            var = jnp.mean(jnp.square(x - mu), axis=-1, keepdims=True)
            return (x - mu) * jax.lax.rsqrt(var + LN_EPS) * g + b
        N, L, C = x.shape
        H = NHEAD
        D = C // H
        q = (x @ Wq).reshape(N, L, H, D)
        k = (x @ Wk).reshape(N, L, H, D)
        v = (x @ Wv).reshape(N, L, H, D)
        Q = jax.nn.elu(q) + 1.0
        K = jax.nn.elu(k) + 1.0
        v = v / L
        KV = jnp.einsum('nshd,nshv->nhdv', K, v)
        Z = 1.0 / (jnp.einsum('nlhd,nhd->nlh', Q, K.sum(axis=1)) + ATT_EPS)
        msg = jnp.einsum('nlhd,nhdv,nlh->nlhv', Q, KV, Z) * L
        msg = msg.reshape(N, L, C) @ Wm
        msg = _layernorm(msg, g1, b1)
        h = jnp.concatenate([x, msg], axis=-1) @ W1
        h = jax.nn.relu(h) @ W2
        msg = _layernorm(h, g2, b2)
        return x + msg

    def _L1_ffn_ref(x, router_w, router_b, W1, b1, W2, b2):
        import jax, jax.numpy as jnp
        import numpy as np
        B, K, D = (512, 16, 256)
        E = 32
        H = int(D * 0.25)
        xf = x.reshape(-1, D)
        logits = xf @ router_w.T + router_b
        idx = jnp.argmax(logits, axis=-1)
        w1t = jnp.take(W1, idx, axis=0)
        h = jnp.einsum('nd,ndh->nh', xf, w1t) + jnp.take(b1, idx, axis=0)
        h = jax.nn.relu(h)
        w2t = jnp.take(W2, idx, axis=0)
        out = jnp.einsum('nh,nhd->nd', h, w2t) + jnp.take(b2, idx, axis=0)
        out = jax.nn.relu(out)
        return out.reshape(x.shape)
    edge_index = jnp.stack([src, dst])
    xn = _layernorm(x, axis=-1)
    x = x + _L0_gnn_ref(xn, edge_index, L0_gnn_W, L0_gnn_att_src, L0_gnn_att_dst, L0_gnn_bias) + _L0_mix_ref(xn[None], L0_mix_Wqkv, L0_mix_ln1_g, L0_mix_ln1_b, L0_mix_W1, L0_mix_b1, L0_mix_W2, L0_mix_b2, L0_mix_ln2_g, L0_mix_ln2_b)[0]
    x = x + _L0_ffn_ref(_layernorm(x, axis=-1)[None], L0_ffn_Wg, L0_ffn_bg, L0_ffn_W1, L0_ffn_b1, L0_ffn_W2, L0_ffn_b2)[0]
    xn = _layernorm(x, axis=-1)
    x = x + _L1_gnn_ref(xn, edge_index, L1_gnn_W, L1_gnn_a_src, L1_gnn_a_dst, L1_gnn_bias_gat, L1_gnn_W_res, L1_gnn_b_res, L1_gnn_gamma, L1_gnn_beta) + _L1_mix_ref(xn[None], L1_mix_Wq, L1_mix_Wk, L1_mix_Wv, L1_mix_Wm, L1_mix_W1, L1_mix_W2, L1_mix_g1, L1_mix_b1, L1_mix_g2, L1_mix_b2)[0]
    x = x + _L1_ffn_ref(_layernorm(x, axis=-1)[None], L1_ffn_router_w, L1_ffn_router_b, L1_ffn_W1, L1_ffn_b1, L1_ffn_W2, L1_ffn_b2)[0]
    return x

_drawn_inputs = setup_inputs


def setup_inputs(seed=0):
    import zlib

    import numpy as np

    out = dict(_drawn_inputs(seed))
    spreads = {'L0_gnn_bias': (0.0, 0.1),
     'L0_mix_ln1_g': (1.0, 0.2),
     'L0_mix_ln1_b': (0.0, 0.1),
     'L0_mix_ln2_g': (1.0, 0.2),
     'L0_mix_ln2_b': (0.0, 0.1),
     'L1_gnn_bias_gat': (0.0, 0.1),
     'L1_gnn_b_res': (0.0, 0.1),
     'L1_gnn_gamma': (1.0, 0.2),
     'L1_gnn_beta': (0.0, 0.1),
     'L1_mix_g1': (1.0, 0.2),
     'L1_mix_b1': (0.0, 0.314),
     'L1_mix_g2': (1.0, 0.2),
     'L1_mix_b2': (0.0, 0.1)}
    factors = {'L0_gnn_att_dst': 4.871,
     'L0_mix_Wqkv': 4.138,
     'L0_mix_b1': 4.072,
     'L0_ffn_bg': 3.226,
     'L0_ffn_b1': 7.46,
     'L0_ffn_b2': 4.925,
     'L1_gnn_a_dst': 2.771,
     'L1_mix_Wq': 4.485,
     'L1_mix_Wk': 2.758,
     'L1_ffn_router_b': 4.048,
     'L1_ffn_b1': 8.0,
     'L1_ffn_b2': 7.7}
    for name, (base, spread) in spreads.items():
        noise = np.random.default_rng([zlib.crc32(name.encode()), seed]).standard_normal(out[name].shape)
        drawn = base * np.exp(spread * noise) if base else spread * noise
        out[name] = jnp.asarray(drawn.astype(out[name].dtype))
    for name, factor in factors.items():
        out[name] = (out[name] * factor).astype(out[name].dtype)
    return out
```

```python
from contextlib import ExitStack

import concourse.bass as bass
from concourse import mybir

F32 = mybir.dt.float32
I32 = mybir.dt.int32
BF16 = mybir.dt.bfloat16
ALU = mybir.AluOpType
ACT = mybir.ActivationFunctionType
AX = mybir.AxisListType

N = 3125
D = 256
E = 50000
P = 125
NT = N // P
KD = D // 128
EC = E // P
ET = -(-E // 128)
EPAD = ET * 128 - E
NW = ET + NT
WG = -(-NW // 128)
ROW = D + 8
NOWHERE = 1 << 20


def link_of(eng, sem):
    done = [0]

    def link(ins):
        done[0] += 1
        ins.then_inc(sem, 1)
        eng.wait_ge(sem, done[0])

    return link


def small_numbers(nc, engine, row, most):
    _, numbers = nc.values_load_multi_w_load_instructions(
        row, engines=[engine], min_val=0, max_val=most,
        skip_runtime_bounds_check_because="the row counts bucket ends or experts passed, so it is 0 to most for any inputs")
    return numbers


class Memory:

    used = {}
    semaphores = []

    def __init__(self, nc, stack, prefix):
        self.nc, self.stack, self.prefix = nc, stack, prefix

    def name(self, name):
        name = self.prefix + name
        self.used[name] = self.used.get(name, 0) + 1
        return name if self.used[name] == 1 else f"{name}_{self.used[name]}"

    def sb(self, name, shape, dt=F32):
        return self.stack.enter_context(self.nc.sbuf_tensor(self.name(name), shape, dt))

    def ps(self, name, shape, dt=F32):
        return self.stack.enter_context(self.nc.psum_tensor(self.name(name), shape, dt))

    def sem(self, name):
        sem = self.nc.alloc_semaphore(name=self.name(name))
        self.semaphores.append(sem)
        return sem


def clear_semaphores(nc):
    nc.clear_and_free_semaphores(list(Memory.semaphores))
    nc.all_engine_barrier()
    Memory.semaphores.clear()


def build_constants(nc, keep):
    c = {}
    c["ident"] = keep.sb("ident", [128, 128])
    c["ident16"] = keep.sb("ident16", [128, 128], BF16)
    c["before"] = keep.sb("before", [128, 128])
    c["ones"] = keep.sb("ones", [128, 128])
    c["half"] = keep.sb("half", [128, NT])
    c["eps"] = keep.sb("eps", [128, NT])
    c["count_i"] = keep.sb("count_i", [128, 512], I32)
    c["count"] = keep.sb("count", [128, 512])
    with ExitStack() as stack:
        m = Memory(nc, stack, "k_")
        made, counted = m.sem("made"), m.sem("counted")
        with nc.Block() as block:

            @block.gpsimd
            def _(pool):
                pool.memset(c["ident"][:], 0.0).then_inc(made, 1)
                pool.memset(c["ones"][:], 1.0).then_inc(made, 1)
                pool.memset(c["half"][:], -0.5)
                pool.memset(c["eps"][:], 1e-5)
                pool.iota(c["count_i"][:], [[1, 512]], base=0, channel_multiplier=0).then_inc(counted, 1)
                pool.wait_ge(made, 2)
                pool.affine_select(out=c["ident"][:], in_=c["ident"][:], compare_op=ALU.not_equal, fill=1.0,
                                   base=0, pattern=[[-1, 128]], channel_multiplier=1).then_inc(made, 1)
                pool.affine_select(out=c["before"][:], in_=c["ones"][:], compare_op=ALU.is_gt, fill=0.0,
                                   base=0, pattern=[[1, 128]], channel_multiplier=-1).then_inc(made, 1)

            @block.vector
            def _(dve):
                dve.wait_ge(counted, 1)
                dve.tensor_copy(c["count"][:], c["count_i"][:])
                dve.wait_ge(made, 4)
                dve.tensor_copy(c["ident16"][:], c["ident"][:])
    return c


def sort_edges(nc, c, src, dst, edge_tiles, ends):
    with ExitStack() as stack:
        m = Memory(nc, stack, "s_")
        dst_i, src_i = m.sb("dst_i", [P, EC], I32), m.sb("src_i", [P, EC], I32)
        next_i = m.sb("next_i", [P, EC], I32)
        dst_f, next_f, drop = m.sb("dst_f", [P, EC]), m.sb("next_f", [P, EC]), m.sb("drop", [P, EC])
        pairs = m.sb("pairs", [P, EC, 2], I32)
        pad = m.sb("pad", [1, EPAD, 2], I32)
        bound = m.sb("bound", [128, NT])
        below = m.sb("below", [P, NT, EC])
        member = m.sb("member", [P, NT, EC])
        rank = m.sb("rank", [P, NT, EC])
        tally = m.sb("tally", [P, NT + 1])
        prior = m.sb("prior", [P, NT])
        base = m.sb("base", [P, NT])
        place_f, place_i = m.sb("place_f", [P, EC]), m.sb("place_i", [P, EC], I32)
        place_now, pair_now = m.sb("place_now", [P, 4], I32), m.sb("pair_now", [P, 4, 2], I32)
        flag_i = m.sb("flag_i", [1, 1], I32)
        ps_ends = m.ps("ps_ends", [128, NT + 1])
        ps_prior = m.ps("ps_prior", [P, NT])
        loaded, packed, padded = m.sem("loaded"), m.sem("packed"), m.sem("padded")
        step, tallied, summed, flagged = m.sem("step"), m.sem("tallied"), m.sem("summed"), m.sem("flagged")
        copied, placed, taken, scattered = m.sem("copied"), m.sem("placed"), m.sem("taken"), m.sem("scattered")
        rounds = m.sem("rounds")
        flat = edge_tiles.rearrange("t (e c) -> (t e) c", c=2)

        with nc.Block() as block:

            @block.sync
            def _(sp):
                sp.dma_start(dst_i[:], dst.rearrange("(p c) -> p c", p=P)).then_inc(loaded, 16)
                sp.dma_start(src_i[:], src.rearrange("(p c) -> p c", p=P)).then_inc(loaded, 16)
                sp.dma_start(next_i[0:P - 1, :], dst[1:1 + (P - 1) * EC].rearrange("(p c) -> p c", p=P - 1)
                             ).then_inc(loaded, 16)
                sp.dma_start(next_i[P - 1:P, 0:EC - 1], dst[(P - 1) * EC + 1:E].rearrange("(a c) -> a c", a=1)
                             ).then_inc(loaded, 16)
                sp.dma_start(next_i[P - 1:P, EC - 1:EC], dst[E - 1:E].rearrange("(a c) -> a c", a=1)
                             ).then_inc(loaded, 16)
                sp.wait_ge(packed, 2)
                sp.dma_start(flat[0:E, :].rearrange("(p c) t -> p (c t)", p=P),
                             pairs[:].rearrange("p c t -> p (c t)")).then_inc(copied, 16)
                sp.wait_ge(padded, 2)
                sp.dma_start(flat[E:E + EPAD, :].rearrange("(a c) t -> a (c t)", a=1),
                             pad[:].rearrange("a c t -> a (c t)")).then_inc(copied, 16)
                sp.wait_ge(copied, 32)

            @block.vector
            def _(dve):
                link = link_of(dve, step)
                dve.memset(pad[:, :, 0], NOWHERE).then_inc(padded, 1)
                dve.memset(pad[:, :, 1], 0).then_inc(padded, 1)
                dve.tensor_scalar(bound[:], c["count"][:, 0:NT], float(P), float(P), ALU.mult, ALU.add)
                dve.wait_ge(loaded, 80)
                dve.tensor_copy(pairs[:, :, 0], dst_i[:]).then_inc(packed, 1)
                dve.tensor_copy(pairs[:, :, 1], src_i[:]).then_inc(packed, 1)
                dve.tensor_copy(dst_f[:], dst_i[:])
                link(dve.tensor_copy(next_f[:], next_i[:]))
                link(dve.tensor_tensor(drop[:], next_f[:], dst_f[:], ALU.is_lt))
                dve.tensor_reduce(tally[:, NT:NT + 1], drop[:], AX.X, ALU.add)
                link(dve.tensor_tensor(below[:], dst_f[:].unsqueeze(1).to_broadcast([P, NT, EC]),
                                       bound[0:P, :].unsqueeze(2).to_broadcast([P, NT, EC]), ALU.is_lt))
                dve.tensor_reduce(tally[:, 0:NT], below[:], AX.X, ALU.add).then_inc(tallied, 1)
                dve.wait_ge(summed, 1)
                link(dve.tensor_copy(ends[:], ps_ends[:]))
                link(dve.tensor_copy(flag_i[:], ends[0:1, NT:NT + 1]))
                dve.nop().then_inc(flagged, 1)
                drops = dve.value_load(flag_i[0:1, 0:1], min_val=0, max_val=E)
                with dve.If(drops > 0):
                    dve.tensor_copy(member[:, 0:1, :], below[:, 0:1, :])
                    link(dve.tensor_tensor(member[:, 1:NT, :], below[:, 1:NT, :], below[:, 0:NT - 1, :],
                                           ALU.subtract))
                    link(dve.tensor_tensor_scan(rank[:].rearrange("p b c -> p (b c)"),
                                                member[:].rearrange("p b c -> p (b c)"),
                                                member[:].rearrange("p b c -> p (b c)"), 0.0, ALU.add, ALU.bypass))
                    link(dve.tensor_copy(prior[:], ps_prior[:]))
                    dve.tensor_scalar(base[:, 0:1], prior[:, 0:1], -1.0, None, ALU.add)
                    link(dve.tensor_tensor(base[:, 1:NT], prior[:, 1:NT], prior[:, 0:NT - 1], ALU.subtract))
                    link(dve.tensor_tensor(base[:, 1:NT], base[:, 1:NT], ends[0:P, 0:NT - 1], ALU.add))
                    link(dve.scalar_tensor_tensor(base[:, 1:NT], base[:, 1:NT], -1.0, tally[:, 0:NT - 1],
                                                  ALU.add, ALU.subtract))
                    link(dve.tensor_tensor(rank[:], rank[:], base[:].unsqueeze(2).to_broadcast([P, NT, EC]), ALU.add))
                    link(dve.tensor_tensor(rank[:], rank[:], member[:], ALU.mult))
                    link(dve.tensor_reduce(place_f[:], rank[:].rearrange("p b c -> p c b"), AX.X, ALU.add))
                    dve.tensor_copy(place_i[:], place_f[:]).then_inc(placed, 1)
                dve.nop()

            @block.tensor
            def _(pe):
                pe.wait_ge(tallied, 1)
                pe.matmul(ps_ends[:], c["ones"][0:P, :], tally[:], start=True, stop=True)
                pe.matmul(ps_prior[:], c["before"][0:P, 0:P], tally[:, 0:NT], start=True, stop=True).then_inc(summed, 1)

            @block.gpsimd
            def _(pool):
                pool.wait_ge(flagged, 1)
                drops = pool.value_load(flag_i[0:1, 0:1], min_val=0, max_val=E)
                pool.wait_ge(copied, 32)
                with pool.If(drops > 0):
                    pool.wait_ge(placed, 1)
                    with pool.Fori(0, EC // 4) as i:
                        pool.tensor_copy(place_now[:], place_i[:, bass.ds(i * 4, 4)]).then_inc(taken, 1)
                        pool.tensor_copy(pair_now[:], pairs[:, bass.ds(i * 4, 4), :]).then_inc(taken, 1)
                        pool.wait_ge(taken, i * 2 + 2)
                        pool.sem_inc(rounds, 1)
                        for j in range(4):
                            pool.indirect_dma_start(
                                out=flat[0:E, :], out_offset=bass.IndirectOffsetOnAxis(ap=place_now[:, j:j + 1], axis=0),
                                in_=pair_now[:, j, :], in_offset=None).then_inc(scattered, 16)
                        pool.wait_ge(scattered, i * 64 + 64)
                pool.nop()


def list_windows(nc, c, edge_tiles, ends, win):
    with ExitStack() as stack:
        m = Memory(nc, stack, "w_")
        number_i, number = m.sb("number_i", [128, WG], I32), m.sb("number", [128, WG])
        cum, cum_i = m.sb("cum", [128, NT + 1]), m.sb("cum_i", [128, 2, NT + 1], I32)
        edge = m.sb("edge", [128, 2, NT + 1])
        size, some = m.sb("size", [128, NT]), m.sb("some", [128, NT])
        tiles, upto = m.sb("tiles", [128, NT]), m.sb("upto", [128, NT])
        past, term = m.sb("past", [128, WG, NT]), m.sb("term", [128, WG, NT])
        bucket, begin, skip = m.sb("bucket", [128, WG]), m.sb("begin", [128, WG]), m.sb("skip", [128, WG])
        first_node = m.sb("first_node", [128, WG])
        begin_i, tile_i = m.sb("begin_i", [128, WG], I32), m.sb("tile_i", [128, WG], I32)
        got = m.sb("got", [128, WG, 256], I32)
        dst_w, src_w = m.sb("dst_w", [128, WG, 128]), m.sb("src_w", [128, WG, 128])
        ps_dst, ps_src = m.ps("ps_dst", [128, WG, 128]), m.ps("ps_src", [128, WG, 128])
        ps_bucket = m.ps("ps_bucket", [1, WG, 128])
        numbered, step, found = m.sem("numbered"), m.sem("step"), m.sem("found")
        gathered, split, turned = m.sem("gathered"), m.sem("split"), m.sem("turned")

        with nc.Block() as block:

            @block.gpsimd
            def _(pool):
                pool.iota(number_i[:], [[128, WG]], base=0, channel_multiplier=1).then_inc(numbered, 1)
                pool.wait_ge(found, 1)
                for g in range(WG):
                    pool.indirect_dma_start(out=got[:, g, :], out_offset=None, in_=edge_tiles,
                                            in_offset=bass.IndirectOffsetOnAxis(ap=tile_i[:, g:g + 1], axis=0)
                                            ).then_inc(gathered, 16)

            @block.vector
            def _(dve):
                link = link_of(dve, step)
                dve.wait_ge(numbered, 1)
                dve.tensor_copy(number[:], number_i[:])
                dve.memset(cum[:, 0:1], 0.0)
                link(dve.tensor_copy(cum[:, 1:NT + 1], ends[:, 0:NT]))
                dve.tensor_copy(cum_i[:, 0, :], cum[:])
                link(dve.tensor_scalar(cum_i[:, 1, :], cum[:], 127.0, None, ALU.add))
                link(dve.tensor_scalar(cum_i[:], cum_i[:], 7, None, ALU.arith_shift_right))
                dve.tensor_copy(edge[:], cum_i[:])
                link(dve.tensor_tensor(size[:], cum[:, 1:NT + 1], cum[:, 0:NT], ALU.subtract))
                dve.tensor_scalar(some[:], size[:], 0.0, None, ALU.is_gt)
                link(dve.tensor_tensor(tiles[:], edge[:, 1, 1:NT + 1], edge[:, 0, 0:NT], ALU.subtract))
                link(dve.tensor_tensor(tiles[:], tiles[:], some[:], ALU.mult))
                link(dve.tensor_tensor_scan(upto[:], tiles[:], tiles[:], 0.0, ALU.add, ALU.bypass))
                wide = [128, WG, NT]
                link(dve.tensor_tensor(past[:], upto[:].unsqueeze(1).to_broadcast(wide),
                                       number[:].unsqueeze(2).to_broadcast(wide), ALU.is_le))
                dve.tensor_reduce(bucket[:], past[:], AX.X, ALU.add)
                link(dve.tensor_tensor(term[:], past[:], size[:].unsqueeze(1).to_broadcast(wide), ALU.mult))
                link(dve.tensor_reduce(begin[:], term[:], AX.X, ALU.add))
                dve.tensor_copy(begin_i[:], begin[:])
                link(dve.tensor_tensor(term[:], past[:], tiles[:].unsqueeze(1).to_broadcast(wide), ALU.mult))
                dve.tensor_reduce(skip[:], term[:], AX.X, ALU.add)
                link(dve.tensor_scalar(begin_i[:], begin_i[:], 7, None, ALU.arith_shift_right))
                link(dve.tensor_copy(begin[:], begin_i[:]))
                link(dve.tensor_tensor(begin[:], begin[:], number[:], ALU.add))
                link(dve.tensor_tensor(begin[:], begin[:], skip[:], ALU.subtract))
                dve.tensor_scalar(tile_i[:], begin[:], float(ET - 1), None, ALU.min).then_inc(found, 1)
                link(dve.tensor_scalar(first_node[:], bucket[:], float(P), None, ALU.mult))
                dve.wait_ge(gathered, 16 * WG)
                pairs = got[:].rearrange("p g (e c) -> p g e c", c=2)
                dve.tensor_copy(src_w[:], pairs[:, :, :, 1])
                for g in range(WG):
                    last = dve.tensor_scalar(dst_w[:, g, :], pairs[:, g, :, 0], first_node[:, g:g + 1], None,
                                             ALU.subtract)
                last.then_inc(split, 1)
                dve.wait_ge(turned, 1)
                dve.tensor_copy(win["dst"][:], ps_dst[:])
                dve.tensor_copy(win["src"][:], ps_src[:])
                dve.tensor_copy(win["bucket"][:], ps_bucket[:])

            @block.tensor
            def _(pe):
                pe.wait_ge(split, 1)
                for g in range(WG):
                    pe.transpose(ps_dst[:, g, :], dst_w[:, g, :], c["ident"][:])
                    pe.transpose(ps_src[:, g, :], src_w[:, g, :], c["ident"][:])
                    last = pe.transpose(ps_bucket[:, g, :], bucket[:, g:g + 1], c["ident"][:])
                last.then_inc(turned, 1)

TB = 5
TI = NT // TB
CUTS = [(0, 3 * P), (3 * P, TB * P)]
EPS_LN = 1e-5
EPS_ATT = 1e-6
SLOPE = 0.2
GW = 4
NG = NW // GW
RING = 4


class Steps:

    def __init__(self, eng, sem, per, turn):
        self.eng, self.sem, self.per, self.turn, self.done = eng, sem, per, turn, 0

    def link(self, ins):
        self.done += 1
        ins.then_inc(self.sem, 1)
        self.eng.wait_ge(self.sem, self.turn * self.per + self.done)

    def end(self):
        assert self.done == self.per, self.done


def layer_norm_all(nc, c, x, xn):
    with ExitStack() as stack:
        m = Memory(nc, stack, "n_")
        stats, moments, scale = m.sb("stats", [P, NT, 6]), m.sb("moments", [P, NT, 2]), m.sb("scale", [P, NT])
        step, known, scaled, varied_set = (m.sem(n) for n in "step known scaled varied_set".split())
        varied = m.sb("varied", [P, NT])
        with nc.Block() as block:

            @block.gpsimd
            def _(pool):
                pool.wait_ge(known, 1)
                pool.tensor_scalar(varied[:], moments[:, :, 1], EPS_LN, None, ALU.add).then_inc(varied_set, 1)
                pool.wait_ge(varied_set, 1)
                pool.tensor_tensor(scale[:], varied[:], c["half"][0:P, 0:NT], ALU.pow).then_inc(scaled, 1)

            @block.vector
            def _(dve):
                link = link_of(dve, step)
                for t in range(NT):
                    last = dve.bn_stats(stats[:, t, :], x[:, t, :])
                link(last)
                for t in range(NT):
                    last = dve.bn_aggr(moments[:, t, :], stats[:, t, :])
                last.then_inc(known, 1)
                dve.wait_ge(scaled, 1)
                for t in range(NT):
                    dve.tensor_scalar(xn[:, t, :], x[:, t, :], moments[:, t, 0:1], scale[:, t:t + 1],
                                      ALU.subtract, ALU.mult)


def project(nc, c, xn, w, heads, rows, scores, qt, kv_block, acc, res):
    with ExitStack() as stack:
        m = Memory(nc, stack, "p_")
        wa, wb, wq = m.sb("wa", [128, KD, 2 * D]), m.sb("wb", [128, KD, 2 * D]), m.sb("wq", [128, KD, D])
        ws = m.sb("ws", [128, KD, 16])
        att, prod = m.sb("att", [128, 2, D]), m.sb("prod", [128, 2, D])
        bias = m.sb("bias", [P, 2, D])
        xs = m.sb("xs", [P, TB, D])
        xt = m.sb("xt", [128, KD, TB * P])
        row = m.sb("row", [P, TB, ROW])
        kneg, kexp, kel = m.sb("kneg", [P, D]), m.sb("kexp", [P, D]), m.sb("kel", [P, TB, D])
        vext = m.sb("vext", [P, TB, KD, 129])
        qneg, qexp = m.sb("qneg", [128, 2, 3 * P]), m.sb("qexp", [128, 2, 3 * P])
        kv_sum = m.sb("kv_sum", [128, KD, 129])
        ps_t, ps_q = m.ps("ps_t", [128, 2, 512]), m.ps("ps_q", [128, 2, 512])
        ps_a, ps_b = m.ps("ps_a", [P, 2 * D]), m.ps("ps_b", [P, 2 * D])
        ps_s, ps_kvp = m.ps("ps_s", [P, 512]), m.ps("ps_kvp", [128, 512])
        names = ("loaded weighted step staged turned xt_ready h_ready row_ready scores_read kv_ready kneg_ready "
                 "kexp_ready kel_ready v_ready kvp_ready kvp_read q_ready qneg_ready qexp_ready q_read cleared")
        s = {n: m.sem(n) for n in names.split()}
        stored = [m.sem(f"stored{j}") for j in range(TB)]
        hd = D // heads
        has_res = res is not None
        loads = 6 + 3 * has_res
        nb = 2 * D if has_res else D

        with nc.Block() as block:

            @block.sync
            def _(sp):
                halves = "(k p) n -> p k n"
                sp.dma_start(wa[:, :, 0:D], w["proj"].rearrange(halves, p=128)).then_inc(s["loaded"], 16)
                sp.dma_start(wa[:, :, D:2 * D], w["v"].rearrange(halves, p=128)).then_inc(s["loaded"], 16)
                sp.dma_start(wb[:, :, 0:D], w["k"].rearrange(halves, p=128)).then_inc(s["loaded"], 16)
                sp.dma_start(wq[:], w["q"].rearrange("(k p) n -> p k n", p=128)).then_inc(s["loaded"], 16)
                sp.dma_start(att[:, 0, :], w["att_src"].partition_broadcast(128)).then_inc(s["loaded"], 16)
                sp.dma_start(att[:, 1, :], w["att_dst"].partition_broadcast(128)).then_inc(s["loaded"], 16)
                if has_res:
                    sp.dma_start(wb[:, :, D:2 * D], w["res"].rearrange(halves, p=128)).then_inc(s["loaded"], 16)
                    sp.dma_start(bias[:, 0, :], w["bias_gat"].partition_broadcast(P)).then_inc(s["loaded"], 16)
                    sp.dma_start(bias[:, 1, :], w["b_res"].partition_broadcast(P)).then_inc(s["loaded"], 16)
                for j in range(TB):
                    sp.sem_inc(stored[j], 16)
                with sp.Fori(0, TI) as i:
                    for j in range(TB):
                        sp.wait_ge(s["row_ready"], i * TB + j + 2)
                        sp.wait_ge(s["scores_read"], i * TB + j + 2)
                        sp.dma_start(rows[bass.ds((i * TB + j) * P, P), :], row[:, j, :]).then_inc(stored[j], 16)
                for j in range(TB):
                    sp.wait_ge(stored[j], 16 * (TI + 1))

            @block.gpsimd
            def _(pool):
                with pool.Fori(0, TI) as i:
                    for j in range(TB):
                        pool.wait_ge(s["turned"], i * TB + j + 1)
                        pool.tensor_copy(xs[:, j:j + 1, :], xn[:, bass.ds(i * TB + j, 1), :]).then_inc(s["staged"], 1)

            @block.tensor
            def _(pe):
                def turn_rows(i, j):
                    pe.wait_ge(s["staged"], i * TB + j + 1)
                    if j == 0:
                        pe.wait_ge(s["xt_ready"], i * TB + 1)
                    for k in range(KD):
                        last = pe.transpose(ps_t[:, j % 2, k * P:(k + 1) * P],
                                            xs[:, j, 128 * k:128 * k + 128], c["ident"][0:P, 0:P])
                    last.then_inc(s["turned"], 1)

                def products(i, j):
                    n = i * TB + j
                    xt_j = [xt[:, k, j * P:(j + 1) * P] for k in range(KD)]
                    pe.wait_ge(s["xt_ready"], n + 2)
                    pe.wait_ge(s["row_ready"], n + 1)
                    pe.wait_ge(s["v_ready"], n + 1)
                    for k in range(KD):
                        pe.matmul(ps_a[:], xt_j[k], wa[:, k, :], start=(k == 0), stop=(k == KD - 1))
                    pe.wait_ge(s["scores_read"], n + 1)
                    for k in range(KD):
                        last = pe.matmul(ps_s[:, 0:16], xt_j[k], ws[:, k, :], start=(k == 0), stop=(k == KD - 1))
                    last.then_inc(s["h_ready"], 1)
                    pe.wait_ge(s["kel_ready"], n + 1)
                    for k in range(KD):
                        last = pe.matmul(ps_b[:, 0:nb], xt_j[k], wb[:, k, 0:nb], start=(k == 0), stop=(k == KD - 1))
                    last.then_inc(s["kv_ready"], 1)

                def outer(i, j):
                    n = i * TB + j
                    pe.wait_ge(s["kel_ready"], n + 2)
                    pe.wait_ge(s["v_ready"], n + 2)
                    pe.wait_ge(s["kvp_read"], n + 1)
                    for k in range(KD):
                        last = pe.matmul(ps_kvp[:, k * 129:k * 129 + 129], kel[:, j, 128 * k:128 * k + 128],
                                         vext[:, j, k, :], start=True, stop=True)
                    last.then_inc(s["kvp_ready"], 1)

                for free in ("xt_ready", "row_ready", "scores_read", "v_ready", "kel_ready", "kvp_read"):
                    pe.sem_inc(s[free], 1)
                pe.sem_inc(s["q_read"], 2)
                pe.sem_inc(s["q_ready"], 4)
                pe.sem_inc(s["turned"], TB)
                pe.wait_ge(s["weighted"], 1)
                with pe.Fori(0, TI) as i:
                    turn_rows(i, 0)
                    for j in range(TB):
                        if j + 1 < TB:
                            turn_rows(i, j + 1)
                        products(i, j)
                        if j >= 1:
                            outer(i, j - 1)
                    for q in range(4):
                        lo, hi = CUTS[q // 2]
                        half = q % 2
                        pe.wait_ge(s["q_read"], i * 4 + q + 1)
                        for k in range(KD):
                            last = pe.matmul(ps_q[:, q % 2, 0:hi - lo], wq[:, k, 128 * half:128 * half + 128],
                                             xt[:, k, lo:hi], start=(k == 0), stop=(k == KD - 1))
                        last.then_inc(s["q_ready"], 1)
                    outer(i, TB - 1)

            @block.scalar
            def _(act):
                def take_xt(i, j):
                    n = i * TB + j
                    act.wait_ge(s["turned"], n + 1 + TB)
                    act.copy(xt[:, :, j * P:(j + 1) * P],
                             ps_t[:, j % 2, 0:KD * P].rearrange("p (k n) -> p k n", k=KD)).then_inc(s["xt_ready"], 1)

                def evacuate(i, j):
                    n = i * TB + j
                    act.wait_ge(s["h_ready"], n + 1)
                    act.wait_ge(stored[j], i * 16 + 16)
                    if has_res:
                        act.copy(acc[:, bass.ds(n, 1), 0:D], ps_a[:, 0:D])
                    act.copy(row[:, j, 0:D], ps_a[:, 0:D]).then_inc(s["row_ready"], 1)
                    act.activation(vext[:, j, :, 0:128], ps_a[:, D:2 * D].rearrange("p (k n) -> p k n", k=KD),
                                   ACT.Copy, scale=w["v_scale"]).then_inc(s["v_ready"], 1)
                    act.wait_ge(s["kneg_ready"], n + 1)
                    act.activation(kexp[:], kneg[:], ACT.Exp).then_inc(s["kexp_ready"], 1)

                with act.Fori(0, TI) as i:
                    act.wait_ge(s["q_ready"], i * 4 + 4)
                    take_xt(i, 0)
                    for j in range(TB):
                        if j + 1 < TB:
                            take_xt(i, j + 1)
                        evacuate(i, j)
                    for q in range(4):
                        lo, hi = CUTS[q // 2]
                        act.wait_ge(s["qneg_ready"], i * 4 + q + 1)
                        act.activation(qexp[:, q % 2, 0:hi - lo], qneg[:, q % 2, 0:hi - lo],
                                       ACT.Exp).then_inc(s["qexp_ready"], 1)

            @block.vector
            def _(dve):
                link = link_of(dve, s["step"])
                dve.memset(vext[:, :, :, 128:129], 1.0)
                dve.memset(kv_sum[:], 0.0)
                link(dve.memset(ws[:], 0.0))
                dve.wait_ge(s["loaded"], 16 * loads)
                for k in range(KD):
                    for side in range(2):
                        link(dve.tensor_tensor(prod[:, side, :], wa[:, k, 0:D], att[:, side, :], ALU.mult))
                        last = dve.tensor_reduce(ws[:, k, 8 * side:8 * side + heads],
                                                 prod[:, side, :].rearrange("p (h d) -> p h d", h=heads), AX.X, ALU.add)
                last.then_inc(s["weighted"], 1)
                if has_res:
                    link(dve.tensor_tensor(bias[:, 0, :], bias[:, 0, :], bias[:, 1, :], ALU.add))

                def scores_and_keys(i, j):
                    n = i * TB + j
                    dve.wait_ge(s["h_ready"], n + 1)
                    dve.wait_ge(stored[j], i * 16 + 16)
                    dve.tensor_copy(row[:, j, D:D + 8], ps_s[:, 0:8])
                    dve.tensor_copy(scores[:, bass.ds(n, 1), :], ps_s[:, 0:16]).then_inc(s["scores_read"], 1)
                    dve.wait_ge(s["kv_ready"], n + 1)
                    dve.tensor_scalar(kneg[:], ps_b[:, 0:D], 0.0, None, ALU.min).then_inc(s["kneg_ready"], 1)
                    if has_res:
                        dve.tensor_tensor(res[:, bass.ds(n, 1), :], ps_b[:, D:2 * D], bias[:, 0, :], ALU.add)
                    dve.wait_ge(s["kexp_ready"], n + 1)
                    dve.scalar_tensor_tensor(kel[:, j, :], ps_b[:, 0:D], 0.0, kexp[:], ALU.max,
                                             ALU.add).then_inc(s["kel_ready"], 1)

                def add_outer(i, j):
                    n = i * TB + j
                    dve.wait_ge(s["kvp_read"], n + 1)
                    dve.wait_ge(s["kvp_ready"], n + 1)
                    dve.tensor_tensor(kv_sum[:], kv_sum[:], ps_kvp[:, 0:KD * 129].rearrange("p (k n) -> p k n", k=KD),
                                      ALU.add).then_inc(s["kvp_read"], 1)

                def queries(i, q):
                    lo, hi = CUTS[q // 2]
                    dve.wait_ge(s["q_ready"], i * 4 + q + 5)
                    dve.tensor_scalar(qneg[:, q % 2, 0:hi - lo], ps_q[:, q % 2, 0:hi - lo], 0.0, None,
                                      ALU.min).then_inc(s["qneg_ready"], 1)

                def queries_done(i, q):
                    lo, hi = CUTS[q // 2]
                    dve.wait_ge(s["qexp_ready"], i * 4 + q + 1)
                    dve.scalar_tensor_tensor(qt[:, q % 2, bass.ds(i * (TB * P) + lo, hi - lo)],
                                             ps_q[:, q % 2, 0:hi - lo], 0.0, qexp[:, q % 2, 0:hi - lo],
                                             ALU.max, ALU.add).then_inc(s["q_read"], 1)

                with dve.Fori(0, TI) as i:
                    for j in range(TB):
                        scores_and_keys(i, j)
                        if j >= 1:
                            add_outer(i, j - 1)
                    queries(i, 0)
                    for q in range(4):
                        if q + 1 < 4:
                            queries(i, q + 1)
                        queries_done(i, q)
                    add_outer(i, TB - 1)

        with nc.Block() as block:

            @block.vector
            def _(dve):
                dve.memset(kv_block[:], 0.0).then_inc(s["cleared"], 1)
                dve.wait_ge(s["cleared"], 1)
                for q in range(4):
                    rows_q = slice(32 * q, 32 * q + 32)
                    dve.tensor_copy(kv_block[rows_q, :, 32 * q:32 * q + 32], kv_sum[rows_q, :, 32 * q:32 * q + 32])
                    dve.tensor_copy(kv_block[rows_q, :, 128 + q:129 + q], kv_sum[rows_q, :, 128:129])


def bound_scores(nc, c, heads, scores, dst_parts, acc, acc_odd, self_loops):
    with ExitStack() as stack:
        m = Memory(nc, stack, "b_")
        most, most_t, diag = m.sb("most", [P, 8]), m.sb("most_t", [8, 1]), m.sb("diag", [8, 8])
        z = m.sb("z", [P, NT, 8])
        own, bound = m.sb("own", [P, NT, 8]), m.sb("bound", [P, NT, 8])
        dst_side = m.sb("dst_side", [128, NT + 1, 16])
        ps_t, ps_b = m.ps("ps_t", [8, P]), m.ps("ps_b", [P, 8])
        step, reduced, turned, spread, logit, weight = (m.sem(n) for n in
                                                        "step reduced turned spread logit weight".split())
        diagonal = m.sem("diagonal")
        with nc.Block() as block:

            @block.vector
            def _(dve):
                link = link_of(dve, step)
                dve.memset(dst_side[:, NT:NT + 1, :], 0.0)
                dve.tensor_reduce(most[:], scores[:, :, 0:8].rearrange("p t h -> p h t"), AX.X, ALU.max).then_inc(reduced, 1)
                dve.tensor_copy(dst_side[0:P, 0:NT, 0:8], scores[:, :, 8:16])
                dve.wait_ge(turned, 1)
                link(dve.tensor_reduce(most_t[:], ps_t[:], AX.X, ALU.max))
                dve.tensor_scalar(diag[:], c["ident"][0:8, 0:8], most_t[:], None, ALU.mult).then_inc(diagonal, 1)
                dve.wait_ge(spread, 1)
                link(dve.tensor_copy(most[:], ps_b[:]))
                link(dve.tensor_tensor(z[:], scores[:, :, 8:16], most[:].unsqueeze(1).to_broadcast([P, NT, 8]), ALU.add))
                link(dve.scalar_tensor_tensor(dst_side[0:P, 0:NT, 8:16], z[:], SLOPE, z[:], ALU.mult, ALU.max))
                dve.tensor_copy(bound[:], dst_side[0:P, 0:NT, 8:16])
                for part in range(3):
                    cols = slice(16 * part, 16 * part + 16)
                    link(dve.tensor_copy(dst_parts[0:P, :, cols], dst_side[0:P]))
                    if part < 2:
                        link(dve.tensor_tensor(dst_side[0:P], dst_side[0:P], dst_parts[0:P, :, cols], ALU.subtract))
                if not self_loops:
                    dve.memset(acc[:], 0.0)
                else:
                    link(dve.tensor_tensor(z[:], scores[:, :, 0:8], scores[:, :, 8:16], ALU.add))
                    link(dve.scalar_tensor_tensor(own[:], z[:], SLOPE, z[:], ALU.mult, ALU.max))
                    dve.tensor_tensor(own[:], own[:], bound[:], ALU.subtract).then_inc(logit, 1)
                    dve.wait_ge(weight, 1)
                    for h in range(heads):
                        cols = slice(h * (D // heads), (h + 1) * (D // heads))
                        dve.tensor_tensor(acc[:, 0:NT, cols], acc[:, 0:NT, cols],
                                          z[:, :, h:h + 1].to_broadcast([P, NT, D // heads]), ALU.mult)
                    dve.tensor_copy(acc[:, 0:NT, D:D + 8], z[:])
                    dve.memset(acc[:, NT:NT + 1, :], 0.0)

            @block.gpsimd
            def _(pool):
                pool.memset(acc_odd[:], 0.0)

            @block.scalar
            def _(act):
                if self_loops:
                    act.wait_ge(logit, 1)
                    act.activation(z[:], own[:], ACT.Exp).then_inc(weight, 1)

            @block.tensor
            def _(pe):
                pe.wait_ge(reduced, 1)
                pe.transpose(ps_t[:], most[:], c["ident"][0:P, 0:P]).then_inc(turned, 1)
                pe.wait_ge(diagonal, 1)
                pe.matmul(ps_b[:], c["ones"][0:8, 0:P], diag[:], start=True, stop=True).then_inc(spread, 1)


def edges(nc, c, heads, rows, win, dst_parts, acc, acc_odd):
    hd = D // heads
    with ExitStack() as stack:
        m = Memory(nc, stack, "e_")
        idx = m.sb("idx", [128, 2, RING * GW], I32)
        got = m.sb("got", [128, RING, GW, ROW])
        hot = m.sb("hot", [128, RING, GW, 128])
        hot_t = m.sb("hot_t", [128, 2, GW, 128], BF16)
        z, lk = m.sb("z", [128, GW, heads]), m.sb("lk", [128, GW, heads])
        logit = m.sb("logit", [128, GW, heads])
        ps_t = m.ps("ps_t", [128, GW, 128])
        ps_d = m.ps("ps_d", [128, 2, 512])
        ps_m = m.ps("ps_m", [128, GW, 512])
        names = "indexed rounds hot_ready hot_turned hot_t_ready dst_ready summed logit_ready weight_ready weighed scattered added"
        s = {n: m.sem(n) for n in names.split()}
        gathered = [m.sem(f"gathered{r}") for r in range(RING)]
        flat_src = win["src"][:].rearrange("p g e -> p (g e)")
        flat_dst = win["dst"][:].rearrange("p g e -> p (g e)")
        flat_bucket = win["bucket"][:].rearrange("p g e -> p (g e)")

        with nc.Block() as block:

            @block.gpsimd
            def _(pool):
                def gather(g, copies, half, r, first=False):
                    if not first:
                        pool.wait_ge(s["scattered"], g * GW - (RING - 1) * GW)
                    if r == 0:
                        pool.tensor_copy(idx[:, half, :], flat_src[:, bass.ds(g * GW, RING * GW)]).then_inc(s["indexed"], 1)
                        pool.wait_ge(s["indexed"], copies)
                    pool.sem_inc(s["rounds"], 1)
                    for j in range(GW):
                        at = r * GW + j
                        pool.indirect_dma_start(out=got[:, r, j, :], out_offset=None, in_=rows,
                                                in_offset=bass.IndirectOffsetOnAxis(ap=idx[:, half, at:at + 1], axis=0)
                                                ).then_inc(gathered[r], 16)

                for k in range(2 * RING):
                    gather(k, k // RING + 1, k // RING, k % RING, k < RING)
                with pool.Fori(1, NG // (2 * RING)) as i:
                    for k in range(2 * RING):
                        gather(i * (2 * RING) + k, i * 2 + k // RING + 1, k // RING, k % RING)
                gather(NG, NG // RING + 1, 0, 0)

            @block.tensor
            def _(pe):
                def turn_hot(g, r):
                    pe.wait_ge(s["hot_ready"], g + 1)
                    for j in range(GW):
                        last = pe.transpose(ps_t[:, j, :], hot[:, r, j, :], c["ident"][:])
                    last.then_inc(s["hot_turned"], 1)

                def spread_dst(g, r):
                    buckets = small_numbers(nc, mybir.EngineType.PE, flat_bucket[0:1, bass.ds(g * GW, GW)], NT)
                    pe.wait_ge(s["hot_t_ready"], g + 1)
                    for j in range(GW):
                        for part in range(3):
                            last = pe.matmul(ps_d[:, r % 2, 16 * j:16 * j + 16], hot_t[0:P, r % 2, j, :],
                                             dst_parts[0:P, bass.ds(buckets[j], 1), 16 * part:16 * part + 16],
                                             start=(part == 0), stop=(part == 2))
                    last.then_inc(s["dst_ready"], 1)

                def scatter(g, r, first):
                    pe.wait_ge(s["weighed"], g + 1)
                    for j in range(GW):
                        if not first:
                            pe.wait_ge(s["added"], g * GW + j - GW + 1)
                        pe.matmul(ps_m[:, j, 0:ROW], hot[:, r, j, :], got[:, r, j, :], start=True,
                                  stop=True).then_inc(s["scattered"], 1)

                def step(g, r, first=False):
                    turn_hot(g + 2, (r + 2) % RING)
                    scatter(g, r, first)
                    spread_dst(g + 2, (r + 2) % RING)

                for r in range(2):
                    turn_hot(r, r)
                    spread_dst(r, r)
                for r in range(RING):
                    step(r, r, r == 0)
                with pe.Fori(1, NG // RING) as i:
                    for r in range(RING):
                        step(i * RING + r, r)

            @block.scalar
            def _(act):
                def take_hot_t(g, r):
                    act.wait_ge(s["hot_turned"], g + 1)
                    act.copy(hot_t[:, r % 2, :, :], ps_t[:]).then_inc(s["hot_t_ready"], 1)

                def raise_logits(g, r):
                    act.wait_ge(s["logit_ready"], g + 1)
                    act.activation(got[:, r, :, D:D + heads], logit[:], ACT.Exp).then_inc(s["weight_ready"], 1)

                def step(g, r):
                    take_hot_t(g + 2, (r + 2) % RING)
                    raise_logits(g + 1, (r + 1) % RING)

                take_hot_t(0, 0)
                take_hot_t(1, 1)
                raise_logits(0, 0)
                for r in range(RING):
                    step(r, r)
                with act.Fori(1, NG // RING) as i:
                    for r in range(RING):
                        step(i * RING + r, r)

            @block.vector
            def _(dve):
                def mark(g, r):
                    dve.tensor_tensor(hot[:, r, :, :], c["count"][:, 0:128].unsqueeze(1).to_broadcast([128, GW, 128]),
                                      flat_dst[:, bass.ds(g * GW, GW)].unsqueeze(2).to_broadcast([128, GW, 128]),
                                      ALU.is_equal).then_inc(s["hot_ready"], 1)

                def logits(g, r, rows_in):
                    dst = ps_d[:, r % 2, 0:16 * GW].rearrange("p (w c) -> p w c", c=16)
                    dve.wait_ge(gathered[r], rows_in)
                    dve.wait_ge(s["dst_ready"], g + 1)
                    dve.tensor_tensor(z[:], got[:, r, :, D:D + heads], dst[:, :, 0:heads], ALU.add).then_inc(s["summed"], 1)
                    dve.wait_ge(s["summed"], g * 2 + 1)
                    dve.scalar_tensor_tensor(lk[:], z[:], SLOPE, z[:], ALU.mult, ALU.max).then_inc(s["summed"], 1)
                    dve.wait_ge(s["summed"], g * 2 + 2)
                    dve.tensor_tensor(logit[:], lk[:], dst[:, :, 8:8 + heads], ALU.subtract).then_inc(s["logit_ready"], 1)

                def weigh(g, r):
                    dve.wait_ge(s["weight_ready"], g + 1)
                    h = got[:, r, :, 0:D].rearrange("p w (h d) -> p w h d", h=heads)
                    dve.tensor_tensor(h, h, got[:, r, :, D:D + heads].unsqueeze(3).to_broadcast([128, GW, heads, hd]),
                                      ALU.mult).then_inc(s["weighed"], 1)

                def add(g, first=False):
                    buckets = small_numbers(nc, mybir.EngineType.DVE, flat_bucket[0:1, bass.ds(g * GW, GW)], NT)
                    for j in range(GW):
                        at = (acc, acc_odd)[j % 2][:, bass.ds(buckets[j], 1), 0:D + heads]
                        if not first or j >= 2:
                            dve.wait_ge(s["added"], g * GW + j - 1)
                        dve.wait_ge(s["scattered"], g * GW + j + 1)
                        dve.tensor_tensor(at, at, ps_m[0:P, j:j + 1, 0:D + heads], ALU.add).then_inc(s["added"], 1)

                def step(g, r, turn, next_turn):
                    weigh(g, r)
                    if not isinstance(turn, int) or r > 0:
                        add(g - 1, isinstance(turn, int) and r == 1)
                    mark(g + 3, (r + 3) % RING)
                    logits(g + 1, (r + 1) % RING, (next_turn if r == RING - 1 else turn) * (16 * GW) + 16 * GW)

                for r in range(3):
                    mark(r, r)
                logits(0, 0, 16 * GW)
                for r in range(RING):
                    step(r, r, 0, 1)
                with dve.Fori(1, NG // RING) as i:
                    for r in range(RING):
                        step(i * RING + r, r, i, i + 1)
                add(NG - 1)
                dve.wait_ge(s["added"], NG * GW)
                dve.tensor_tensor(acc[:, 0:NT, 0:D + heads], acc[:, 0:NT, 0:D + heads], acc_odd[:, 0:NT, 0:D + heads], ALU.add)

TINY = 1e-30


def wide(ap, shape):
    return ap.unsqueeze(1).to_broadcast(shape)


class Norm:

    def __init__(self, m, per_turn):
        self.stats, self.moments = m.sb("stats", [P, TB, 6]), m.sb("moments", [P, TB, 2])
        self.varied, self.scale = m.sb("varied", [P, TB]), m.sb("scale", [P, TB])
        self.known, self.varied_set, self.scaled, self.hold = (m.sem(n) for n in "known varied_set scaled hold".split())
        self.per_turn = per_turn

    def raise_all(self, pool, c, i):
        for q in range(self.per_turn):
            n = i * self.per_turn + q
            pool.wait_ge(self.known, n + 1)
            pool.tensor_tensor(self.varied[:], self.moments[:, :, 1], c["eps"][0:P, 0:TB], ALU.add).then_inc(self.varied_set, 1)
            pool.wait_ge(self.varied_set, n + 1)
            pool.tensor_tensor(self.scale[:], self.varied[:], c["half"][0:P, 0:TB], ALU.pow).then_inc(self.scaled, 1)

    def apply(self, dve, steps, i, q, src, dst, gain, shift, ready):
        for j in range(TB):
            last = dve.bn_stats(self.stats[:, j, :], src[:, j, :])
        steps.link(last)
        dve.sem_inc(self.hold, 1)
        for j in range(TB):
            last = dve.bn_aggr(self.moments[:, j, :], self.stats[:, j, :])
        last.then_inc(self.known, 1)
        dve.wait_ge(self.scaled, i * self.per_turn + q + 1)
        for j in range(TB):
            last = dve.scalar_tensor_tensor(dst[:, j, :], src[:, j, :], self.moments[:, j, 0:1], gain,
                                            ALU.subtract, ALU.mult)
        steps.link(last)
        for j in range(TB):
            last = dve.scalar_tensor_tensor(dst[:, j, :], dst[:, j, :], self.scale[:, j:j + 1], shift,
                                            ALU.mult, ALU.add)
            if ready is not None:
                last.then_inc(ready, 1)
        if ready is None:
            steps.link(last)


def attend(dve, steps, i, j, ps, attended, free, scale, zz, r):
    dve.wait_ge(attended, i * TB + j + 1)
    both = ps.rearrange("p (k n) -> p k n", k=KD)
    steps.link(dve.tensor_scalar(zz[:, j], both[:, :, 128:132], scale, EPS_ATT * scale, ALU.mult, ALU.add))
    steps.link(dve.reciprocal(zz[:, j], zz[:, j]))
    dve.tensor_tensor(r[:, j, :].rearrange("p (k h d) -> p k h d", k=KD, h=4),
                      both[:, :, 0:128].rearrange("p k (h d) -> p k h d", h=4),
                      zz[:, j].unsqueeze(3).to_broadcast([P, KD, 4, 32]), ALU.mult).then_inc(free, 1)


def since(n, j):
    return n + 1 if j == 0 else n


def mix_elu_gelu(nc, c, w, x, xn, qt, kv_block):
    with ExitStack() as stack:
        m = Memory(nc, stack, "m_")
        w1, w2 = m.sb("w1", [128, KD, D]), m.sb("w2", [128, KD, D])
        b1 = m.sb("b1", [128, KD])
        rows5 = m.sb("rows5", [P, 5, D])
        qs = m.sb("qs", [128, KD, TB * P])
        zz = m.sb("zz", [P, TB, KD, 4])
        r, x1, xb = m.sb("r", [P, TB, D]), m.sb("x1", [P, TB, D]), m.sb("xb", [P, TB, D])
        x1t, ht = m.sb("x1t", [128, KD, TB * P]), m.sb("ht", [128, KD, TB * P])
        ps_a, ps_t = m.ps("ps_a", [P, 2, 512]), m.ps("ps_t", [128, 2, 512])
        ps_h, ps_y = m.ps("ps_h", [128, 2, 512]), m.ps("ps_y", [P, 2, 512])
        names = "loaded step qs_ready attended att_read x1_ready turned x1t_ready hid hid_ready y_ready y_read"
        s = {n: m.sem(n) for n in names.split()}
        norm = Norm(m, 2)
        with nc.Block() as block:

            @block.sync
            def _(sp):
                halves = "(k p) n -> p k n"
                sp.dma_start(w1[:], w["w1"].rearrange(halves, p=128)).then_inc(s["loaded"], 16)
                sp.dma_start(w2[:], w["w2"].rearrange(halves, p=128)).then_inc(s["loaded"], 16)
                sp.dma_start(b1[:], w["b1"]).then_inc(s["loaded"], 16)
                for n, name in enumerate(("ln1_g", "ln1_b", "b2", "ln2_g", "ln2_b")):
                    sp.dma_start(rows5[:, n, :], w[name].partition_broadcast(P)).then_inc(s["loaded"], 16)

            @block.gpsimd
            def _(pool):
                with pool.Fori(0, TI) as i:
                    norm.raise_all(pool, c, i)

            @block.scalar
            def _(act):
                act.wait_ge(s["loaded"], 16 * 8)
                with act.Fori(0, TI) as i:
                    act.copy(qs[:], qt[:, :, bass.ds(i * (TB * P), TB * P)]).then_inc(s["qs_ready"], 1)
                    for j in range(TB):
                        act.wait_ge(s["turned"], i * TB + j + 1)
                        act.copy(x1t[:, :, j * P:(j + 1) * P],
                                 ps_t[:, j % 2, 0:KD * P].rearrange("p (k n) -> p k n", k=KD)).then_inc(s["x1t_ready"], 1)
                    for q in range(4):
                        lo, hi = CUTS[q // 2]
                        act.wait_ge(s["hid"], i * 4 + q + 1)
                        act.activation(ht[:, q % 2, lo:hi], ps_h[:, q % 2, 0:hi - lo], ACT.Gelu,
                                       bias=b1[:, q % 2:q % 2 + 1]).then_inc(s["hid_ready"], 1)

            @block.tensor
            def _(pe):
                for one in ("att_read", "x1t_ready", "y_read"):
                    pe.sem_inc(s[one], 1)
                pe.sem_inc(s["hid_ready"], 2)
                pe.wait_ge(s["loaded"], 16 * 8)
                with pe.Fori(0, TI) as i:
                    pe.wait_ge(s["qs_ready"], i + 1)
                    for j in range(TB):
                        pe.wait_ge(s["att_read"], since(i * TB + j, j))
                        for k in range(KD):
                            last = pe.matmul(ps_a[:, j % 2, 132 * k:132 * k + 132], qs[:, k, j * P:(j + 1) * P],
                                             kv_block[:, k, :], start=True, stop=True)
                        last.then_inc(s["attended"], 1)
                    for j in range(TB):
                        pe.wait_ge(s["x1_ready"], i * TB + j + 1)
                        pe.wait_ge(s["x1t_ready"], since(i * TB + j, j))
                        for k in range(KD):
                            last = pe.transpose(ps_t[:, j % 2, k * P:(k + 1) * P], x1[:, j, 128 * k:128 * k + 128],
                                                c["ident"][0:P, 0:P])
                        last.then_inc(s["turned"], 1)
                    for q in range(4):
                        lo, hi = CUTS[q // 2]
                        half = slice(128 * (q % 2), 128 * (q % 2) + 128)
                        pe.wait_ge(s["x1t_ready"], i * TB + hi // P + 1)
                        pe.wait_ge(s["hid_ready"], i * 4 + q + 1)
                        for k in range(KD):
                            last = pe.matmul(ps_h[:, q % 2, 0:hi - lo], w1[:, k, half], x1t[:, k, lo:hi],
                                             start=(k == 0), stop=(k == KD - 1))
                        last.then_inc(s["hid"], 1)
                    for j in range(TB):
                        pe.wait_ge(s["hid_ready"], i * 4 + (4 if j < 3 else 6))
                        pe.wait_ge(s["y_read"], since(i * TB + j, j))
                        for k in range(KD):
                            last = pe.matmul(ps_y[:, j % 2, 0:D], ht[:, k, j * P:(j + 1) * P], w2[:, k, :],
                                             start=(k == 0), stop=(k == KD - 1))
                        last.then_inc(s["y_ready"], 1)

            @block.vector
            def _(dve):
                dve.wait_ge(s["loaded"], 16 * 8)
                with dve.Fori(0, TI) as i:
                    steps = Steps(dve, s["step"], 2 * TB + 8, i)
                    here = bass.ds(i * TB, TB)
                    for j in range(TB):
                        attend(dve, steps, i, j, ps_a[:, j % 2, 0:KD * 132], s["attended"], s["att_read"], 1.0, zz, r)
                    dve.wait_ge(s["att_read"], i * TB + TB + 1)
                    steps.link(dve.tensor_tensor(r[:], r[:], xn[:, here, :], ALU.add))
                    norm.apply(dve, steps, i, 0, r, x1, rows5[:, 0, :], rows5[:, 1, :], s["x1_ready"])
                    dve.wait_ge(s["x1_ready"], i * TB + TB)
                    steps.link(dve.tensor_tensor(xb[:], x1[:], wide(rows5[:, 2, :], [P, TB, D]), ALU.add))
                    for j in range(TB):
                        dve.wait_ge(s["y_ready"], i * TB + j + 1)
                        dve.tensor_tensor(r[:, j, :], ps_y[:, j % 2, 0:D], xb[:, j, :], ALU.add).then_inc(s["y_read"], 1)
                    dve.wait_ge(s["y_read"], i * TB + TB + 1)
                    norm.apply(dve, steps, i, 1, r, r, rows5[:, 3, :], rows5[:, 4, :], None)
                    steps.link(dve.tensor_tensor(x[:, here, :], x[:, here, :], r[:], ALU.add))
                    steps.end()


def mix_concat(nc, c, w, x, xn, qt, kv_block):
    K2 = 2 * KD
    with ExitStack() as stack:
        m = Memory(nc, stack, "m_")
        wm = m.sb("wm", [128, KD, D])
        w1, w2 = m.sb("w1", [128, K2, 2 * D]), m.sb("w2", [128, K2, D])
        rows4 = m.sb("rows4", [P, 4, D])
        qs = m.sb("qs", [128, KD, TB * P])
        zz = m.sb("zz", [P, TB, KD, 4])
        r, msg = m.sb("r", [P, TB, D]), m.sb("msg", [P, TB, D])
        y, xs = m.sb("y", [P, TB, D]), m.sb("xs", [P, TB, D])
        rt, cat = m.sb("rt", [128, KD, TB * P]), m.sb("cat", [128, K2, TB * P])
        ht = m.sb("ht", [128, K2, TB * P])
        ps_a, ps_t = m.ps("ps_a", [P, 2, 512]), m.ps("ps_t", [128, 2, 512])
        ps_h, ps_y = m.ps("ps_h", [128, 2, 512]), m.ps("ps_y", [P, 2, 512])
        names = ("loaded step staged qs_ready attended att_read turned t_ready hid hid_ready y_ready y_read "
                 "msg_ready")
        s = {n: m.sem(n) for n in names.split()}
        norm = Norm(m, 2)
        with nc.Block() as block:

            @block.sync
            def _(sp):
                halves = "(k p) n -> p k n"
                sp.dma_start(wm[:], w["wm"].rearrange(halves, p=128)).then_inc(s["loaded"], 16)
                sp.dma_start(w1[:], w["w1"].rearrange(halves, p=128)).then_inc(s["loaded"], 16)
                sp.dma_start(w2[:], w["w2"].rearrange(halves, p=128)).then_inc(s["loaded"], 16)
                for n, name in enumerate(("g1", "b1", "g2", "b2")):
                    sp.dma_start(rows4[:, n, :], w[name].partition_broadcast(P)).then_inc(s["loaded"], 16)

            @block.gpsimd
            def _(pool):
                with pool.Fori(0, TI) as i:
                    pool.wait_ge(s["turned"], i * (3 * TB) + TB)
                    pool.tensor_copy(xs[:], xn[:, bass.ds(i * TB, TB), :]).then_inc(s["staged"], 1)
                    norm.raise_all(pool, c, i)

            @block.scalar
            def _(act):
                def take_turned(i, kind, j, to):
                    act.wait_ge(s["turned"], (i + 1) * (3 * TB) + kind * TB + j + 1)
                    act.copy(to[:, :, j * P:(j + 1) * P],
                             ps_t[:, (kind * TB + j) % 2, 0:KD * P].rearrange("p (k n) -> p k n", k=KD)
                             ).then_inc(s["t_ready"], 1)

                def take_y(i, kind, j):
                    act.wait_ge(s["y_ready"], i * (2 * TB) + kind * TB + j + 1)
                    act.copy(y[:, j, :], ps_y[:, (kind * TB + j) % 2, 0:D]).then_inc(s["y_read"], 1)

                with act.Fori(0, TI) as i:
                    act.copy(qs[:], qt[:, :, bass.ds(i * (TB * P), TB * P)]).then_inc(s["qs_ready"], 1)
                    for j in range(TB):
                        take_turned(i, 0, j, cat[:, 0:KD, :])
                    for j in range(TB):
                        take_turned(i, 1, j, rt)
                    for j in range(TB):
                        take_y(i, 0, j)
                    for j in range(TB):
                        take_turned(i, 2, j, cat[:, KD:K2, :])
                    for q in range(8):
                        lo, hi = CUTS[q // 4]
                        act.wait_ge(s["hid"], i * 8 + q + 1)
                        act.activation(ht[:, q % 4, lo:hi], ps_h[:, q % 2, 0:hi - lo], ACT.Relu).then_inc(s["hid_ready"], 1)
                    for j in range(TB):
                        take_y(i, 1, j)

            @block.tensor
            def _(pe):
                def turn(i, kind, j, of, ready, count):
                    n = i * (3 * TB) + kind * TB + j
                    pe.wait_ge(ready, count)
                    pe.wait_ge(s["t_ready"], n + 2 if kind + j == 0 else n + 1)
                    for k in range(KD):
                        last = pe.transpose(ps_t[:, (kind * TB + j) % 2, k * P:(k + 1) * P],
                                            of[:, j, 128 * k:128 * k + 128], c["ident"][0:P, 0:P])
                    last.then_inc(s["turned"], 1)

                for one, n in (("att_read", 1), ("t_ready", 2), ("hid_ready", 2), ("y_read", 2), ("turned", 3 * TB)):
                    pe.sem_inc(s[one], n)
                pe.wait_ge(s["loaded"], 16 * 7)
                with pe.Fori(0, TI) as i:
                    for j in range(TB):
                        turn(i, 0, j, xs, s["staged"], i + 1)
                    pe.wait_ge(s["qs_ready"], i + 1)
                    for j in range(TB):
                        pe.wait_ge(s["att_read"], since(i * TB + j, j))
                        for k in range(KD):
                            last = pe.matmul(ps_a[:, j % 2, 132 * k:132 * k + 132], qs[:, k, j * P:(j + 1) * P],
                                             kv_block[:, k, :], start=True, stop=True)
                        last.then_inc(s["attended"], 1)
                    for j in range(TB):
                        turn(i, 1, j, r, s["att_read"], i * TB + j + 2)
                    for j in range(TB):
                        pe.wait_ge(s["t_ready"], i * (3 * TB) + TB + j + 3)
                        pe.wait_ge(s["y_read"], i * (2 * TB) + j + 1)
                        for k in range(KD):
                            last = pe.matmul(ps_y[:, j % 2, 0:D], rt[:, k, j * P:(j + 1) * P], wm[:, k, :],
                                             start=(k == 0), stop=(k == KD - 1))
                        last.then_inc(s["y_ready"], 1)
                    for j in range(TB):
                        turn(i, 2, j, msg, s["msg_ready"], i * TB + j + 1)
                    for q in range(8):
                        lo, hi = CUTS[q // 4]
                        out = slice(128 * (q % 4), 128 * (q % 4) + 128)
                        pe.wait_ge(s["t_ready"], i * (3 * TB) + 2 * TB + hi // P + 2)
                        pe.wait_ge(s["hid_ready"], i * 8 + q + 1)
                        for k in range(K2):
                            last = pe.matmul(ps_h[:, q % 2, 0:hi - lo], w1[:, k, out], cat[:, k, lo:hi],
                                             start=(k == 0), stop=(k == K2 - 1))
                        last.then_inc(s["hid"], 1)
                    for j in range(TB):
                        pe.wait_ge(s["hid_ready"], i * 8 + (6 if j < 3 else 10))
                        pe.wait_ge(s["y_read"], i * (2 * TB) + TB + j + 1)
                        for k in range(K2):
                            last = pe.matmul(ps_y[:, (TB + j) % 2, 0:D], ht[:, k, j * P:(j + 1) * P], w2[:, k, :],
                                             start=(k == 0), stop=(k == K2 - 1))
                        last.then_inc(s["y_ready"], 1)

            @block.vector
            def _(dve):
                dve.wait_ge(s["loaded"], 16 * 7)
                with dve.Fori(0, TI) as i:
                    steps = Steps(dve, s["step"], 2 * TB + 7, i)
                    here = bass.ds(i * TB, TB)
                    for j in range(TB):
                        attend(dve, steps, i, j, ps_a[:, j % 2, 0:KD * 132], s["attended"], s["att_read"], 1.0 / N, zz, r)
                    dve.wait_ge(s["y_read"], i * (2 * TB) + TB + 2)
                    norm.apply(dve, steps, i, 0, y, msg, rows4[:, 0, :], rows4[:, 1, :], s["msg_ready"])
                    steps.link(dve.tensor_tensor(x[:, here, :], x[:, here, :], xn[:, here, :], ALU.add))
                    dve.wait_ge(s["y_read"], i * (2 * TB) + 2 * TB + 2)
                    norm.apply(dve, steps, i, 1, y, r, rows4[:, 2, :], rows4[:, 3, :], None)
                    steps.link(dve.tensor_tensor(x[:, here, :], x[:, here, :], r[:], ALU.add))
                    steps.end()


def finish_gat_relu(nc, c, w, x, acc):
    with ExitStack() as stack:
        m = Memory(nc, stack, "f_")
        bias, den = m.sb("bias", [P, D]), m.sb("den", [P, NT, 8])
        loaded, step = m.sem("loaded"), m.sem("step")
        with nc.Block() as block:

            @block.sync
            def _(sp):
                sp.dma_start(bias[:], w["gat_bias"].partition_broadcast(P)).then_inc(loaded, 16)

            @block.vector
            def _(dve):
                link = link_of(dve, step)
                out = acc[:, 0:NT, 0:D]
                link(dve.tensor_scalar(den[:], acc[:, 0:NT, D:D + 8], TINY, None, ALU.max))
                link(dve.reciprocal(den[:], den[:]))
                heads = out.rearrange("p t (h d) -> p t h d", h=8)
                link(dve.tensor_tensor(heads, heads, den[:].unsqueeze(3).to_broadcast([P, NT, 8, 32]), ALU.mult))
                dve.wait_ge(loaded, 16)
                link(dve.tensor_tensor(out, out, wide(bias[:], [P, NT, D]), ALU.add))
                dve.scalar_tensor_tensor(x[:], out, 0.0, x[:], ALU.max, ALU.add)


def finish_gat_norm(nc, c, w, x, acc, res):
    with ExitStack() as stack:
        m = Memory(nc, stack, "f_")
        both, den = m.sb("both", [P, 2, D]), m.sb("den", [P, NT, 4])
        stats, moments = m.sb("stats", [P, NT, 6]), m.sb("moments", [P, NT, 2])
        varied, scale = m.sb("varied", [P, NT]), m.sb("scale", [P, NT])
        loaded, step, known, varied_set, scaled = (m.sem(n) for n in "loaded step known varied_set scaled".split())
        with nc.Block() as block:

            @block.sync
            def _(sp):
                sp.dma_start(both[:, 0, :], w["gamma"].partition_broadcast(P)).then_inc(loaded, 16)
                sp.dma_start(both[:, 1, :], w["beta"].partition_broadcast(P)).then_inc(loaded, 16)

            @block.gpsimd
            def _(pool):
                pool.wait_ge(known, 1)
                pool.tensor_scalar(varied[:], moments[:, :, 1], EPS_LN, None, ALU.add).then_inc(varied_set, 1)
                pool.wait_ge(varied_set, 1)
                pool.tensor_tensor(scale[:], varied[:], c["half"][0:P, 0:NT], ALU.pow).then_inc(scaled, 1)

            @block.vector
            def _(dve):
                link = link_of(dve, step)
                out = acc[:, 0:NT, 0:D]
                link(dve.tensor_scalar(den[:], acc[:, 0:NT, D:D + 4], TINY, None, ALU.max))
                link(dve.reciprocal(den[:], den[:]))
                heads = out.rearrange("p t (h d) -> p t h d", h=4)
                link(dve.tensor_tensor(heads, heads, den[:].unsqueeze(3).to_broadcast([P, NT, 4, 64]), ALU.mult))
                link(dve.tensor_tensor(out, out, res[:], ALU.add))
                for t in range(NT):
                    last = dve.bn_stats(stats[:, t, :], acc[:, t, 0:D])
                link(last)
                for t in range(NT):
                    last = dve.bn_aggr(moments[:, t, :], stats[:, t, :])
                last.then_inc(known, 1)
                dve.wait_ge(loaded, 32)
                dve.wait_ge(scaled, 1)
                for t in range(NT):
                    last = dve.scalar_tensor_tensor(acc[:, t, 0:D], acc[:, t, 0:D], moments[:, t, 0:1],
                                                    both[:, 0, :], ALU.subtract, ALU.mult)
                link(last)
                for t in range(NT):
                    last = dve.scalar_tensor_tensor(acc[:, t, 0:D], acc[:, t, 0:D], scale[:, t:t + 1],
                                                    both[:, 1, :], ALU.mult, ALU.add)
                link(last)
                dve.tensor_tensor(x[:], x[:], out, ALU.add)


def slot_tiles(items, experts):
    return (items + experts * 127) // 128


def gate(nc, c, wg, bg, experts, xn, normed, logits):
    with ExitStack() as stack:
        m = Memory(nc, stack, "g_")
        wgs, bias = m.sb("wgs", [128, KD, experts]), m.sb("bias", [P, experts])
        xs, xt = m.sb("xs", [P, TB, D]), m.sb("xt", [128, TB, KD * P])
        ps_t, ps_g = m.ps("ps_t", [128, 2, 512]), m.ps("ps_g", [P, 2, 512])
        names = "loaded staged turned xt_ready gated read stored"
        s = {n: m.sem(n) for n in names.split()}
        with nc.Block() as block:

            @block.sync
            def _(sp):
                sp.dma_start(wgs[:], wg.rearrange("(k p) n -> p k n", p=128)).then_inc(s["loaded"], 16)
                sp.dma_start(bias[:], bg.partition_broadcast(P)).then_inc(s["loaded"], 16)
                sp.dma_start(normed.rearrange("(t p) n -> p t n", p=P), xn[:]).then_inc(s["stored"], 16)
                sp.wait_ge(s["stored"], 16)

            @block.gpsimd
            def _(pool):
                with pool.Fori(0, TI) as i:
                    for j in range(TB):
                        pool.wait_ge(s["turned"], i * TB + j + 1)
                        pool.tensor_copy(xs[:, j:j + 1, :], xn[:, bass.ds(i * TB + j, 1), :]).then_inc(s["staged"], 1)

            @block.scalar
            def _(act):
                with act.Fori(0, TI) as i:
                    for j in range(TB):
                        act.wait_ge(s["turned"], i * TB + j + 1 + TB)
                        act.copy(xt[:, j, :], ps_t[:, j % 2, 0:KD * P]).then_inc(s["xt_ready"], 1)

            @block.tensor
            def _(pe):
                pe.sem_inc(s["turned"], TB)
                pe.sem_inc(s["xt_ready"], 1)
                pe.sem_inc(s["read"], 1)
                pe.wait_ge(s["loaded"], 32)
                with pe.Fori(0, TI) as i:
                    for j in range(TB):
                        n = i * TB + j
                        pe.wait_ge(s["staged"], n + 1)
                        pe.wait_ge(s["xt_ready"], since(n, j))
                        for k in range(KD):
                            last = pe.transpose(ps_t[:, j % 2, k * P:(k + 1) * P], xs[:, j, 128 * k:128 * k + 128],
                                                c["ident"][0:P, 0:P])
                        last.then_inc(s["turned"], 1)
                        pe.wait_ge(s["xt_ready"], n + 2)
                        pe.wait_ge(s["read"], since(n, j))
                        for k in range(KD):
                            last = pe.matmul(ps_g[:, j % 2, 0:experts], xt[:, j, k * P:(k + 1) * P], wgs[:, k, :],
                                             start=(k == 0), stop=(k == KD - 1))
                        last.then_inc(s["gated"], 1)

            @block.vector
            def _(dve):
                dve.wait_ge(s["loaded"], 32)
                with dve.Fori(0, TI) as i:
                    for j in range(TB):
                        n = i * TB + j
                        dve.wait_ge(s["gated"], n + 1)
                        dve.tensor_tensor(logits[:, bass.ds(n, 1), :], ps_g[:, j % 2, 0:experts], bias[:],
                                          ALU.add).then_inc(s["read"], 1)


def choose(nc, c, experts, picks, logits, chosen, prob):
    with ExitStack() as stack:
        m = Memory(nc, stack, "c_")
        best = m.sb("best", [P, picks, NT])
        rank, named = m.sb("rank", [P, NT, experts]), m.sb("named", [P, NT, experts])
        gap, e, total = m.sb("gap", [P, NT]), m.sb("e", [P, NT]), m.sb("total", [P, NT])
        step, gapped, raised = m.sem("step"), m.sem("gapped"), m.sem("raised")
        full = [P, NT, experts]
        with nc.Block() as block:

            @block.scalar
            def _(act):
                if picks == 2:
                    act.wait_ge(gapped, 1)
                    act.activation(e[:], gap[:], ACT.Exp).then_inc(raised, 1)

            @block.vector
            def _(dve):
                link = link_of(dve, step)
                link(dve.tensor_scalar(rank[:], c["count"][0:P, 0:experts].unsqueeze(1).to_broadcast(full),
                                       float(experts), None, ALU.subtract))
                for q in range(picks):
                    link(dve.tensor_reduce(best[:, q, :], logits[:], AX.X, ALU.max))
                    link(dve.tensor_tensor(named[:], logits[:], best[:, q, :].unsqueeze(2).to_broadcast(full), ALU.is_equal))
                    link(dve.tensor_tensor(named[:], named[:], rank[:], ALU.mult))
                    link(dve.tensor_reduce(chosen[:, :, q:q + 1].rearrange("p t q -> p (t q)") if picks == 1 else chosen[:, :, q],
                                           named[:], AX.X, ALU.min))
                    if q + 1 < picks:
                        link(dve.tensor_tensor(named[:], rank[:], chosen[:, :, q].unsqueeze(2).to_broadcast(full), ALU.is_equal))
                        link(dve.scalar_tensor_tensor(logits[:], named[:], -3e38, logits[:], ALU.mult, ALU.add))
                link(dve.tensor_scalar(chosen[:], chosen[:], float(experts), None, ALU.add))
                if picks == 2:
                    dve.tensor_tensor(gap[:], best[:, 1, :], best[:, 0, :], ALU.subtract).then_inc(gapped, 1)
                    dve.wait_ge(raised, 1)
                    link(dve.tensor_scalar(total[:], e[:], 1.0, None, ALU.add))
                    link(dve.reciprocal(prob[:, :, 0], total[:]))
                    dve.tensor_tensor(prob[:, :, 1], e[:], prob[:, :, 0], ALU.mult)


def route(nc, c, experts, picks, chosen, slots, place_i, expert_i, token_i):
    C = NT * picks
    T = slot_tiles(N * picks, experts)
    with ExitStack() as stack:
        m = Memory(nc, stack, "r_")
        member, rank = m.sb("member", [P, experts, C]), m.sb("rank", [P, experts, C])
        tally = m.sb("tally", [P, experts])
        cnt, prior = m.sb("cnt", [128, experts]), m.sb("prior", [P, experts])
        cnt_i = m.sb("cnt_i", [128, experts], I32)
        tiles, upto = m.sb("tiles", [128, experts]), m.sb("upto", [128, experts])
        base, place_f = m.sb("base", [P, experts]), m.sb("place_f", [P, C])
        past, expert_f = m.sb("past", [1, T, experts]), m.sb("expert_f", [1, T])
        node = m.sb("node", [P, NT, picks], I32)
        none = m.sb("none", [T, 128], I32)
        list_i, list_f = m.sb("list_i", [T, 128], I32), m.sb("list_f", [T, 128])
        ps_cnt, ps_prior, ps_list = m.ps("ps_cnt", [128, experts]), m.ps("ps_prior", [P, experts]), m.ps("ps_list", [128, T])
        names = "emptied wiped step tallied summed placed scattered listed floated turned"
        s = {n: m.sem(n) for n in names.split()}
        with nc.Block() as block:

            @block.sync
            def _(sp):
                sp.wait_ge(s["emptied"], 1)
                sp.dma_start(slots.rearrange("(t e) a -> t (e a)", e=128), none[:]).then_inc(s["wiped"], 16)
                sp.wait_ge(s["wiped"], 16)
                sp.wait_ge(s["scattered"], 16 * C)
                sp.dma_start(list_i[:], slots.rearrange("(t e) a -> t (e a)", e=128)).then_inc(s["listed"], 16)

            @block.gpsimd
            def _(pool):
                pool.memset(none[:], 0).then_inc(s["emptied"], 1)
                pool.iota(node[:], [[P, NT], [0, picks]], base=0, channel_multiplier=1).then_inc(s["emptied"], 1)
                pool.wait_ge(s["emptied"], 2)
                pool.wait_ge(s["wiped"], 16)
                pool.wait_ge(s["placed"], 1)
                flat = node[:].rearrange("p t q -> p (t q)")
                for k in range(C):
                    pool.indirect_dma_start(out=slots, out_offset=bass.IndirectOffsetOnAxis(ap=place_i[:, k:k + 1], axis=0),
                                            in_=flat[:, k:k + 1], in_offset=None).then_inc(s["scattered"], 16)

            @block.vector
            def _(dve):
                link = link_of(dve, s["step"])
                full = [P, experts, C]
                link(dve.tensor_tensor(member[:], chosen[:].rearrange("p t q -> p (t q)").unsqueeze(1).to_broadcast(full),
                                       c["count"][0:P, 0:experts].unsqueeze(2).to_broadcast(full), ALU.is_equal))
                link(dve.tensor_reduce(tally[:], member[:], AX.X, ALU.add))
                dve.sem_inc(s["tallied"], 1)
                flat = "p b c -> p (b c)"
                link(dve.tensor_tensor_scan(rank[:].rearrange(flat), member[:].rearrange(flat),
                                            member[:].rearrange(flat), 0.0, ALU.add, ALU.bypass))
                dve.wait_ge(s["summed"], 1)
                dve.tensor_copy(prior[:], ps_prior[:])
                link(dve.tensor_copy(cnt[:], ps_cnt[:]))
                link(dve.tensor_scalar(cnt_i[:], cnt[:], 127.0, None, ALU.add))
                link(dve.tensor_scalar(cnt_i[:], cnt_i[:], 7, None, ALU.arith_shift_right))
                link(dve.tensor_copy(tiles[:], cnt_i[:]))
                link(dve.tensor_tensor_scan(upto[:], tiles[:], tiles[:], 0.0, ALU.add, ALU.bypass))
                link(dve.tensor_tensor(base[:], upto[0:P, :], tiles[0:P, :], ALU.subtract))
                link(dve.tensor_scalar(base[:], base[:], 128.0, -1.0, ALU.mult, ALU.add))
                link(dve.tensor_tensor(base[:], base[:], prior[:], ALU.add))
                link(dve.tensor_tensor(base[:, 1:experts], base[:, 1:experts], rank[:, 0:experts - 1, C - 1], ALU.subtract))
                link(dve.tensor_tensor(rank[:], rank[:], base[:].unsqueeze(2).to_broadcast(full), ALU.add))
                link(dve.tensor_tensor(rank[:], rank[:], member[:], ALU.mult))
                link(dve.tensor_reduce(place_f[:], rank[:].rearrange("p b c -> p c b"), AX.X, ALU.add))
                dve.tensor_copy(place_i[:], place_f[:]).then_inc(s["placed"], 1)
                tall = [1, T, experts]
                link(dve.tensor_tensor(past[:], upto[0:1, :].unsqueeze(1).to_broadcast(tall),
                                       c["count"][0:1, 0:T].unsqueeze(2).to_broadcast(tall), ALU.is_le))
                link(dve.tensor_reduce(expert_f[:], past[:], AX.X, ALU.add))
                dve.tensor_scalar(expert_i[:], expert_f[:], float(experts - 1), None, ALU.min)
                dve.wait_ge(s["listed"], 16)
                dve.tensor_copy(list_f[:], list_i[:]).then_inc(s["floated"], 1)
                dve.wait_ge(s["turned"], 1)
                dve.tensor_copy(token_i[:], ps_list[:])

            @block.tensor
            def _(pe):
                pe.wait_ge(s["tallied"], 1)
                pe.matmul(ps_cnt[:], c["ones"][0:P, :], tally[:], start=True, stop=True)
                pe.matmul(ps_prior[:], c["before"][0:P, 0:P], tally[:], start=True, stop=True).then_inc(s["summed"], 1)
                pe.wait_ge(s["floated"], 1)
                pe.transpose(ps_list[:], list_f[:], c["ident"][0:T, 0:T]).then_inc(s["turned"], 1)


def split_biases(nc, experts, biases, pick):
    with ExitStack() as stack:
        m = Memory(nc, stack, "s_")
        number_i, number = m.sb("number_i", [96, experts], I32), m.sb("number", [96, experts])
        row_i, row = m.sb("row_i", [96, 1], I32), m.sb("row", [96, 1])
        same = m.sb("same", [96, experts])
        whole = [m.sb(f"whole{n}", [96, src.shape[1]]) for n, (src, _) in enumerate(biases)]
        part = [m.sb(f"part{n}", [96, src.shape[1]], BF16) for n, (src, _) in enumerate(biases)]
        counted, wiped, loaded, step = (m.sem(n) for n in "counted wiped loaded step".split())
        with nc.Block() as block:

            @block.gpsimd
            def _(pool):
                pool.iota(number_i[:], [[1, experts]], base=0, channel_multiplier=0).then_inc(counted, 1)
                for part_no in range(3):
                    pool.wait_ge(counted, part_no + 1)
                    pool.iota(row_i[32 * part_no:32 * part_no + 32, :], [[0, 1]], base=0, channel_multiplier=1
                              ).then_inc(counted, 1)

            @block.sync
            def _(sp):
                sp.wait_ge(wiped, len(biases))
                for n, (src, _) in enumerate(biases):
                    for part_no in range(3):
                        sp.dma_start(whole[n][32 * part_no:32 * part_no + experts, :], src).then_inc(loaded, 16)

            @block.vector
            def _(dve):
                link = link_of(dve, step)
                for n in range(len(biases)):
                    dve.memset(whole[n][:], 0.0).then_inc(wiped, 1)
                dve.wait_ge(counted, 4)
                dve.tensor_copy(number[:], number_i[:])
                link(dve.tensor_copy(row[:], row_i[:]))
                link(dve.tensor_scalar(same[:], number[:], row[:, 0:1], None, ALU.is_equal))
                dve.tensor_copy(pick[:], same[:].unsqueeze(2).to_broadcast([96, experts, 128]))
                dve.wait_ge(loaded, 16 * 3 * len(biases))
                for n, (_, target) in enumerate(biases):
                    for part_no in range(3):
                        rows = slice(32 * part_no, 32 * part_no + 32)
                        link(dve.tensor_copy(part[n][:], whole[n][:]))
                        dve.tensor_copy(target[rows, :], part[n][rows, :])
                        link(dve.tensor_tensor(whole[n][:], whole[n][:], part[n][:], ALU.subtract))


def experts_wide(nc, c, w, normed, token_i, expert_i, results):
    EX, H = 8, 1024
    HC = H // 128
    T = slot_tiles(2 * N, EX)
    with ExitStack() as stack:
        m = Memory(nc, stack, "x_")
        b1, b2, pick = m.sb("b1", [96, H], BF16), m.sb("b2", [96, D], BF16), m.sb("pick", [96, EX, 128], BF16)
        split_biases(nc, EX, [(w["b1"], b1), (w["b2"], b2)], pick)
        w1, w2 = m.sb("w1", [128, EX, KD, H]), m.sb("w2", [128, EX, HC, D])
        idx = m.sb("idx", [128, 2], I32)
        got, xt = m.sb("got", [128, 2, D]), m.sb("xt", [128, D])
        hs, ht = m.sb("hs", [128, H]), m.sb("ht", [128, HC, 128])
        y = m.sb("y", [128, 2, D])
        ps_x, ps_h = m.ps("ps_x", [128, 512]), m.ps("ps_h", [128, 2, 512])
        ps_t, ps_y = m.ps("ps_t", [128, 2, 512]), m.ps("ps_y", [128, 512])
        names = ("loaded indexed rounds rounds_pe x_turned xt_ready hid hs_ready h_turned ht_ready y_ready y_read")
        s = {n: m.sem(n) for n in names.split()}
        gathered = [m.sem(f"gathered{r}") for r in range(2)]
        stored = [m.sem(f"stored{r}") for r in range(2)]
        with nc.Block() as block:

            @block.sync
            def _(sp):
                for e in range(EX):
                    sp.dma_start(w1[:, e, :, :], w["w1"][e].rearrange("(k p) n -> p k n", p=128)).then_inc(s["loaded"], 16)
                    sp.dma_start(w2[:, e, :, :], w["w2"][e].rearrange("(k p) n -> p k n", p=128)).then_inc(s["loaded"], 16)
                for r in range(2):
                    sp.sem_inc(stored[r], 16)
                with sp.Fori(0, T // 2) as i:
                    for r in range(2):
                        t = i * 2 + r
                        sp.wait_ge(s["y_read"], t + 2)
                        sp.dma_start(results[bass.ds(t * 128, 128), :], y[:, r, :]).then_inc(stored[r], 16)
                for r in range(2):
                    sp.wait_ge(stored[r], 16 * (T // 2 + 1))

            @block.gpsimd
            def _(pool):
                with pool.Fori(0, T // 2) as i:
                    for r in range(2):
                        t = i * 2 + r
                        pool.wait_ge(s["x_turned"], t + 1)
                        pool.tensor_copy(idx[:, r:r + 1], token_i[:, bass.ds(t, 1)]).then_inc(s["indexed"], 1)
                        pool.wait_ge(s["indexed"], t + 1)
                        pool.sem_inc(s["rounds"], 1)
                        pool.indirect_dma_start(out=got[:, r, :], out_offset=None, in_=normed,
                                                in_offset=bass.IndirectOffsetOnAxis(ap=idx[:, r:r + 1], axis=0)
                                                ).then_inc(gathered[r], 16)

            @block.tensor
            def _(pe):
                pe.sem_inc(s["x_turned"], 2)
                pe.sem_inc(s["xt_ready"], 1)
                pe.sem_inc(s["hs_ready"], 2)
                pe.sem_inc(s["ht_ready"], 2)
                pe.sem_inc(s["y_read"], 1)
                pe.wait_ge(s["loaded"], 16 * (2 * EX))
                with pe.Fori(0, T // 2) as i:
                    for r in range(2):
                        t = i * 2 + r
                        e = pe.value_load(expert_i[0:1, bass.ds(t, 1)], min_val=0, max_val=EX - 1)
                        pe.wait_ge(gathered[r], i * 16 + 16)
                        pe.wait_ge(s["xt_ready"], t + 1)
                        for k in range(KD):
                            last = pe.transpose(ps_x[:, 128 * k:128 * k + 128], got[:, r, 128 * k:128 * k + 128], c["ident"][:])
                        last.then_inc(s["x_turned"], 1)
                        pe.wait_ge(s["xt_ready"], t + 2)
                        for half in range(2):
                            cols = slice(512 * half, 512 * half + 512)
                            pe.wait_ge(s["hs_ready"], t * 2 + half + 1)
                            for k in range(KD):
                                pe.matmul(ps_h[:, half, :], xt[:, 128 * k:128 * k + 128], w1[:, bass.ds(e, 1), k, cols],
                                          start=(k == 0), stop=False)
                            pe.matmul(ps_h[:, half, :], pick[:, bass.ds(e, 1), :], b1[:, cols],
                                      start=False, stop=True).then_inc(s["hid"], 1)
                        for half in range(2):
                            pe.wait_ge(s["hs_ready"], t * 2 + half + 3)
                            pe.wait_ge(s["ht_ready"], t * 2 + half + 1)
                            for q in range(4):
                                last = pe.transpose(ps_t[:, half, 128 * q:128 * q + 128],
                                                    hs[:, 512 * half + 128 * q:512 * half + 128 * q + 128], c["ident"][:])
                            last.then_inc(s["h_turned"], 1)
                        pe.wait_ge(s["y_read"], t + 1)
                        for q in range(HC):
                            if q % 4 == 0:
                                pe.wait_ge(s["ht_ready"], t * 2 + q // 4 + 3)
                            pe.matmul(ps_y[:, 0:D], ht[:, q, :], w2[:, bass.ds(e, 1), q, :], start=(q == 0), stop=False)
                        pe.matmul(ps_y[:, 0:D], pick[:, bass.ds(e, 1), :], b2[:], start=False, stop=True
                                  ).then_inc(s["y_ready"], 1)

            @block.scalar
            def _(act):
                with act.Fori(0, T // 2) as i:
                    for r in range(2):
                        t = i * 2 + r
                        act.wait_ge(s["x_turned"], t + 3)
                        act.copy(xt[:], ps_x[:, 0:D]).then_inc(s["xt_ready"], 1)
                        for half in range(2):
                            act.wait_ge(s["hid"], t * 2 + half + 1)
                            act.activation(hs[:, 512 * half:512 * half + 512], ps_h[:, half, :], ACT.Relu).then_inc(s["hs_ready"], 1)

            @block.vector
            def _(dve):
                with dve.Fori(0, T // 2) as i:
                    for r in range(2):
                        t = i * 2 + r
                        for half in range(2):
                            dve.wait_ge(s["h_turned"], t * 2 + half + 1)
                            dve.tensor_copy(ht[:, 4 * half:4 * half + 4, :], ps_t[:, half, :]).then_inc(s["ht_ready"], 1)
                        dve.wait_ge(s["y_ready"], t + 1)
                        dve.wait_ge(stored[r], i * 16 + 16)
                        dve.tensor_copy(y[:, r, :], ps_y[:, 0:D]).then_inc(s["y_read"], 1)


def experts_narrow(nc, c, w, normed, token_i, expert_i, results):
    EX, H = 32, 64
    T = slot_tiles(N, EX)
    with ExitStack() as stack:
        m = Memory(nc, stack, "x_")
        w1, w2 = m.sb("w1", [128, EX, KD, H]), m.sb("w2", [H, EX, D])
        b1, b2, pick = m.sb("b1", [96, H], BF16), m.sb("b2", [96, D], BF16), m.sb("pick", [96, EX, 128], BF16)
        split_biases(nc, EX, [(w["b1"], b1), (w["b2"], b2)], pick)
        idx = m.sb("idx", [128, 2], I32)
        got, xt = m.sb("got", [128, 2, D]), m.sb("xt", [128, D])
        hs, ht = m.sb("hs", [128, H]), m.sb("ht", [H, 128])
        y = m.sb("y", [128, 2, D])
        ps_x, ps_h = m.ps("ps_x", [128, 512]), m.ps("ps_h", [128, 512])
        ps_t, ps_y = m.ps("ps_t", [H, 512]), m.ps("ps_y", [128, 512])
        names = ("loaded indexed rounds rounds_pe x_turned xt_ready hid hs_ready h_turned ht_ready y_ready y_read")
        s = {n: m.sem(n) for n in names.split()}
        gathered = [m.sem(f"gathered{r}") for r in range(2)]
        stored = [m.sem(f"stored{r}") for r in range(2)]
        with nc.Block() as block:

            @block.sync
            def _(sp):
                for k in range(KD):
                    sp.dma_start(w1[:, :, k, :], w["w1"][:, 128 * k:128 * k + 128, :].rearrange("e p n -> p e n")
                                 ).then_inc(s["loaded"], 16)
                sp.dma_start(w2[:], w["w2"].rearrange("e p n -> p e n")).then_inc(s["loaded"], 16)
                for r in range(2):
                    sp.sem_inc(stored[r], 16)
                with sp.Fori(0, T // 2) as i:
                    for r in range(2):
                        t = i * 2 + r
                        sp.wait_ge(s["y_read"], t + 2)
                        sp.dma_start(results[bass.ds(t * 128, 128), :], y[:, r, :]).then_inc(stored[r], 16)
                for r in range(2):
                    sp.wait_ge(stored[r], 16 * (T // 2 + 1))

            @block.gpsimd
            def _(pool):
                with pool.Fori(0, T // 2) as i:
                    for r in range(2):
                        t = i * 2 + r
                        pool.wait_ge(s["x_turned"], t + 1)
                        pool.tensor_copy(idx[:, r:r + 1], token_i[:, bass.ds(t, 1)]).then_inc(s["indexed"], 1)
                        pool.wait_ge(s["indexed"], t + 1)
                        pool.sem_inc(s["rounds"], 1)
                        pool.indirect_dma_start(out=got[:, r, :], out_offset=None, in_=normed,
                                                in_offset=bass.IndirectOffsetOnAxis(ap=idx[:, r:r + 1], axis=0)
                                                ).then_inc(gathered[r], 16)

            @block.tensor
            def _(pe):
                pe.sem_inc(s["x_turned"], 2)
                for one in ("xt_ready", "hs_ready", "ht_ready", "y_read"):
                    pe.sem_inc(s[one], 1)
                pe.wait_ge(s["loaded"], 16 * 3)
                with pe.Fori(0, T // 2) as i:
                    for r in range(2):
                        t = i * 2 + r
                        e = pe.value_load(expert_i[0:1, bass.ds(t, 1)], min_val=0, max_val=EX - 1)
                        pe.wait_ge(gathered[r], i * 16 + 16)
                        pe.wait_ge(s["xt_ready"], t + 1)
                        for k in range(KD):
                            last = pe.transpose(ps_x[:, 128 * k:128 * k + 128], got[:, r, 128 * k:128 * k + 128], c["ident"][:])
                        last.then_inc(s["x_turned"], 1)
                        pe.wait_ge(s["xt_ready"], t + 2)
                        pe.wait_ge(s["hs_ready"], t + 1)
                        for k in range(KD):
                            pe.matmul(ps_h[:, 0:H], xt[:, 128 * k:128 * k + 128], w1[:, bass.ds(e, 1), k, :],
                                      start=(k == 0), stop=False)
                        pe.matmul(ps_h[:, 0:H], pick[:, bass.ds(e, 1), :], b1[:],
                                  start=False, stop=True).then_inc(s["hid"], 1)
                        pe.wait_ge(s["hs_ready"], t + 2)
                        pe.wait_ge(s["ht_ready"], t + 1)
                        pe.sem_inc(s["rounds_pe"], 1)
                        pe.transpose(ps_t[:, 0:128], hs[:], c["ident"][:]).then_inc(s["h_turned"], 1)
                        pe.wait_ge(s["ht_ready"], t + 2)
                        pe.wait_ge(s["y_read"], t + 1)
                        pe.matmul(ps_y[:, 0:D], ht[:], w2[:, bass.ds(e, 1), :], start=True, stop=False)
                        pe.matmul(ps_y[:, 0:D], pick[:, bass.ds(e, 1), :], b2[:], start=False, stop=True
                                  ).then_inc(s["y_ready"], 1)

            @block.scalar
            def _(act):
                with act.Fori(0, T // 2) as i:
                    for r in range(2):
                        t = i * 2 + r
                        act.wait_ge(s["x_turned"], t + 3)
                        act.copy(xt[:], ps_x[:, 0:D]).then_inc(s["xt_ready"], 1)
                        act.wait_ge(s["hid"], t + 1)
                        act.activation(hs[:], ps_h[:, 0:H], ACT.Relu).then_inc(s["hs_ready"], 1)

            @block.vector
            def _(dve):
                with dve.Fori(0, T // 2) as i:
                    for r in range(2):
                        t = i * 2 + r
                        dve.wait_ge(s["h_turned"], t + 1)
                        dve.tensor_copy(ht[:], ps_t[:, 0:128]).then_inc(s["ht_ready"], 1)
                        dve.wait_ge(s["y_ready"], t + 1)
                        dve.wait_ge(stored[r], i * 16 + 16)
                        dve.tensor_scalar(y[:, r, :], ps_y[:, 0:D], 0.0, None, ALU.max).then_inc(s["y_read"], 1)


def combine(nc, c, picks, results, place_i, prob, x):
    with ExitStack() as stack:
        m = Memory(nc, stack, "o_")
        got = m.sb("got", [P, TB, picks, D])
        idx = m.sb("idx", [P, TB, picks], I32)
        indexed, rounds, added = m.sem("indexed"), m.sem("rounds"), m.sem("added")
        first_added = m.sem("first_added")
        fetched = [m.sem(f"fetched{j}") for j in range(TB)]
        with nc.Block() as block:

            @block.gpsimd
            def _(pool):
                with pool.Fori(0, TI) as i:
                    for j in range(TB):
                        n = i * TB + j
                        pool.wait_ge(added, n + 1)
                        pool.tensor_copy(idx[:, j, :], place_i[:, bass.ds(n * picks, picks)]).then_inc(indexed, 1)
                        pool.wait_ge(indexed, n + 1)
                        pool.sem_inc(rounds, 1)
                        for q in range(picks):
                            pool.indirect_dma_start(out=got[:, j, q, :], out_offset=None, in_=results,
                                                    in_offset=bass.IndirectOffsetOnAxis(ap=idx[:, j, q:q + 1], axis=0)
                                                    ).then_inc(fetched[j], 16)

            @block.vector
            def _(dve):
                dve.sem_inc(added, TB)
                with dve.Fori(0, TI) as i:
                    for j in range(TB):
                        at = x[:, bass.ds(i * TB + j, 1), :]
                        dve.wait_ge(fetched[j], i * (16 * picks) + 16 * picks)
                        if picks == 1:
                            dve.tensor_tensor(at, at, got[:, j, 0:1, :], ALU.add).then_inc(added, 1)
                        else:
                            for q in range(2):
                                last = dve.scalar_tensor_tensor(at, got[:, j, q:q + 1, :], prob[:, bass.ds(i * TB + j, 1), q], at,
                                                                ALU.mult, ALU.add)
                                if q == 0:
                                    last.then_inc(first_added, 1)
                                    dve.wait_ge(first_added, i * TB + j + 1)
                            last.then_inc(added, 1)

WEIGHTS = {
    "L0_gnn_W": (D, D), "L0_gnn_att_src": (D,), "L0_gnn_att_dst": (D,), "L0_gnn_bias": (D,),
    "L0_mix_Wqkv": (D, 3 * D), "L0_mix_ln1_g": (D,), "L0_mix_ln1_b": (D,), "L0_mix_W1": (D, D),
    "L0_mix_b1": (128, KD), "L0_mix_W2": (D, D), "L0_mix_b2": (D,), "L0_mix_ln2_g": (D,), "L0_mix_ln2_b": (D,),
    "L0_ffn_Wg": (D, 8), "L0_ffn_bg": (8,), "L0_ffn_W1": (8, D, 1024), "L0_ffn_b1": (8, 1024),
    "L0_ffn_W2": (8, 1024, D), "L0_ffn_b2": (8, D),
    "L1_gnn_W": (D, D), "L1_gnn_a_src": (D,), "L1_gnn_a_dst": (D,), "L1_gnn_bias_gat": (D,),
    "L1_gnn_W_res": (D, D), "L1_gnn_b_res": (D,), "L1_gnn_gamma": (D,), "L1_gnn_beta": (D,),
    "L1_mix_Wq": (D, D), "L1_mix_Wk": (D, D), "L1_mix_Wv": (D, D), "L1_mix_Wm": (D, D),
    "L1_mix_W1": (2 * D, 2 * D), "L1_mix_W2": (2 * D, D), "L1_mix_g1": (D,), "L1_mix_b1": (D,),
    "L1_mix_g2": (D,), "L1_mix_b2": (D,),
    "L1_ffn_router_w": (D, 32), "L1_ffn_router_b": (32,), "L1_ffn_W1": (32, D, 64), "L1_ffn_b1": (32, 64),
    "L1_ffn_W2": (32, 64, D), "L1_ffn_b2": (32, D),
}


def build_program(nc, x_in, src, dst, w, out):
    Memory.used.clear()
    Memory.semaphores.clear()
    edge_tiles = nc.dram_tensor("edge_tiles", (ET, 256), I32).ap()
    rows = nc.dram_tensor("source_rows", (N, ROW), F32).ap()
    normed = nc.dram_tensor("normed_rows", (N, D), F32).ap()
    T = slot_tiles(2 * N, 8)
    slots = nc.dram_tensor("slots", (T * 128, 1), I32).ap()
    results = nc.dram_tensor("results", (T * 128, D), F32).ap()
    with ExitStack() as stack:
        keep = Memory(nc, stack, "")
        c = build_constants(nc, keep)
        ends = keep.sb("ends", [128, NT + 1])
        win = {"src": keep.sb("win_src", [128, WG, 128], I32), "dst": keep.sb("win_dst", [128, WG, 128]),
               "bucket": keep.sb("win_bucket", [1, WG, 128], I32)}
        sort_edges(nc, c, src, dst, edge_tiles, ends)
        list_windows(nc, c, edge_tiles, ends, win)
        x = keep.sb("x", [P, NT, D])
        loaded = keep.sem("x_loaded")
        with nc.Block() as block:

            @block.sync
            def _(sp):
                sp.dma_start(x[:], x_in.rearrange("(t p) n -> p t n", p=P)).then_inc(loaded, 16)
                sp.wait_ge(loaded, 16)

        for layer in range(2):
            with ExitStack() as stack1:
                L = Memory(nc, stack1, f"l{layer}_")
                xn = L.sb("xn", [P, NT, D])
                qt, kv_block = L.sb("qt", [128, KD, N]), L.sb("kv_block", [128, KD, 132])
                layer_norm_all(nc, c, x, xn)
                with ExitStack() as stack2:
                    A = Memory(nc, stack2, f"a{layer}_")
                    scores, dst_parts = A.sb("scores", [P, NT, 16]), A.sb("dst_parts", [P, NT + 1, 48], BF16)
                    acc = A.sb("acc", [P, NT + 1, ROW])
                    if layer == 0:
                        qkv = w["L0_mix_Wqkv"]
                        weights = dict(proj=w["L0_gnn_W"], att_src=w["L0_gnn_att_src"], att_dst=w["L0_gnn_att_dst"],
                                       q=qkv[:, 0:D], k=qkv[:, D:2 * D], v=qkv[:, 2 * D:3 * D], v_scale=1.0)
                        project(nc, c, xn, weights, 8, rows, scores, qt, kv_block, acc, None)
                        with ExitStack() as stack3:
                            acc_odd = Memory(nc, stack3, f"b{layer}_").sb("acc_odd", [P, NT + 1, ROW])
                            bound_scores(nc, c, 8, scores, dst_parts, acc, acc_odd, False)
                            edges(nc, c, 8, rows, win, dst_parts, acc, acc_odd)
                        finish_gat_relu(nc, c, dict(gat_bias=w["L0_gnn_bias"]), x, acc)
                    else:
                        res = A.sb("res", [P, NT, D])
                        weights = dict(proj=w["L1_gnn_W"], att_src=w["L1_gnn_a_src"], att_dst=w["L1_gnn_a_dst"],
                                       q=w["L1_mix_Wq"], k=w["L1_mix_Wk"], v=w["L1_mix_Wv"], res=w["L1_gnn_W_res"],
                                       bias_gat=w["L1_gnn_bias_gat"], b_res=w["L1_gnn_b_res"], v_scale=1.0 / N)
                        project(nc, c, xn, weights, 4, rows, scores, qt, kv_block, acc, res)
                        with ExitStack() as stack3:
                            acc_odd = Memory(nc, stack3, f"b{layer}_").sb("acc_odd", [P, NT + 1, ROW])
                            bound_scores(nc, c, 4, scores, dst_parts, acc, acc_odd, True)
                            edges(nc, c, 4, rows, win, dst_parts, acc, acc_odd)
                        finish_gat_norm(nc, c, dict(gamma=w["L1_gnn_gamma"], beta=w["L1_gnn_beta"]), x, acc, res)
                if layer == 0:
                    mixer = dict(w1=w["L0_mix_W1"], b1=w["L0_mix_b1"], w2=w["L0_mix_W2"], b2=w["L0_mix_b2"],
                                 ln1_g=w["L0_mix_ln1_g"], ln1_b=w["L0_mix_ln1_b"],
                                 ln2_g=w["L0_mix_ln2_g"], ln2_b=w["L0_mix_ln2_b"])
                    mix_elu_gelu(nc, c, mixer, x, xn, qt, kv_block)
                else:
                    mixer = dict(wm=w["L1_mix_Wm"], w1=w["L1_mix_W1"], w2=w["L1_mix_W2"], g1=w["L1_mix_g1"],
                                 b1=w["L1_mix_b1"], g2=w["L1_mix_g2"], b2=w["L1_mix_b2"])
                    mix_concat(nc, c, mixer, x, xn, qt, kv_block)
            experts, picks = (8, 2) if layer == 0 else (32, 1)
            names = ("L0_ffn_Wg", "L0_ffn_bg", "L0_ffn_") if layer == 0 else ("L1_ffn_router_w", "L1_ffn_router_b", "L1_ffn_")
            with ExitStack() as stack1:
                F = Memory(nc, stack1, f"f{layer}_")
                place_i, expert_i = F.sb("place", [P, NT * picks], I32), F.sb("expert", [1, T], I32)
                token_i = F.sb("token", [128, T], I32)
                prob = F.sb("prob", [P, NT, 2])
                with ExitStack() as stack2:
                    G = Memory(nc, stack2, f"g{layer}_")
                    xn, logits = G.sb("xn", [P, NT, D]), G.sb("logits", [P, NT, experts])
                    chosen = G.sb("chosen", [P, NT, picks])
                    layer_norm_all(nc, c, x, xn)
                    gate(nc, c, w[names[0]], w[names[1]], experts, xn, normed, logits)
                    choose(nc, c, experts, picks, logits, chosen, prob)
                    route(nc, c, experts, picks, chosen, slots, place_i, expert_i, token_i)
                parts = {n: w[names[2] + o] for n, o in (("w1", "W1"), ("b1", "b1"), ("w2", "W2"), ("b2", "b2"))}
                run = experts_wide if layer == 0 else experts_narrow
                run(nc, c, parts, normed, token_i, expert_i, results)
                combine(nc, c, picks, results, place_i, prob, x)
            clear_semaphores(nc)
        with nc.Block() as block:
            stored = keep.sem("x_stored")

            @block.sync
            def _(sp):
                sp.dma_start(out.rearrange("(t p) n -> p t n", p=P), x[:]).then_inc(stored, 16)
                sp.wait_ge(stored, 16)


_TURNED = ("L0_mix_Wqkv", "L0_mix_W1", "L0_mix_W2", "L0_ffn_Wg", "L0_ffn_W1", "L0_ffn_W2", "L1_ffn_router_w")


def kernel(**inputs):
    import numpy as _np
    import concourse.bacc as _bacc
    from concourse import mybir as _mybir
    from concourse.bass_utils import run_bass_kernel_spmd as _run

    nc = _bacc.Bacc("TRN2", target_bir_lowering=False, num_devices=1)
    arrays, args = {}, {}
    for name in ("x", "src", "dst", *WEIGHTS):
        a = _np.asarray(inputs[name])
        if name in _TURNED:
            a = _np.swapaxes(a, -1, -2)
        if name == "L0_mix_b1":
            a = a.reshape(KD, 128).T
        elif name in WEIGHTS:
            a = a.reshape(WEIGHTS[name])
        arrays[f"in_{name}"] = _np.ascontiguousarray(a)
        args[name] = nc.dram_tensor(f"in_{name}", a.shape, _mybir.dt.from_np(a.dtype), kind="ExternalInput").ap()
    out = nc.dram_tensor("out_x", (N, D), F32, kind="ExternalOutput").ap()
    build_program(nc, args["x"], args["src"], args["dst"], {n: args[n] for n in WEIGHTS}, out)
    r = _run(nc, [arrays], core_ids=[0])
    return r.results[0]["out_x"]
```

```python
from contextlib import ExitStack

import concourse.bass as bass
from concourse import mybir

F32 = mybir.dt.float32
I32 = mybir.dt.int32
BF16 = mybir.dt.bfloat16
ALU = mybir.AluOpType
ACT = mybir.ActivationFunctionType
AX = mybir.AxisListType

N = 3125
D = 256
E = 50000
P = 125
NT = N // P
KD = D // 128
EC = E // P
ET = -(-E // 128)
EPAD = ET * 128 - E
NW = ET + NT
WG = -(-NW // 128)
ROW = D + 8
NOWHERE = 1 << 20


def link_of(eng, sem):
    done = [0]

    def link(ins):
        done[0] += 1
        ins.then_inc(sem, 1)
        eng.wait_ge(sem, done[0])

    return link


def small_numbers(nc, engine, row, most):
    _, numbers = nc.values_load_multi_w_load_instructions(
        row, engines=[engine], min_val=0, max_val=most,
        skip_runtime_bounds_check_because="the row counts bucket ends or experts passed, so it is 0 to most for any inputs")
    return numbers


class Memory:

    used = {}
    semaphores = []

    def __init__(self, nc, stack, prefix):
        self.nc, self.stack, self.prefix = nc, stack, prefix

    def name(self, name):
        name = self.prefix + name
        self.used[name] = self.used.get(name, 0) + 1
        return name if self.used[name] == 1 else f"{name}_{self.used[name]}"

    def sb(self, name, shape, dt=F32):
        return self.stack.enter_context(self.nc.sbuf_tensor(self.name(name), shape, dt))

    def ps(self, name, shape, dt=F32):
        return self.stack.enter_context(self.nc.psum_tensor(self.name(name), shape, dt))

    def sem(self, name):
        sem = self.nc.alloc_semaphore(name=self.name(name))
        self.semaphores.append(sem)
        return sem


def clear_semaphores(nc):
    nc.clear_and_free_semaphores(list(Memory.semaphores))
    nc.all_engine_barrier()
    Memory.semaphores.clear()


def build_constants(nc, keep, x_in, x, x_loaded):
    c = {}
    c["ident"] = keep.sb("ident", [128, 128])
    c["before"] = keep.sb("before", [128, 128])
    c["ones"] = keep.sb("ones", [128, 128])
    c["half"] = keep.sb("half", [128, NT])
    c["eps"] = keep.sb("eps", [128, NT])
    c["count"] = keep.sb("count", [128, 128])
    with ExitStack() as stack:
        m = Memory(nc, stack, "k_")
        count_i = m.sb("count_i", [128, 128], I32)
        made, counted = m.sem("made"), m.sem("counted")
        with nc.Block() as block:

            @block.sync
            def _(sp):
                sp.dma_start(x[:], x_in.rearrange("(t p) n -> p t n", p=P)).then_inc(x_loaded, 16)

            @block.gpsimd
            def _(pool):
                pool.memset(c["ident"][:], 0.0).then_inc(made, 1)
                pool.memset(c["ones"][:], 1.0).then_inc(made, 1)
                pool.memset(c["half"][:], -0.5)
                pool.memset(c["eps"][:], 1e-5)
                pool.iota(count_i[:], [[1, 128]], base=0, channel_multiplier=0).then_inc(counted, 1)
                pool.wait_ge(made, 2)
                pool.affine_select(out=c["ident"][:], in_=c["ident"][:], compare_op=ALU.not_equal, fill=1.0,
                                   base=0, pattern=[[-1, 128]], channel_multiplier=1).then_inc(made, 1)
                pool.affine_select(out=c["before"][:], in_=c["ones"][:], compare_op=ALU.is_gt, fill=0.0,
                                   base=0, pattern=[[1, 128]], channel_multiplier=-1).then_inc(made, 1)

            @block.vector
            def _(dve):
                dve.wait_ge(counted, 1)
                dve.tensor_copy(c["count"][:], count_i[:])
    return c


def sort_edges(nc, c, src, dst, edge_tiles, ends):
    with ExitStack() as stack:
        m = Memory(nc, stack, "s_")
        dst_i, src_i = m.sb("dst_i", [P, EC], I32), m.sb("src_i", [P, EC], I32)
        next_i = m.sb("next_i", [P, EC], I32)
        dst_f, next_f, drop = m.sb("dst_f", [P, EC]), m.sb("next_f", [P, EC]), m.sb("drop", [P, EC])
        pairs = m.sb("pairs", [P, EC, 2], I32)
        pad = m.sb("pad", [1, EPAD, 2], I32)
        bound = m.sb("bound", [128, NT])
        below = m.sb("below", [P, NT, EC])
        member = m.sb("member", [P, NT, EC])
        rank = m.sb("rank", [P, NT, EC])
        tally = m.sb("tally", [P, NT + 1])
        prior = m.sb("prior", [P, NT])
        base = m.sb("base", [P, NT])
        place_f, place_i = m.sb("place_f", [P, EC]), m.sb("place_i", [P, EC], I32)
        place_now, pair_now = m.sb("place_now", [P, 4], I32), m.sb("pair_now", [P, 4, 2], I32)
        flag_i = m.sb("flag_i", [1, 1], I32)
        ps_ends = m.ps("ps_ends", [128, NT + 1])
        ps_prior = m.ps("ps_prior", [P, NT])
        loaded, packed, padded = m.sem("loaded"), m.sem("packed"), m.sem("padded")
        step, tallied, summed, flagged = m.sem("step"), m.sem("tallied"), m.sem("summed"), m.sem("flagged")
        copied, placed, taken, scattered = m.sem("copied"), m.sem("placed"), m.sem("taken"), m.sem("scattered")
        rounds = m.sem("rounds")
        flat = edge_tiles.rearrange("t (e c) -> (t e) c", c=2)

        with nc.Block() as block:

            @block.sync
            def _(sp):
                sp.dma_start(dst_i[:], dst.rearrange("(p c) -> p c", p=P)).then_inc(loaded, 16)
                sp.dma_start(src_i[:], src.rearrange("(p c) -> p c", p=P)).then_inc(loaded, 16)
                sp.dma_start(next_i[0:P - 1, :], dst[1:1 + (P - 1) * EC].rearrange("(p c) -> p c", p=P - 1)
                             ).then_inc(loaded, 16)
                sp.dma_start(next_i[P - 1:P, 0:EC - 1], dst[(P - 1) * EC + 1:E].rearrange("(a c) -> a c", a=1)
                             ).then_inc(loaded, 16)
                sp.dma_start(next_i[P - 1:P, EC - 1:EC], dst[E - 1:E].rearrange("(a c) -> a c", a=1)
                             ).then_inc(loaded, 16)
                sp.wait_ge(packed, 2)
                sp.dma_start(flat[0:E, :].rearrange("(p c) t -> p (c t)", p=P),
                             pairs[:].rearrange("p c t -> p (c t)")).then_inc(copied, 16)
                sp.wait_ge(padded, 2)
                sp.dma_start(flat[E:E + EPAD, :].rearrange("(a c) t -> a (c t)", a=1),
                             pad[:].rearrange("a c t -> a (c t)")).then_inc(copied, 16)
                sp.wait_ge(copied, 32)

            @block.vector
            def _(dve):
                link = link_of(dve, step)
                dve.memset(pad[:, :, 0], NOWHERE).then_inc(padded, 1)
                dve.memset(pad[:, :, 1], 0).then_inc(padded, 1)
                dve.tensor_scalar(bound[:], c["count"][:, 0:NT], float(P), float(P), ALU.mult, ALU.add)
                dve.wait_ge(loaded, 80)
                dve.tensor_copy(pairs[:, :, 0], dst_i[:]).then_inc(packed, 1)
                dve.tensor_copy(pairs[:, :, 1], src_i[:]).then_inc(packed, 1)
                dve.tensor_copy(dst_f[:], dst_i[:])
                link(dve.tensor_copy(next_f[:], next_i[:]))
                link(dve.tensor_tensor(drop[:], next_f[:], dst_f[:], ALU.is_lt))
                dve.tensor_reduce(tally[:, NT:NT + 1], drop[:], AX.X, ALU.add)
                link(dve.tensor_tensor(below[:], dst_f[:].unsqueeze(1).to_broadcast([P, NT, EC]),
                                       bound[0:P, :].unsqueeze(2).to_broadcast([P, NT, EC]), ALU.is_lt))
                dve.tensor_reduce(tally[:, 0:NT], below[:], AX.X, ALU.add).then_inc(tallied, 1)
                dve.wait_ge(summed, 1)
                link(dve.tensor_copy(ends[:], ps_ends[:]))
                link(dve.tensor_copy(flag_i[:], ends[0:1, NT:NT + 1]))
                dve.nop().then_inc(flagged, 1)
                drops = dve.value_load(flag_i[0:1, 0:1], min_val=0, max_val=E)
                with dve.If(drops > 0):
                    dve.tensor_copy(member[:, 0:1, :], below[:, 0:1, :])
                    link(dve.tensor_tensor(member[:, 1:NT, :], below[:, 1:NT, :], below[:, 0:NT - 1, :],
                                           ALU.subtract))
                    link(dve.tensor_tensor_scan(rank[:].rearrange("p b c -> p (b c)"),
                                                member[:].rearrange("p b c -> p (b c)"),
                                                member[:].rearrange("p b c -> p (b c)"), 0.0, ALU.add, ALU.bypass))
                    link(dve.tensor_copy(prior[:], ps_prior[:]))
                    dve.tensor_scalar(base[:, 0:1], prior[:, 0:1], -1.0, None, ALU.add)
                    link(dve.tensor_tensor(base[:, 1:NT], prior[:, 1:NT], prior[:, 0:NT - 1], ALU.subtract))
                    link(dve.tensor_tensor(base[:, 1:NT], base[:, 1:NT], ends[0:P, 0:NT - 1], ALU.add))
                    link(dve.scalar_tensor_tensor(base[:, 1:NT], base[:, 1:NT], -1.0, tally[:, 0:NT - 1],
                                                  ALU.add, ALU.subtract))
                    link(dve.tensor_tensor(rank[:], rank[:], base[:].unsqueeze(2).to_broadcast([P, NT, EC]), ALU.add))
                    link(dve.tensor_tensor(rank[:], rank[:], member[:], ALU.mult))
                    link(dve.tensor_reduce(place_f[:], rank[:].rearrange("p b c -> p c b"), AX.X, ALU.add))
                    dve.tensor_copy(place_i[:], place_f[:]).then_inc(placed, 1)
                dve.nop()

            @block.tensor
            def _(pe):
                pe.wait_ge(tallied, 1)
                pe.matmul(ps_ends[:], c["ones"][0:P, :], tally[:], start=True, stop=True)
                pe.matmul(ps_prior[:], c["before"][0:P, 0:P], tally[:, 0:NT], start=True, stop=True).then_inc(summed, 1)

            @block.gpsimd
            def _(pool):
                pool.wait_ge(flagged, 1)
                drops = pool.value_load(flag_i[0:1, 0:1], min_val=0, max_val=E)
                pool.wait_ge(copied, 32)
                with pool.If(drops > 0):
                    pool.wait_ge(placed, 1)
                    with pool.Fori(0, EC // 4) as i:
                        pool.tensor_copy(place_now[:], place_i[:, bass.ds(i * 4, 4)]).then_inc(taken, 1)
                        pool.tensor_copy(pair_now[:], pairs[:, bass.ds(i * 4, 4), :]).then_inc(taken, 1)
                        pool.wait_ge(taken, i * 2 + 2)
                        pool.sem_inc(rounds, 1)
                        for j in range(4):
                            pool.indirect_dma_start(
                                out=flat[0:E, :], out_offset=bass.IndirectOffsetOnAxis(ap=place_now[:, j:j + 1], axis=0),
                                in_=pair_now[:, j, :], in_offset=None).then_inc(scattered, 16)
                        pool.wait_ge(scattered, i * 64 + 64)
                pool.nop()


def list_windows(nc, c, edge_tiles, ends, win):
    with ExitStack() as stack:
        m = Memory(nc, stack, "w_")
        number_i, number = m.sb("number_i", [128, WG], I32), m.sb("number", [128, WG])
        cum, cum_i = m.sb("cum", [128, NT + 1]), m.sb("cum_i", [128, 2, NT + 1], I32)
        edge = m.sb("edge", [128, 2, NT + 1])
        size, some = m.sb("size", [128, NT]), m.sb("some", [128, NT])
        tiles, upto = m.sb("tiles", [128, NT]), m.sb("upto", [128, NT])
        past, term = m.sb("past", [128, WG, NT]), m.sb("term", [128, WG, NT])
        bucket, begin, skip = m.sb("bucket", [128, WG]), m.sb("begin", [128, WG]), m.sb("skip", [128, WG])
        first_node = m.sb("first_node", [128, WG])
        begin_i, tile_i = m.sb("begin_i", [128, WG], I32), m.sb("tile_i", [128, WG], I32)
        got = m.sb("got", [128, WG, 256], I32)
        dst_w, src_w = m.sb("dst_w", [128, WG, 128]), m.sb("src_w", [128, WG, 128])
        ps_dst, ps_src = m.ps("ps_dst", [128, WG, 128]), m.ps("ps_src", [128, WG, 128])
        ps_bucket = m.ps("ps_bucket", [1, WG, 128])
        numbered, step, found = m.sem("numbered"), m.sem("step"), m.sem("found")
        gathered, split, turned = m.sem("gathered"), m.sem("split"), m.sem("turned")

        with nc.Block() as block:

            @block.gpsimd
            def _(pool):
                pool.iota(number_i[:], [[128, WG]], base=0, channel_multiplier=1).then_inc(numbered, 1)
                pool.wait_ge(found, 1)
                for g in range(WG):
                    pool.indirect_dma_start(out=got[:, g, :], out_offset=None, in_=edge_tiles,
                                            in_offset=bass.IndirectOffsetOnAxis(ap=tile_i[:, g:g + 1], axis=0)
                                            ).then_inc(gathered, 16)

            @block.vector
            def _(dve):
                link = link_of(dve, step)
                dve.wait_ge(numbered, 1)
                dve.tensor_copy(number[:], number_i[:])
                dve.memset(cum[:, 0:1], 0.0)
                link(dve.tensor_copy(cum[:, 1:NT + 1], ends[:, 0:NT]))
                dve.tensor_copy(cum_i[:, 0, :], cum[:])
                link(dve.tensor_scalar(cum_i[:, 1, :], cum[:], 127.0, None, ALU.add))
                link(dve.tensor_scalar(cum_i[:], cum_i[:], 7, None, ALU.arith_shift_right))
                dve.tensor_copy(edge[:], cum_i[:])
                link(dve.tensor_tensor(size[:], cum[:, 1:NT + 1], cum[:, 0:NT], ALU.subtract))
                dve.tensor_scalar(some[:], size[:], 0.0, None, ALU.is_gt)
                link(dve.tensor_tensor(tiles[:], edge[:, 1, 1:NT + 1], edge[:, 0, 0:NT], ALU.subtract))
                link(dve.tensor_tensor(tiles[:], tiles[:], some[:], ALU.mult))
                link(dve.tensor_tensor_scan(upto[:], tiles[:], tiles[:], 0.0, ALU.add, ALU.bypass))
                wide = [128, WG, NT]
                link(dve.tensor_tensor(past[:], upto[:].unsqueeze(1).to_broadcast(wide),
                                       number[:].unsqueeze(2).to_broadcast(wide), ALU.is_le))
                dve.tensor_reduce(bucket[:], past[:], AX.X, ALU.add)
                link(dve.tensor_tensor(term[:], past[:], size[:].unsqueeze(1).to_broadcast(wide), ALU.mult))
                link(dve.tensor_reduce(begin[:], term[:], AX.X, ALU.add))
                dve.tensor_copy(begin_i[:], begin[:])
                link(dve.tensor_tensor(term[:], past[:], tiles[:].unsqueeze(1).to_broadcast(wide), ALU.mult))
                dve.tensor_reduce(skip[:], term[:], AX.X, ALU.add)
                link(dve.tensor_scalar(begin_i[:], begin_i[:], 7, None, ALU.arith_shift_right))
                link(dve.tensor_copy(begin[:], begin_i[:]))
                link(dve.tensor_tensor(begin[:], begin[:], number[:], ALU.add))
                link(dve.tensor_tensor(begin[:], begin[:], skip[:], ALU.subtract))
                dve.tensor_scalar(tile_i[:], begin[:], float(ET - 1), None, ALU.min).then_inc(found, 1)
                link(dve.tensor_scalar(first_node[:], bucket[:], float(P), None, ALU.mult))
                dve.wait_ge(gathered, 16 * WG)
                pairs = got[:].rearrange("p g (e c) -> p g e c", c=2)
                dve.tensor_copy(src_w[:], pairs[:, :, :, 1])
                for g in range(WG):
                    last = dve.tensor_scalar(dst_w[:, g, :], pairs[:, g, :, 0], first_node[:, g:g + 1], None,
                                             ALU.subtract)
                last.then_inc(split, 1)
                dve.wait_ge(turned, 1)
                dve.tensor_copy(win["dst"][:], ps_dst[:])
                dve.tensor_copy(win["src"][:], ps_src[:])
                dve.tensor_copy(win["bucket"][:], ps_bucket[:])

            @block.tensor
            def _(pe):
                pe.wait_ge(split, 1)
                for g in range(WG):
                    pe.transpose(ps_dst[:, g, :], dst_w[:, g, :], c["ident"][:])
                    pe.transpose(ps_src[:, g, :], src_w[:, g, :], c["ident"][:])
                    last = pe.transpose(ps_bucket[:, g, :], bucket[:, g:g + 1], c["ident"][:])
                last.then_inc(turned, 1)

TB = 5
TI = NT // TB
CUTS = [(0, 3 * P), (3 * P, TB * P)]
EPS_LN = 1e-5
EPS_ATT = 1e-6
SLOPE = 0.2
GW = 4
NG = NW // GW
RING = 4


class Steps:

    def __init__(self, eng, sem, per, turn):
        self.eng, self.sem, self.per, self.turn, self.done = eng, sem, per, turn, 0

    def link(self, ins):
        self.done += 1
        ins.then_inc(self.sem, 1)
        self.eng.wait_ge(self.sem, self.turn * self.per + self.done)

    def end(self):
        assert self.done == self.per, self.done


def layer_norm_all(nc, c, x, xn, x_loaded):
    with ExitStack() as stack:
        m = Memory(nc, stack, "n_")
        stats, moments, scale = m.sb("stats", [P, NT, 6]), m.sb("moments", [P, NT, 2]), m.sb("scale", [P, NT])
        varied, shift = m.sb("varied", [P, NT]), m.sb("shift", [P, NT])
        measured, known, scaled, varied_set, shifted = (m.sem(n) for n in
                                                        "measured known scaled varied_set shifted".split())
        turns = [slice(TB * i, TB * i + TB) for i in range(TI)]
        with nc.Block() as block:

            @block.gpsimd
            def _(pool):
                for i, t in enumerate(turns):
                    pool.wait_ge(known, i + 1)
                    pool.tensor_scalar(varied[:, t], moments[:, t, 1], EPS_LN, None, ALU.add).then_inc(varied_set, 1)
                    pool.wait_ge(varied_set, i + 1)
                    pool.tensor_tensor(scale[:, t], varied[:, t], c["half"][0:P, t], ALU.pow).then_inc(scaled, 1)

            @block.vector
            def _(dve):
                def shift_turn(i):
                    dve.wait_ge(scaled, i + 1)
                    t = turns[i]
                    dve.scalar_tensor_tensor(shift[:, t], moments[:, t, 0], -1.0, scale[:, t], ALU.mult,
                                             ALU.mult).then_inc(shifted, 1)

                dve.wait_ge(x_loaded, 16)
                for i in range(TI):
                    for t in range(TB * i, TB * i + TB):
                        last = dve.bn_stats(stats[:, t, :], x[:, t, :])
                    last.then_inc(measured, 1)
                    if i >= 1:
                        shift_turn(i - 1)
                    dve.wait_ge(measured, i + 1)
                    for t in range(TB * i, TB * i + TB):
                        last = dve.bn_aggr(moments[:, t, :], stats[:, t, :])
                    last.then_inc(known, 1)
                shift_turn(TI - 1)

            @block.scalar
            def _(act):
                for i in range(TI):
                    act.wait_ge(shifted, i + 1)
                    for t in range(TB * i, TB * i + TB):
                        act.activation(xn[:, t, :], x[:, t, :], ACT.Identity, bias=shift[:, t:t + 1],
                                       scale=scale[:, t:t + 1])


def project(nc, c, xn, w, heads, rows, scores, qt, kv_block, acc, res):
    with ExitStack() as stack:
        m = Memory(nc, stack, "p_")
        wa, wb, wq = m.sb("wa", [128, KD, 2 * D]), m.sb("wb", [128, KD, 2 * D]), m.sb("wq", [128, KD, D])
        ws = m.sb("ws", [128, KD, 16])
        att, prod = m.sb("att", [128, 2, D]), m.sb("prod", [128, 2, D])
        bias = m.sb("bias", [P, 2, D])
        xs = m.sb("xs", [P, TB, D])
        xt = m.sb("xt", [128, KD, TB * P])
        row = m.sb("row", [P, TB, ROW])
        kneg, kexp, kel = m.sb("kneg", [P, D]), m.sb("kexp", [P, D]), m.sb("kel", [P, TB, D])
        vext = m.sb("vext", [P, TB, KD, 129])
        qneg, qexp = m.sb("qneg", [128, 2, 3 * P]), m.sb("qexp", [128, 2, 3 * P])
        kv_sum = m.sb("kv_sum", [128, KD, 129])
        ps_t, ps_q = m.ps("ps_t", [128, 2, 512]), m.ps("ps_q", [128, 2, 512])
        ps_a, ps_b = m.ps("ps_a", [P, 2 * D]), m.ps("ps_b", [P, 2 * D])
        ps_s, ps_kvp = m.ps("ps_s", [P, 512]), m.ps("ps_kvp", [128, 512])
        names = ("loaded weighted step staged turned xt_ready h_ready row_ready scores_read kv_ready kneg_ready "
                 "kexp_ready kel_ready v_ready kvp_ready kvp_read q_ready qneg_ready qexp_ready q_read cleared")
        s = {n: m.sem(n) for n in names.split()}
        stored = [m.sem(f"stored{j}") for j in range(TB)]
        hd = D // heads
        has_res = res is not None
        loads = 6 + 3 * has_res
        nb = 2 * D if has_res else D

        with nc.Block() as block:

            @block.sync
            def _(sp):
                halves = "(k p) n -> p k n"
                sp.dma_start(wa[:, :, 0:D], w["proj"].rearrange(halves, p=128)).then_inc(s["loaded"], 16)
                sp.dma_start(wa[:, :, D:2 * D], w["v"].rearrange(halves, p=128)).then_inc(s["loaded"], 16)
                sp.dma_start(wb[:, :, 0:D], w["k"].rearrange(halves, p=128)).then_inc(s["loaded"], 16)
                sp.dma_start(wq[:], w["q"].rearrange("(k p) n -> p k n", p=128)).then_inc(s["loaded"], 16)
                sp.dma_start(att[:, 0, :], w["att_src"].partition_broadcast(128)).then_inc(s["loaded"], 16)
                sp.dma_start(att[:, 1, :], w["att_dst"].partition_broadcast(128)).then_inc(s["loaded"], 16)
                if has_res:
                    sp.dma_start(wb[:, :, D:2 * D], w["res"].rearrange(halves, p=128)).then_inc(s["loaded"], 16)
                    sp.dma_start(bias[:, 0, :], w["bias_gat"].partition_broadcast(P)).then_inc(s["loaded"], 16)
                    sp.dma_start(bias[:, 1, :], w["b_res"].partition_broadcast(P)).then_inc(s["loaded"], 16)
                for j in range(TB):
                    sp.sem_inc(stored[j], 16)
                with sp.Fori(0, TI) as i:
                    for j in range(TB):
                        sp.wait_ge(s["row_ready"], i * TB + j + 2)
                        sp.wait_ge(s["scores_read"], i * TB + j + 2)
                        sp.dma_start(rows[bass.ds((i * TB + j) * P, P), :], row[:, j, :]).then_inc(stored[j], 16)
                for j in range(TB):
                    sp.wait_ge(stored[j], 16 * (TI + 1))

            @block.gpsimd
            def _(pool):
                with pool.Fori(0, TI) as i:
                    for j in range(TB):
                        pool.wait_ge(s["turned"], i * TB + j + 1)
                        pool.tensor_copy(xs[:, j:j + 1, :], xn[:, bass.ds(i * TB + j, 1), :]).then_inc(s["staged"], 1)

            @block.tensor
            def _(pe):
                def turn_rows(i, j):
                    pe.wait_ge(s["staged"], i * TB + j + 1)
                    if j == 0:
                        pe.wait_ge(s["xt_ready"], i * TB + 1)
                    for k in range(KD):
                        last = pe.transpose(ps_t[:, j % 2, k * P:(k + 1) * P],
                                            xs[:, j, 128 * k:128 * k + 128], c["ident"][0:P, 0:P])
                    last.then_inc(s["turned"], 1)

                def products(i, j):
                    n = i * TB + j
                    xt_j = [xt[:, k, j * P:(j + 1) * P] for k in range(KD)]
                    pe.wait_ge(s["xt_ready"], n + 2)
                    pe.wait_ge(s["row_ready"], n + 1)
                    pe.wait_ge(s["v_ready"], n + 1)
                    for k in range(KD):
                        pe.matmul(ps_a[:], xt_j[k], wa[:, k, :], start=(k == 0), stop=(k == KD - 1))
                    pe.wait_ge(s["scores_read"], n + 1)
                    for k in range(KD):
                        last = pe.matmul(ps_s[:, 0:16], xt_j[k], ws[:, k, :], start=(k == 0), stop=(k == KD - 1))
                    last.then_inc(s["h_ready"], 1)
                    pe.wait_ge(s["kel_ready"], n + 1)
                    for k in range(KD):
                        last = pe.matmul(ps_b[:, 0:nb], xt_j[k], wb[:, k, 0:nb], start=(k == 0), stop=(k == KD - 1))
                    last.then_inc(s["kv_ready"], 1)

                def outer(i, j):
                    n = i * TB + j
                    pe.wait_ge(s["kel_ready"], n + 2)
                    pe.wait_ge(s["v_ready"], n + 2)
                    pe.wait_ge(s["kvp_read"], n + 1)
                    for k in range(KD):
                        last = pe.matmul(ps_kvp[:, k * 129:k * 129 + 129], kel[:, j, 128 * k:128 * k + 128],
                                         vext[:, j, k, :], start=True, stop=True)
                    last.then_inc(s["kvp_ready"], 1)

                for free in ("xt_ready", "row_ready", "scores_read", "v_ready", "kel_ready", "kvp_read"):
                    pe.sem_inc(s[free], 1)
                pe.sem_inc(s["q_read"], 2)
                pe.sem_inc(s["q_ready"], 4)
                pe.sem_inc(s["turned"], TB)
                pe.wait_ge(s["weighted"], 1)
                with pe.Fori(0, TI) as i:
                    turn_rows(i, 0)
                    for j in range(TB):
                        if j + 1 < TB:
                            turn_rows(i, j + 1)
                        products(i, j)
                        if j >= 1:
                            outer(i, j - 1)
                    for q in range(4):
                        lo, hi = CUTS[q // 2]
                        half = q % 2
                        pe.wait_ge(s["q_read"], i * 4 + q + 1)
                        for k in range(KD):
                            last = pe.matmul(ps_q[:, q % 2, 0:hi - lo], wq[:, k, 128 * half:128 * half + 128],
                                             xt[:, k, lo:hi], start=(k == 0), stop=(k == KD - 1))
                        last.then_inc(s["q_ready"], 1)
                    outer(i, TB - 1)

            @block.scalar
            def _(act):
                def take_xt(i, j):
                    n = i * TB + j
                    act.wait_ge(s["turned"], n + 1 + TB)
                    act.copy(xt[:, :, j * P:(j + 1) * P],
                             ps_t[:, j % 2, 0:KD * P].rearrange("p (k n) -> p k n", k=KD)).then_inc(s["xt_ready"], 1)

                def evacuate(i, j):
                    n = i * TB + j
                    act.wait_ge(s["h_ready"], n + 1)
                    act.wait_ge(stored[j], i * 16 + 16)
                    if has_res:
                        act.copy(acc[:, bass.ds(n, 1), 0:D], ps_a[:, 0:D])
                    act.copy(row[:, j, 0:D], ps_a[:, 0:D]).then_inc(s["row_ready"], 1)
                    act.activation(vext[:, j, :, 0:128], ps_a[:, D:2 * D].rearrange("p (k n) -> p k n", k=KD),
                                   ACT.Copy, scale=w["v_scale"]).then_inc(s["v_ready"], 1)
                    act.wait_ge(s["kneg_ready"], n + 1)
                    act.activation(kexp[:], kneg[:], ACT.Exp).then_inc(s["kexp_ready"], 1)

                with act.Fori(0, TI) as i:
                    act.wait_ge(s["q_ready"], i * 4 + 4)
                    take_xt(i, 0)
                    for j in range(TB):
                        if j + 1 < TB:
                            take_xt(i, j + 1)
                        evacuate(i, j)
                    for q in range(4):
                        lo, hi = CUTS[q // 2]
                        act.wait_ge(s["qneg_ready"], i * 4 + q + 1)
                        act.activation(qexp[:, q % 2, 0:hi - lo], qneg[:, q % 2, 0:hi - lo],
                                       ACT.Exp).then_inc(s["qexp_ready"], 1)

            @block.vector
            def _(dve):
                link = link_of(dve, s["step"])
                dve.memset(vext[:, :, :, 128:129], 1.0)
                dve.memset(kv_sum[:], 0.0)
                link(dve.memset(ws[:], 0.0))
                dve.wait_ge(s["loaded"], 16 * loads)
                for k in range(KD):
                    for side in range(2):
                        link(dve.tensor_tensor(prod[:, side, :], wa[:, k, 0:D], att[:, side, :], ALU.mult))
                        last = dve.tensor_reduce(ws[:, k, 8 * side:8 * side + heads],
                                                 prod[:, side, :].rearrange("p (h d) -> p h d", h=heads), AX.X, ALU.add)
                last.then_inc(s["weighted"], 1)
                if has_res:
                    link(dve.tensor_tensor(bias[:, 0, :], bias[:, 0, :], bias[:, 1, :], ALU.add))

                def scores_and_keys(i, j):
                    n = i * TB + j
                    dve.wait_ge(s["h_ready"], n + 1)
                    dve.wait_ge(stored[j], i * 16 + 16)
                    dve.tensor_copy(row[:, j, D:D + 8], ps_s[:, 0:8])
                    dve.tensor_copy(scores[:, bass.ds(n, 1), :], ps_s[:, 0:16]).then_inc(s["scores_read"], 1)
                    dve.wait_ge(s["kv_ready"], n + 1)
                    dve.tensor_scalar(kneg[:], ps_b[:, 0:D], 0.0, None, ALU.min).then_inc(s["kneg_ready"], 1)
                    if has_res:
                        dve.tensor_tensor(res[:, bass.ds(n, 1), :], ps_b[:, D:2 * D], bias[:, 0, :], ALU.add)
                    dve.wait_ge(s["kexp_ready"], n + 1)
                    dve.scalar_tensor_tensor(kel[:, j, :], ps_b[:, 0:D], 0.0, kexp[:], ALU.max,
                                             ALU.add).then_inc(s["kel_ready"], 1)

                def add_outer(i, j):
                    n = i * TB + j
                    dve.wait_ge(s["kvp_read"], n + 1)
                    dve.wait_ge(s["kvp_ready"], n + 1)
                    dve.tensor_tensor(kv_sum[:], kv_sum[:], ps_kvp[:, 0:KD * 129].rearrange("p (k n) -> p k n", k=KD),
                                      ALU.add).then_inc(s["kvp_read"], 1)

                def queries(i, q):
                    lo, hi = CUTS[q // 2]
                    dve.wait_ge(s["q_ready"], i * 4 + q + 5)
                    dve.tensor_scalar(qneg[:, q % 2, 0:hi - lo], ps_q[:, q % 2, 0:hi - lo], 0.0, None,
                                      ALU.min).then_inc(s["qneg_ready"], 1)

                def queries_done(i, q):
                    lo, hi = CUTS[q // 2]
                    dve.wait_ge(s["qexp_ready"], i * 4 + q + 1)
                    dve.scalar_tensor_tensor(qt[:, q % 2, bass.ds(i * (TB * P) + lo, hi - lo)],
                                             ps_q[:, q % 2, 0:hi - lo], 0.0, qexp[:, q % 2, 0:hi - lo],
                                             ALU.max, ALU.add).then_inc(s["q_read"], 1)

                with dve.Fori(0, TI) as i:
                    for j in range(TB):
                        scores_and_keys(i, j)
                        if j >= 1:
                            add_outer(i, j - 1)
                    queries(i, 0)
                    for q in range(4):
                        if q + 1 < 4:
                            queries(i, q + 1)
                        queries_done(i, q)
                    add_outer(i, TB - 1)

        with nc.Block() as block:

            @block.vector
            def _(dve):
                dve.memset(kv_block[:], 0.0).then_inc(s["cleared"], 1)
                dve.wait_ge(s["cleared"], 1)
                for q in range(4):
                    rows_q = slice(32 * q, 32 * q + 32)
                    dve.tensor_copy(kv_block[rows_q, :, 32 * q:32 * q + 32], kv_sum[rows_q, :, 32 * q:32 * q + 32])
                    dve.tensor_copy(kv_block[rows_q, :, 128 + q:129 + q], kv_sum[rows_q, :, 128:129])


HEADROOM = 60.0


def bound_scores(nc, c, heads, scores, dst_parts, acc, acc_odd, self_loops):
    with ExitStack() as stack:
        m = Memory(nc, stack, "b_")
        most, most_t, diag = m.sb("most", [P, 8]), m.sb("most_t", [8, 1]), m.sb("diag", [8, 8])
        z = m.sb("z", [P, NT, 8])
        own, bound = m.sb("own", [P, NT, 8]), m.sb("bound", [P, NT, 8])
        dst_side = m.sb("dst_side", [128, NT + 1, 16])
        ps_t, ps_b = m.ps("ps_t", [8, P]), m.ps("ps_b", [P, 8])
        step, reduced, turned, spread, logit, weight = (m.sem(n) for n in
                                                        "step reduced turned spread logit weight".split())
        diagonal = m.sem("diagonal")
        with nc.Block() as block:

            @block.vector
            def _(dve):
                link = link_of(dve, step)
                dve.memset(dst_side[:, NT:NT + 1, :], 0.0)
                dve.tensor_reduce(most[:], scores[:, :, 0:8].rearrange("p t h -> p h t"), AX.X, ALU.max).then_inc(reduced, 1)
                dve.tensor_copy(dst_side[0:P, 0:NT, 0:8], scores[:, :, 8:16])
                dve.wait_ge(turned, 1)
                link(dve.tensor_reduce(most_t[:], ps_t[:], AX.X, ALU.max))
                dve.tensor_scalar(diag[:], c["ident"][0:8, 0:8], most_t[:], None, ALU.mult).then_inc(diagonal, 1)
                dve.wait_ge(spread, 1)
                link(dve.tensor_copy(most[:], ps_b[:]))
                link(dve.tensor_tensor(z[:], scores[:, :, 8:16], most[:].unsqueeze(1).to_broadcast([P, NT, 8]), ALU.add))
                link(dve.scalar_tensor_tensor(dst_side[0:P, 0:NT, 8:16], z[:], SLOPE, z[:], ALU.mult, ALU.max))
                link(dve.tensor_scalar(dst_side[0:P, 0:NT, 8:16], dst_side[0:P, 0:NT, 8:16], HEADROOM, None, ALU.subtract))
                dve.tensor_copy(bound[:], dst_side[0:P, 0:NT, 8:16])
                for part in range(3):
                    cols = slice(16 * part, 16 * part + 16)
                    link(dve.tensor_copy(dst_parts[0:P, :, cols], dst_side[0:P]))
                    if part < 2:
                        link(dve.tensor_tensor(dst_side[0:P], dst_side[0:P], dst_parts[0:P, :, cols], ALU.subtract))
                if not self_loops:
                    dve.memset(acc[:], 0.0)
                else:
                    link(dve.tensor_tensor(z[:], scores[:, :, 0:8], scores[:, :, 8:16], ALU.add))
                    link(dve.scalar_tensor_tensor(own[:], z[:], SLOPE, z[:], ALU.mult, ALU.max))
                    dve.tensor_tensor(own[:], own[:], bound[:], ALU.subtract).then_inc(logit, 1)
                    dve.wait_ge(weight, 1)
                    for h in range(heads):
                        cols = slice(h * (D // heads), (h + 1) * (D // heads))
                        dve.tensor_tensor(acc[:, 0:NT, cols], acc[:, 0:NT, cols],
                                          z[:, :, h:h + 1].to_broadcast([P, NT, D // heads]), ALU.mult)
                    dve.tensor_copy(acc[:, 0:NT, D:D + 8], z[:])
                    dve.memset(acc[:, NT:NT + 1, :], 0.0)

            @block.gpsimd
            def _(pool):
                pool.memset(acc_odd[:], 0.0)

            @block.scalar
            def _(act):
                if self_loops:
                    act.wait_ge(logit, 1)
                    act.activation(z[:], own[:], ACT.Exp).then_inc(weight, 1)

            @block.tensor
            def _(pe):
                pe.wait_ge(reduced, 1)
                pe.transpose(ps_t[:], most[:], c["ident"][0:P, 0:P]).then_inc(turned, 1)
                pe.wait_ge(diagonal, 1)
                pe.matmul(ps_b[:], c["ones"][0:8, 0:P], diag[:], start=True, stop=True).then_inc(spread, 1)


def edges(nc, c, heads, rows, win, dst_parts, acc, acc_odd):
    hd = D // heads
    with ExitStack() as stack:
        m = Memory(nc, stack, "e_")
        idx = m.sb("idx", [128, 2, RING * GW], I32)
        got = m.sb("got", [128, RING, GW, ROW])
        hot = m.sb("hot", [128, RING, GW, 128])
        hot_t = m.sb("hot_t", [128, 2, GW, 128], BF16)
        z, lk = m.sb("z", [128, GW, heads]), m.sb("lk", [128, GW, heads])
        logit = m.sb("logit", [128, GW, heads])
        ps_t = m.ps("ps_t", [128, GW, 128])
        ps_d = m.ps("ps_d", [128, 2, 512])
        ps_m = m.ps("ps_m", [128, GW, 512])
        names = "indexed rounds hot_ready hot_turned hot_t_ready dst_ready summed logit_ready weight_ready weighed scattered added"
        s = {n: m.sem(n) for n in names.split()}
        gathered = [m.sem(f"gathered{r}") for r in range(RING)]
        flat_src = win["src"][:].rearrange("p g e -> p (g e)")
        flat_dst = win["dst"][:].rearrange("p g e -> p (g e)")
        flat_bucket = win["bucket"][:].rearrange("p g e -> p (g e)")

        with nc.Block() as block:

            @block.gpsimd
            def _(pool):
                def gather(g, copies, half, r, first=False):
                    if not first:
                        pool.wait_ge(s["scattered"], g * GW - (RING - 1) * GW)
                    if r == 0:
                        pool.tensor_copy(idx[:, half, :], flat_src[:, bass.ds(g * GW, RING * GW)]).then_inc(s["indexed"], 1)
                        pool.wait_ge(s["indexed"], copies)
                    pool.sem_inc(s["rounds"], 1)
                    for j in range(GW):
                        at = r * GW + j
                        pool.indirect_dma_start(out=got[:, r, j, :], out_offset=None, in_=rows,
                                                in_offset=bass.IndirectOffsetOnAxis(ap=idx[:, half, at:at + 1], axis=0)
                                                ).then_inc(gathered[r], 16)

                for k in range(2 * RING):
                    gather(k, k // RING + 1, k // RING, k % RING, k < RING)
                with pool.Fori(1, NG // (2 * RING)) as i:
                    for k in range(2 * RING):
                        gather(i * (2 * RING) + k, i * 2 + k // RING + 1, k // RING, k % RING)
                gather(NG, NG // RING + 1, 0, 0)

            @block.tensor
            def _(pe):
                def turn_hot(g, r):
                    pe.wait_ge(s["hot_ready"], g + 1)
                    for j in range(GW):
                        last = pe.transpose(ps_t[:, j, :], hot[:, r, j, :], c["ident"][:])
                    last.then_inc(s["hot_turned"], 1)

                def spread_dst(g, r):
                    buckets = small_numbers(nc, mybir.EngineType.PE, flat_bucket[0:1, bass.ds(g * GW, GW)], NT)
                    pe.wait_ge(s["hot_t_ready"], g + 1)
                    for j in range(GW):
                        for part in range(3):
                            last = pe.matmul(ps_d[:, r % 2, 16 * j:16 * j + 16], hot_t[0:P, r % 2, j, :],
                                             dst_parts[0:P, bass.ds(buckets[j], 1), 16 * part:16 * part + 16],
                                             start=(part == 0), stop=(part == 2))
                    last.then_inc(s["dst_ready"], 1)

                def scatter(g, r, first):
                    pe.wait_ge(s["weighed"], g + 1)
                    for j in range(GW):
                        if not first:
                            pe.wait_ge(s["added"], g * GW + j - GW + 1)
                        pe.matmul(ps_m[:, j, 0:ROW], hot[:, r, j, :], got[:, r, j, :], start=True,
                                  stop=True).then_inc(s["scattered"], 1)

                def step(g, r, first=False):
                    turn_hot(g + 2, (r + 2) % RING)
                    scatter(g, r, first)
                    spread_dst(g + 2, (r + 2) % RING)

                for r in range(2):
                    turn_hot(r, r)
                    spread_dst(r, r)
                for r in range(RING):
                    step(r, r, r == 0)
                with pe.Fori(1, NG // RING) as i:
                    for r in range(RING):
                        step(i * RING + r, r)

            @block.scalar
            def _(act):
                def take_hot_t(g, r):
                    act.wait_ge(s["hot_turned"], g + 1)
                    act.copy(hot_t[:, r % 2, :, :], ps_t[:]).then_inc(s["hot_t_ready"], 1)

                def raise_logits(g, r):
                    act.wait_ge(s["logit_ready"], g + 1)
                    act.activation(got[:, r, :, D:D + heads], logit[:], ACT.Exp).then_inc(s["weight_ready"], 1)

                def step(g, r):
                    take_hot_t(g + 2, (r + 2) % RING)
                    raise_logits(g + 1, (r + 1) % RING)

                take_hot_t(0, 0)
                take_hot_t(1, 1)
                raise_logits(0, 0)
                for r in range(RING):
                    step(r, r)
                with act.Fori(1, NG // RING) as i:
                    for r in range(RING):
                        step(i * RING + r, r)

            @block.vector
            def _(dve):
                def mark(g, r):
                    dve.tensor_tensor(hot[:, r, :, :], c["count"][:, 0:128].unsqueeze(1).to_broadcast([128, GW, 128]),
                                      flat_dst[:, bass.ds(g * GW, GW)].unsqueeze(2).to_broadcast([128, GW, 128]),
                                      ALU.is_equal).then_inc(s["hot_ready"], 1)

                def logits(g, r, rows_in):
                    dst = ps_d[:, r % 2, 0:16 * GW].rearrange("p (w c) -> p w c", c=16)
                    dve.wait_ge(gathered[r], rows_in)
                    dve.wait_ge(s["dst_ready"], g + 1)
                    dve.tensor_tensor(z[:], got[:, r, :, D:D + heads], dst[:, :, 0:heads], ALU.add).then_inc(s["summed"], 1)
                    dve.wait_ge(s["summed"], g * 2 + 1)
                    dve.scalar_tensor_tensor(lk[:], z[:], SLOPE, z[:], ALU.mult, ALU.max).then_inc(s["summed"], 1)
                    dve.wait_ge(s["summed"], g * 2 + 2)
                    dve.tensor_tensor(logit[:], lk[:], dst[:, :, 8:8 + heads], ALU.subtract).then_inc(s["logit_ready"], 1)

                def weigh(g, r):
                    dve.wait_ge(s["weight_ready"], g + 1)
                    h = got[:, r, :, 0:D].rearrange("p w (h d) -> p w h d", h=heads)
                    dve.tensor_tensor(h, h, got[:, r, :, D:D + heads].unsqueeze(3).to_broadcast([128, GW, heads, hd]),
                                      ALU.mult).then_inc(s["weighed"], 1)

                def add(g, first=False):
                    buckets = small_numbers(nc, mybir.EngineType.DVE, flat_bucket[0:1, bass.ds(g * GW, GW)], NT)
                    for j in range(GW):
                        at = (acc, acc_odd)[j % 2][:, bass.ds(buckets[j], 1), 0:D + heads]
                        if not first or j >= 2:
                            dve.wait_ge(s["added"], g * GW + j - 1)
                        dve.wait_ge(s["scattered"], g * GW + j + 1)
                        dve.tensor_tensor(at, at, ps_m[0:P, j:j + 1, 0:D + heads], ALU.add).then_inc(s["added"], 1)

                def step(g, r, turn, next_turn):
                    weigh(g, r)
                    if not isinstance(turn, int) or r > 0:
                        add(g - 1, isinstance(turn, int) and r == 1)
                    mark(g + 3, (r + 3) % RING)
                    logits(g + 1, (r + 1) % RING, (next_turn if r == RING - 1 else turn) * (16 * GW) + 16 * GW)

                for r in range(3):
                    mark(r, r)
                logits(0, 0, 16 * GW)
                for r in range(RING):
                    step(r, r, 0, 1)
                with dve.Fori(1, NG // RING) as i:
                    for r in range(RING):
                        step(i * RING + r, r, i, i + 1)
                add(NG - 1)
                dve.wait_ge(s["added"], NG * GW)
                dve.tensor_tensor(acc[:, 0:NT, 0:D + heads], acc[:, 0:NT, 0:D + heads], acc_odd[:, 0:NT, 0:D + heads], ALU.add)

TINY = 1e-37


def wide(ap, shape):
    return ap.unsqueeze(1).to_broadcast(shape)


class Norm:

    def __init__(self, m, name):
        self.stats, self.moments = m.sb(name + "_stats", [P, TB, 6]), m.sb(name + "_moments", [P, TB, 2])
        self.varied, self.scale = m.sb(name + "_varied", [P, TB]), m.sb(name + "_scale", [P, TB])
        self.known, self.varied_set, self.scaled, self.hold = (m.sem(f"{name}_{n}") for n in
                                                               "known varied_set scaled hold".split())

    def raise_all(self, pool, c, i):
        pool.wait_ge(self.known, i + 1)
        pool.tensor_tensor(self.varied[:], self.moments[:, :, 1], c["eps"][0:P, 0:TB], ALU.add).then_inc(self.varied_set, 1)
        pool.wait_ge(self.varied_set, i + 1)
        pool.tensor_tensor(self.scale[:], self.varied[:], c["half"][0:P, 0:TB], ALU.pow).then_inc(self.scaled, 1)

    def take_moments(self, dve, steps, src):
        for j in range(TB):
            last = dve.bn_stats(self.stats[:, j, :], src[:, j, :])
        steps.link(last)
        dve.sem_inc(self.hold, 1)
        for j in range(TB):
            last = dve.bn_aggr(self.moments[:, j, :], self.stats[:, j, :])
        last.then_inc(self.known, 1)

    def apply(self, dve, steps, i, src, dst, gain, shift, ready):
        dve.wait_ge(self.scaled, i + 1)
        for j in range(TB):
            last = dve.scalar_tensor_tensor(dst[:, j, :], src[:, j, :], self.moments[:, j, 0:1], gain,
                                            ALU.subtract, ALU.mult)
        steps.link(last)
        for j in range(TB):
            last = dve.scalar_tensor_tensor(dst[:, j, :], dst[:, j, :], self.scale[:, j:j + 1], shift,
                                            ALU.mult, ALU.add)
            if ready is not None:
                last.then_inc(ready, 1)
        if ready is None:
            steps.link(last)


class TurnNorm:

    def __init__(self, m, c):
        self.c = c
        self.stats, self.moments = m.sb("stats", [P, TB, 6]), m.sb("moments", [P, TB, 2])
        self.varied, self.scale = m.sb("varied", [P, TB]), m.sb("scale", [P, TB])
        self.shift = m.sb("shift", [P, TB])
        self.seen, self.hold, self.known, self.varied_set, self.scaled, self.shifted, self.used = (
            m.sem(n) for n in "seen hold known varied_set scaled shifted used".split())

    def take_moments(self, dve, x, i):
        dve.sem_inc(self.hold, 1)
        for j in range(TB):
            last = dve.bn_stats(self.stats[:, j, :], x[:, bass.ds(i * TB + j, 1), :].rearrange("p t n -> p (t n)"))
        last.then_inc(self.seen, 1)
        dve.wait_ge(self.seen, i + 1)
        dve.sem_inc(self.hold, 1)
        for j in range(TB):
            last = dve.bn_aggr(self.moments[:, j, :], self.stats[:, j, :])
        last.then_inc(self.known, 1)

    def raise_variance(self, pool, i):
        pool.wait_ge(self.known, i + 1)
        pool.tensor_tensor(self.varied[:], self.moments[:, :, 1], self.c["eps"][0:P, 0:TB], ALU.add).then_inc(self.varied_set, 1)
        pool.wait_ge(self.varied_set, i + 1)
        pool.wait_ge(self.used, i * TB + TB)
        pool.tensor_tensor(self.scale[:], self.varied[:], self.c["half"][0:P, 0:TB], ALU.pow).then_inc(self.scaled, 1)

    def make_shift(self, dve, i):
        dve.wait_ge(self.scaled, i + 1)
        dve.scalar_tensor_tensor(self.shift[:], self.moments[:, :, 0], -1.0, self.scale[:], ALU.mult,
                                 ALU.mult).then_inc(self.shifted, 1)


def attend(dve, steps, i, j, ps, attended, free, scale, zz, r):
    dve.wait_ge(attended, i * TB + j + 1)
    both = ps.rearrange("p (k n) -> p k n", k=KD)
    steps.link(dve.tensor_scalar(zz[:, j], both[:, :, 128:132], scale, EPS_ATT * scale, ALU.mult, ALU.add))
    steps.link(dve.reciprocal(zz[:, j], zz[:, j]))
    dve.tensor_tensor(r[:, j, :].rearrange("p (k h d) -> p k h d", k=KD, h=4),
                      both[:, :, 0:128].rearrange("p k (h d) -> p k h d", h=4),
                      zz[:, j].unsqueeze(3).to_broadcast([P, KD, 4, 32]), ALU.mult).then_inc(free, 1)


def since(n, j):
    return n + 1 if j == 0 else n


def mix_elu_gelu(nc, c, w, x, xn, qt, kv_block):
    with ExitStack() as stack:
        m = Memory(nc, stack, "m_")
        w1, w2 = m.sb("w1", [128, KD, D]), m.sb("w2", [128, KD, D])
        b1 = m.sb("b1", [128, KD])
        rows5 = m.sb("rows5", [P, 5, D])
        qs = m.sb("qs", [128, KD, TB * P])
        zz = m.sb("zz", [P, TB, KD, 4])
        r, x1, xb = m.sb("r", [P, TB, D]), m.sb("x1", [P, TB, D]), m.sb("xb", [P, TB, D])
        r2 = m.sb("r2", [P, TB, D])
        x1t, ht = m.sb("x1t", [128, KD, TB * P]), m.sb("ht", [128, KD, TB * P])
        ps_a, ps_t = m.ps("ps_a", [P, 2, 512]), m.ps("ps_t", [128, 2, 512])
        ps_h, ps_y = m.ps("ps_h", [128, 2, 512]), m.ps("ps_y", [P, 2, 512])
        names = "loaded step1 step2 qs_ready attended att_read x1_ready turned x1t_ready hid hid_ready y_ready y_read"
        s = {n: m.sem(n) for n in names.split()}
        norm1, norm2 = Norm(m, "norm1"), Norm(m, "norm2")
        with nc.Block() as block:

            @block.sync
            def _(sp):
                halves = "(k p) n -> p k n"
                sp.dma_start(w1[:], w["w1"].rearrange(halves, p=128)).then_inc(s["loaded"], 16)
                sp.dma_start(w2[:], w["w2"].rearrange(halves, p=128)).then_inc(s["loaded"], 16)
                sp.dma_start(b1[:], w["b1"]).then_inc(s["loaded"], 16)
                for n, name in enumerate(("ln1_g", "ln1_b", "b2", "ln2_g", "ln2_b")):
                    sp.dma_start(rows5[:, n, :], w[name].partition_broadcast(P)).then_inc(s["loaded"], 16)

            @block.gpsimd
            def _(pool):
                norm1.raise_all(pool, c, 0)
                with pool.Fori(0, TI - 1) as i:
                    norm1.raise_all(pool, c, i + 1)
                    norm2.raise_all(pool, c, i)
                norm2.raise_all(pool, c, TI - 1)

            @block.scalar
            def _(act):
                def stage_queries(i, first=False):
                    if not first:
                        act.wait_ge(s["attended"], i * TB)
                    act.copy(qs[:], qt[:, :, bass.ds(i * (TB * P), TB * P)]).then_inc(s["qs_ready"], 1)

                def second(i):
                    for j in range(TB):
                        act.wait_ge(s["turned"], i * TB + j + 1)
                        act.copy(x1t[:, :, j * P:(j + 1) * P],
                                 ps_t[:, j % 2, 0:KD * P].rearrange("p (k n) -> p k n", k=KD)).then_inc(s["x1t_ready"], 1)
                    for q in range(4):
                        lo, hi = CUTS[q // 2]
                        act.wait_ge(s["hid"], i * 4 + q + 1)
                        act.activation(ht[:, q % 2, lo:hi], ps_h[:, q % 2, 0:hi - lo], ACT.Gelu,
                                       bias=b1[:, q % 2:q % 2 + 1]).then_inc(s["hid_ready"], 1)

                act.wait_ge(s["loaded"], 16 * 8)
                stage_queries(0, True)
                with act.Fori(0, TI - 1) as i:
                    stage_queries(i + 1)
                    second(i)
                second(TI - 1)

            @block.tensor
            def _(pe):
                def attention(i, j):
                    if j == 0:
                        pe.wait_ge(s["qs_ready"], i + 1)
                    pe.wait_ge(s["att_read"], since(i * TB + j, j))
                    for k in range(KD):
                        last = pe.matmul(ps_a[:, j % 2, 132 * k:132 * k + 132], qs[:, k, j * P:(j + 1) * P],
                                         kv_block[:, k, :], start=True, stop=True)
                    last.then_inc(s["attended"], 1)

                def turn(i, j):
                    pe.wait_ge(s["x1_ready"], i * TB + j + 1)
                    pe.wait_ge(s["x1t_ready"], since(i * TB + j, j))
                    for k in range(KD):
                        last = pe.transpose(ps_t[:, j % 2, k * P:(k + 1) * P], x1[:, j, 128 * k:128 * k + 128],
                                            c["ident"][0:P, 0:P])
                    last.then_inc(s["turned"], 1)

                def hidden(i, q):
                    lo, hi = CUTS[q // 2]
                    half = slice(128 * (q % 2), 128 * (q % 2) + 128)
                    pe.wait_ge(s["x1t_ready"], i * TB + hi // P + 1)
                    pe.wait_ge(s["hid_ready"], i * 4 + q + 1)
                    for k in range(KD):
                        last = pe.matmul(ps_h[:, q % 2, 0:hi - lo], w1[:, k, half], x1t[:, k, lo:hi],
                                         start=(k == 0), stop=(k == KD - 1))
                    last.then_inc(s["hid"], 1)

                def output(i, j):
                    pe.wait_ge(s["hid_ready"], i * 4 + (4 if j < 3 else 6))
                    pe.wait_ge(s["y_read"], since(i * TB + j, j))
                    for k in range(KD):
                        last = pe.matmul(ps_y[:, j % 2, 0:D], ht[:, k, j * P:(j + 1) * P], w2[:, k, :],
                                         start=(k == 0), stop=(k == KD - 1))
                    last.then_inc(s["y_ready"], 1)

                def second(i, between):
                    for j in range(TB):
                        turn(i, j)
                    between(0, 2)
                    for q in range(4):
                        hidden(i, q)
                    between(2, TB)
                    for j in range(TB):
                        output(i, j)

                for one in ("att_read", "x1t_ready", "y_read"):
                    pe.sem_inc(s[one], 1)
                pe.sem_inc(s["hid_ready"], 2)
                pe.wait_ge(s["loaded"], 16 * 8)
                for j in range(TB):
                    attention(0, j)
                with pe.Fori(0, TI - 1) as i:
                    second(i, lambda lo, hi: [attention(i + 1, j) for j in range(lo, hi)])
                second(TI - 1, lambda lo, hi: None)

            @block.vector
            def _(dve):
                def attention(i, steps):
                    for j in range(TB):
                        attend(dve, steps, i, j, ps_a[:, j % 2, 0:KD * 132], s["attended"], s["att_read"], 1.0, zz, r)
                    dve.wait_ge(s["att_read"], i * TB + TB + 1)
                    steps.link(dve.tensor_tensor(r[:], r[:], xn[:, bass.ds(i * TB, TB), :], ALU.add))

                def take_outputs(i):
                    for j in range(TB):
                        dve.wait_ge(s["y_ready"], i * TB + j + 1)
                        dve.tensor_tensor(r2[:, j, :], ps_y[:, j % 2, 0:D], xb[:, j, :], ALU.add).then_inc(s["y_read"], 1)
                    dve.wait_ge(s["y_read"], i * TB + TB + 1)

                def finish(i, steps):
                    norm2.apply(dve, steps, i, r2, r2, rows5[:, 3, :], rows5[:, 4, :], None)
                    here = x[:, bass.ds(i * TB, TB), :]
                    steps.link(dve.tensor_tensor(here, here, r2[:], ALU.add))

                def make_x1(i, steps):
                    norm1.apply(dve, steps, i, r, x1, rows5[:, 0, :], rows5[:, 1, :], s["x1_ready"])

                def shift(i, steps):
                    dve.wait_ge(s["x1_ready"], i * TB + TB)
                    steps.link(dve.tensor_tensor(xb[:], x1[:], wide(rows5[:, 2, :], [P, TB, D]), ALU.add))

                def steps1(i):
                    return Steps(dve, s["step1"], 2 * TB + 4, i)

                def steps2(i):
                    return Steps(dve, s["step2"], 4, i)

                dve.wait_ge(s["loaded"], 16 * 8)
                one = steps1(0)
                attention(0, one)
                norm1.take_moments(dve, one, r)
                make_x1(0, one)
                shift(0, one)
                one.end()
                with dve.Fori(0, TI - 1) as i:
                    one, two = steps1(i + 1), steps2(i)
                    attention(i + 1, one)
                    take_outputs(i)
                    norm1.take_moments(dve, one, r)
                    norm2.take_moments(dve, two, r2)
                    make_x1(i + 1, one)
                    finish(i, two)
                    shift(i + 1, one)
                    one.end()
                    two.end()
                take_outputs(TI - 1)
                two = steps2(TI - 1)
                norm2.take_moments(dve, two, r2)
                finish(TI - 1, two)


def mix_concat(nc, c, w, x, xn, qt, kv_block):
    K2 = 2 * KD
    MSG, ATT, XN, TURNED = 0, TB, 2 * TB, 3 * TB
    WM, OUT, TAKEN = 0, TB, 2 * TB
    with ExitStack() as stack:
        m = Memory(nc, stack, "m_")
        wm = m.sb("wm", [128, KD, D])
        w1, w2 = m.sb("w1", [128, K2, 2 * D]), m.sb("w2", [128, K2, D])
        rows4 = m.sb("rows4", [P, 4, D])
        qs = m.sb("qs", [128, KD, TB * P])
        zz = m.sb("zz", [P, TB, KD, 4])
        r, msg = m.sb("r", [P, TB, D]), m.sb("msg", [P, TB, D])
        y1, y2, xs = m.sb("y1", [P, TB, D]), m.sb("y2", [P, TB, D]), m.sb("xs", [P, TB, D])
        rt, cat = m.sb("rt", [128, KD, TB * P]), m.sb("cat", [128, K2, TB * P])
        ht = m.sb("ht", [128, K2, TB * P])
        ps_a, ps_t = m.ps("ps_a", [P, 2, 512]), m.ps("ps_t", [128, 2, 512])
        ps_h, ps_y = m.ps("ps_h", [128, 2, 512]), m.ps("ps_y", [P, 2, 512])
        names = ("loaded step1 step2 staged qs_ready attended att_read turned t_ready hid hid_ready y_ready y_read "
                 "msg_ready")
        s = {n: m.sem(n) for n in names.split()}
        norm1, norm2 = Norm(m, "norm1"), Norm(m, "norm2")

        def turned_before(i, place):
            return i * TURNED + 2 * TB + place

        def taken_before(i, place):
            return i * TAKEN + TB + place

        with nc.Block() as block:

            @block.sync
            def _(sp):
                halves = "(k p) n -> p k n"
                sp.dma_start(wm[:], w["wm"].rearrange(halves, p=128)).then_inc(s["loaded"], 16)
                sp.dma_start(w1[:], w["w1"].rearrange(halves, p=128)).then_inc(s["loaded"], 16)
                sp.dma_start(w2[:], w["w2"].rearrange(halves, p=128)).then_inc(s["loaded"], 16)
                for n, name in enumerate(("g1", "b1", "g2", "b2")):
                    sp.dma_start(rows4[:, n, :], w[name].partition_broadcast(P)).then_inc(s["loaded"], 16)

            @block.gpsimd
            def _(pool):
                pool.tensor_copy(xs[:], xn[:, 0:TB, :]).then_inc(s["staged"], 1)
                norm1.raise_all(pool, c, 0)
                with pool.Fori(0, TI - 1) as i:
                    pool.wait_ge(s["turned"], turned_before(i, 0))
                    pool.tensor_copy(xs[:], xn[:, bass.ds((i + 1) * TB, TB), :]).then_inc(s["staged"], 1)
                    norm1.raise_all(pool, c, i + 1)
                    norm2.raise_all(pool, c, i)
                norm2.raise_all(pool, c, TI - 1)

            @block.scalar
            def _(act):
                def take_turned(i, place, to):
                    for j in range(TB):
                        act.wait_ge(s["turned"], turned_before(i, place + j) + 1)
                        act.copy(to[:, :, j * P:(j + 1) * P],
                                 ps_t[:, (place + j) % 2, 0:KD * P].rearrange("p (k n) -> p k n", k=KD)
                                 ).then_inc(s["t_ready"], 1)

                def take_y(i, place, to):
                    for j in range(TB):
                        act.wait_ge(s["y_ready"], taken_before(i, place + j) + 1)
                        act.copy(to[:, j, :], ps_y[:, (place + j) % 2, 0:D]).then_inc(s["y_read"], 1)

                def take_hidden(i, lo_q, hi_q):
                    for q in range(lo_q, hi_q):
                        lo, hi = CUTS[q // 4]
                        act.wait_ge(s["hid"], i * 8 + q + 1)
                        act.activation(ht[:, q % 4, lo:hi], ps_h[:, q % 2, 0:hi - lo], ACT.Relu).then_inc(s["hid_ready"], 1)

                def stage_queries(t):
                    act.copy(qs[:], qt[:, :, bass.ds(t * (TB * P), TB * P)]).then_inc(s["qs_ready"], 1)

                def step(i, more):
                    if more:
                        act.wait_ge(s["attended"], (i + 1) * TB)
                        stage_queries(i + 1)
                    take_turned(i, MSG, cat[:, KD:K2, :])
                    take_hidden(i, 0, 6)
                    if more:
                        take_turned(i, ATT, rt)
                    take_hidden(i, 6, 8)
                    if more:
                        take_y(i, WM, y1)
                        take_turned(i, XN, cat[:, 0:KD, :])
                    if not more:
                        act.wait_ge(s["step2"], 5 * i)
                    take_y(i, OUT if more else WM, y2)

                stage_queries(0)
                take_turned(-1, ATT, rt)
                take_y(-1, OUT, y1)
                take_turned(-1, XN, cat[:, 0:KD, :])
                with act.Fori(0, TI - 1) as i:
                    step(i, True)
                step(TI - 1, False)

            @block.tensor
            def _(pe):
                def turn(i, place, of, ready, count):
                    for j in range(TB):
                        before = turned_before(i, place + j)
                        pe.wait_ge(ready, count(j))
                        pe.wait_ge(s["t_ready"], before + 2 if place + j == 0 else before + 1)
                        for k in range(KD):
                            last = pe.transpose(ps_t[:, (place + j) % 2, k * P:(k + 1) * P],
                                                of[:, j, 128 * k:128 * k + 128], c["ident"][0:P, 0:P])
                        last.then_inc(s["turned"], 1)

                def attention(t, tiles):
                    if 0 in tiles:
                        pe.wait_ge(s["qs_ready"], t + 1)
                    for j in tiles:
                        pe.wait_ge(s["att_read"], since(t * TB + j, j))
                        for k in range(KD):
                            last = pe.matmul(ps_a[:, j % 2, 132 * k:132 * k + 132], qs[:, k, j * P:(j + 1) * P],
                                             kv_block[:, k, :], start=True, stop=True)
                        last.then_inc(s["attended"], 1)

                def turn_attention(i):
                    turn(i, ATT, r, s["att_read"], lambda j: (i + 1) * TB + j + 2)

                def messages(i, place):
                    for j in range(TB):
                        before = taken_before(i, place + j)
                        pe.wait_ge(s["t_ready"], turned_before(i, ATT + j) + 3)
                        pe.wait_ge(s["y_read"], before + 1)
                        for k in range(KD):
                            last = pe.matmul(ps_y[:, (place + j) % 2, 0:D], rt[:, k, j * P:(j + 1) * P], wm[:, k, :],
                                             start=(k == 0), stop=(k == KD - 1))
                        last.then_inc(s["y_ready"], 1)

                def turn_input(i):
                    turn(i, XN, xs, s["staged"], lambda j: i + 2)

                def hidden(i, q):
                    lo, hi = CUTS[q // 4]
                    part = slice(128 * (q % 4), 128 * (q % 4) + 128)
                    pe.wait_ge(s["t_ready"], turned_before(i, MSG + hi // P) + 2)
                    pe.wait_ge(s["hid_ready"], i * 8 + q + 1)
                    for k in range(K2):
                        last = pe.matmul(ps_h[:, q % 2, 0:hi - lo], w1[:, k, part], cat[:, k, lo:hi],
                                         start=(k == 0), stop=(k == K2 - 1))
                    last.then_inc(s["hid"], 1)

                def output(i, place):
                    for j in range(TB):
                        pe.wait_ge(s["hid_ready"], i * 8 + (6 if j < 3 else 10))
                        pe.wait_ge(s["y_read"], taken_before(i, place + j) + 1)
                        for k in range(K2):
                            last = pe.matmul(ps_y[:, (place + j) % 2, 0:D], ht[:, k, j * P:(j + 1) * P], w2[:, k, :],
                                             start=(k == 0), stop=(k == K2 - 1))
                        last.then_inc(s["y_ready"], 1)

                def step(i, more):
                    turn(i, MSG, msg, s["msg_ready"], lambda j: i * TB + j + 1)
                    if more:
                        attention(i + 1, range(0, 2))
                    for q in range(4):
                        hidden(i, q)
                    if more:
                        attention(i + 1, range(2, 4))
                    hidden(i, 4)
                    if more:
                        attention(i + 1, range(4, TB))
                    hidden(i, 5)
                    if more:
                        turn_attention(i)
                    hidden(i, 6)
                    hidden(i, 7)
                    if more:
                        messages(i, WM)
                        turn_input(i)
                    output(i, OUT if more else WM)

                for one, n in (("att_read", 1), ("t_ready", 2), ("hid_ready", 2), ("y_read", 2)):
                    pe.sem_inc(s[one], n)
                pe.wait_ge(s["loaded"], 16 * 7)
                attention(0, range(TB))
                turn_attention(-1)
                messages(-1, OUT)
                turn_input(-1)
                with pe.Fori(0, TI - 1) as i:
                    step(i, True)
                step(TI - 1, False)

            @block.vector
            def _(dve):
                def attention(t, steps):
                    for j in range(TB):
                        attend(dve, steps, t, j, ps_a[:, j % 2, 0:KD * 132], s["attended"], s["att_read"], 1.0 / N, zz, r)

                def make_msg(t, taken, steps):
                    dve.wait_ge(s["y_read"], taken)
                    norm1.take_moments(dve, steps, y1)
                    norm1.apply(dve, steps, t, y1, msg, rows4[:, 0, :], rows4[:, 1, :], s["msg_ready"])
                    steps.end()

                def finish(i, taken, steps):
                    here = x[:, bass.ds(i * TB, TB), :]
                    steps.link(dve.tensor_tensor(here, here, xn[:, bass.ds(i * TB, TB), :], ALU.add))
                    dve.wait_ge(s["y_read"], taken)
                    norm2.take_moments(dve, steps, y2)
                    norm2.apply(dve, steps, i, y2, y2, rows4[:, 2, :], rows4[:, 3, :], None)
                    steps.link(dve.tensor_tensor(here, here, y2[:], ALU.add))
                    steps.end()

                def steps1(t):
                    return Steps(dve, s["step1"], 2 * TB + 2, t)

                def steps2(i):
                    return Steps(dve, s["step2"], 5, i)

                dve.wait_ge(s["loaded"], 16 * 7)
                one = steps1(0)
                attention(0, one)
                make_msg(0, TB + 2, one)
                with dve.Fori(0, TI - 1) as i:
                    one = steps1(i + 1)
                    attention(i + 1, one)
                    make_msg(i + 1, taken_before(i, WM + TB) + 2, one)
                    finish(i, taken_before(i, OUT + TB) + 2, steps2(i))
                finish(TI - 1, taken_before(TI - 1, WM + TB) + 2, steps2(TI - 1))


def finish_gat_relu(nc, c, w, x, acc):
    with ExitStack() as stack:
        m = Memory(nc, stack, "f_")
        bias, den = m.sb("bias", [P, D]), m.sb("den", [P, NT, 8])
        loaded, step, divided, biased = (m.sem(n) for n in "loaded step divided biased".split())
        turns = [slice(TB * i, TB * i + TB) for i in range(TI)]
        with nc.Block() as block:

            @block.sync
            def _(sp):
                sp.dma_start(bias[:], w["gat_bias"].partition_broadcast(P)).then_inc(loaded, 16)

            @block.gpsimd
            def _(pool):
                pool.wait_ge(loaded, 16)
                for i, t in enumerate(turns):
                    pool.wait_ge(divided, i + 1)
                    pool.tensor_tensor(acc[:, t, 0:D], acc[:, t, 0:D], wide(bias[:], [P, TB, D]), ALU.add
                                       ).then_inc(biased, 1)

            @block.vector
            def _(dve):
                link = link_of(dve, step)

                def finish(i):
                    t = turns[i]
                    dve.wait_ge(biased, i + 1)
                    dve.scalar_tensor_tensor(x[:, t, :], acc[:, t, 0:D], 0.0, x[:, t, :], ALU.max, ALU.add)

                link(dve.tensor_scalar(den[:], acc[:, 0:NT, D:D + 8], TINY, None, ALU.max))
                link(dve.reciprocal(den[:], den[:]))
                for i, t in enumerate(turns):
                    heads = acc[:, t, 0:D].rearrange("p t (h d) -> p t h d", h=8)
                    dve.tensor_tensor(heads, heads, den[:, t, :].unsqueeze(3).to_broadcast([P, TB, 8, 32]),
                                      ALU.mult).then_inc(divided, 1)
                    if i >= 3:
                        finish(i - 3)
                for i in range(TI - 3, TI):
                    finish(i)


def finish_gat_norm(nc, c, w, x, acc, res):
    with ExitStack() as stack:
        m = Memory(nc, stack, "f_")
        both, den = m.sb("both", [P, 2, D]), m.sb("den", [P, NT, 4])
        stats, moments = m.sb("stats", [P, NT, 6]), m.sb("moments", [P, NT, 2])
        varied, scale, shift = m.sb("varied", [P, NT]), m.sb("scale", [P, NT]), m.sb("shift", [P, NT])
        names = "loaded step measured known varied_set scaled shifted normed beta_added"
        s = {n: m.sem(n) for n in names.split()}
        turns = [slice(TB * i, TB * i + TB) for i in range(TI)]
        with nc.Block() as block:

            @block.sync
            def _(sp):
                sp.dma_start(both[:, 0, :], w["gamma"].partition_broadcast(P)).then_inc(s["loaded"], 16)
                sp.dma_start(both[:, 1, :], w["beta"].partition_broadcast(P)).then_inc(s["loaded"], 16)

            @block.gpsimd
            def _(pool):
                pool.wait_ge(s["loaded"], 32)
                for i, t in enumerate(turns):
                    pool.tensor_tensor(x[:, t, :], x[:, t, :], wide(both[:, 1, :], [P, TB, D]), ALU.add
                                       ).then_inc(s["beta_added"], 1)
                    pool.wait_ge(s["known"], i + 1)
                    pool.tensor_scalar(varied[:, t], moments[:, t, 1], EPS_LN, None, ALU.add).then_inc(s["varied_set"], 1)
                    pool.wait_ge(s["varied_set"], i + 1)
                    pool.tensor_tensor(scale[:, t], varied[:, t], c["half"][0:P, t], ALU.pow).then_inc(s["scaled"], 1)

            @block.scalar
            def _(act):
                for i in range(TI):
                    act.wait_ge(s["shifted"], i + 1)
                    for t in range(TB * i, TB * i + TB):
                        last = act.activation(acc[:, t, 0:D], acc[:, t, 0:D], ACT.Identity, bias=shift[:, t:t + 1],
                                              scale=scale[:, t:t + 1])
                    last.then_inc(s["normed"], 1)

            @block.vector
            def _(dve):
                link = link_of(dve, s["step"])

                def shift_turn(i):
                    dve.wait_ge(s["scaled"], i + 1)
                    t = turns[i]
                    dve.scalar_tensor_tensor(shift[:, t], moments[:, t, 0], -1.0, scale[:, t], ALU.mult,
                                             ALU.mult).then_inc(s["shifted"], 1)

                def finish(i):
                    here = acc[:, turns[i], 0:D]
                    dve.wait_ge(s["normed"], i + 1)
                    link(dve.tensor_tensor(here, here, wide(both[:, 0, :], [P, TB, D]), ALU.mult))
                    dve.wait_ge(s["beta_added"], i + 1)
                    dve.tensor_tensor(x[:, turns[i], :], x[:, turns[i], :], here, ALU.add)

                link(dve.tensor_scalar(den[:], acc[:, 0:NT, D:D + 4], TINY, None, ALU.max))
                link(dve.reciprocal(den[:], den[:]))
                dve.wait_ge(s["loaded"], 32)
                for i, turn in enumerate(turns):
                    here = acc[:, turn, 0:D]
                    heads = here.rearrange("p t (h d) -> p t h d", h=4)
                    link(dve.tensor_tensor(heads, heads, den[:, turn, :].unsqueeze(3).to_broadcast([P, TB, 4, 64]),
                                           ALU.mult))
                    link(dve.tensor_tensor(here, here, res[:, turn, :], ALU.add))
                    for t in range(TB * i, TB * i + TB):
                        last = dve.bn_stats(stats[:, t, :], acc[:, t, 0:D])
                    last.then_inc(s["measured"], 1)
                    if i >= 1:
                        shift_turn(i - 1)
                    dve.wait_ge(s["measured"], i + 1)
                    for t in range(TB * i, TB * i + TB):
                        last = dve.bn_aggr(moments[:, t, :], stats[:, t, :])
                    last.then_inc(s["known"], 1)
                    if i >= 2:
                        finish(i - 2)
                shift_turn(TI - 1)
                finish(TI - 2)
                finish(TI - 1)


def slot_tiles(items, experts):
    return (items + experts * 127) // 128


def gate(nc, c, wg, bg, experts, x, normed, logits, of_layer):
    with ExitStack() as stack:
        m = Memory(nc, stack, "g_")
        wgs, bias = m.sb("wgs", [128, KD, experts]), m.sb("bias", [P, experts])
        xs, xt = m.sb("xs", [P, TB, D]), m.sb("xt", [128, TB, KD * P])
        ps_t, ps_g = m.ps("ps_t", [128, 2, 512]), m.ps("ps_g", [P, 2, 512])
        names = "loaded turned xt_ready gated read stored"
        s = {n: m.sem(n) for n in names.split()}
        norm = TurnNorm(m, c)
        with nc.Block() as block:

            @block.sync
            def _(sp):
                sp.dma_start(wgs[:], wg.rearrange("(k p) n -> p k n", p=128)).then_inc(s["loaded"], 16)
                sp.dma_start(bias[:], bg.partition_broadcast(P)).then_inc(s["loaded"], 16)
                sp.sem_inc(s["stored"], 16)
                with sp.Fori(0, TI) as i:
                    sp.wait_ge(norm.used, i * TB + 2 * TB)
                    sp.dma_start(normed[bass.ds(i * (TB * P), TB * P), :].rearrange("(t p) n -> p t n", p=P), xs[:]
                                 ).then_inc(s["stored"], 16)
                of_layer.start_loads(sp)
                sp.wait_ge(s["stored"], 16 * TI + 16)

            @block.gpsimd
            def _(pool):
                pool.sem_inc(norm.used, TB)
                with pool.Fori(0, TI) as i:
                    norm.raise_variance(pool, i)

            @block.scalar
            def _(act):
                with act.Fori(0, TI) as i:
                    act.wait_ge(norm.shifted, i + 1)
                    act.wait_ge(s["stored"], i * 16 + 16)
                    for j in range(TB):
                        act.wait_ge(s["turned"], i * TB + j + 1)
                        act.activation(xs[:, j, :], x[:, bass.ds(i * TB + j, 1), :].rearrange("p t n -> p (t n)"),
                                       ACT.Identity, bias=norm.shift[:, j:j + 1], scale=norm.scale[:, j:j + 1]
                                       ).then_inc(norm.used, 1)
                    for j in range(TB):
                        act.wait_ge(s["turned"], i * TB + j + 1 + TB)
                        act.copy(xt[:, j, :], ps_t[:, j % 2, 0:KD * P]).then_inc(s["xt_ready"], 1)

            @block.tensor
            def _(pe):
                pe.sem_inc(s["turned"], TB)
                pe.sem_inc(s["xt_ready"], 1)
                pe.sem_inc(s["read"], 1)
                pe.wait_ge(s["loaded"], 32)

                def turn(i, j):
                    n = i * TB + j
                    pe.wait_ge(norm.used, n + 1 + TB)
                    pe.wait_ge(s["xt_ready"], since(n, j))
                    for k in range(KD):
                        last = pe.transpose(ps_t[:, j % 2, k * P:(k + 1) * P], xs[:, j, 128 * k:128 * k + 128],
                                            c["ident"][0:P, 0:P])
                    last.then_inc(s["turned"], 1)

                with pe.Fori(0, TI) as i:
                    turn(i, 0)
                    for j in range(TB):
                        n = i * TB + j
                        if j + 1 < TB:
                            turn(i, j + 1)
                        pe.wait_ge(s["xt_ready"], n + 2)
                        pe.wait_ge(s["read"], since(n, j))
                        for k in range(KD):
                            last = pe.matmul(ps_g[:, j % 2, 0:experts], xt[:, j, k * P:(k + 1) * P], wgs[:, k, :],
                                             start=(k == 0), stop=(k == KD - 1))
                        last.then_inc(s["gated"], 1)

            @block.vector
            def _(dve):
                def take_logits(i):
                    for j in range(TB):
                        n = i * TB + j
                        dve.wait_ge(s["gated"], n + 1)
                        dve.tensor_tensor(logits[:, bass.ds(n, 1), :], ps_g[:, j % 2, 0:experts], bias[:],
                                          ALU.add).then_inc(s["read"], 1)

                dve.wait_ge(s["loaded"], 32)
                norm.take_moments(dve, x, 0)
                norm.make_shift(dve, 0)
                with dve.Fori(0, TI - 1) as i:
                    norm.take_moments(dve, x, i + 1)
                    take_logits(i)
                    norm.make_shift(dve, i + 1)
                take_logits(TI - 1)


def choose(nc, c, experts, picks, logits, chosen, prob):
    with ExitStack() as stack:
        m = Memory(nc, stack, "c_")
        best = m.sb("best", [P, picks, NT])
        rank, named = m.sb("rank", [P, NT, experts]), m.sb("named", [P, NT, experts])
        gap, e, total = m.sb("gap", [P, NT]), m.sb("e", [P, NT]), m.sb("total", [P, NT])
        step, gapped, raised = m.sem("step"), m.sem("gapped"), m.sem("raised")
        full = [P, NT, experts]
        with nc.Block() as block:

            @block.scalar
            def _(act):
                if picks == 2:
                    act.wait_ge(gapped, 1)
                    act.activation(e[:], gap[:], ACT.Exp).then_inc(raised, 1)

            @block.vector
            def _(dve):
                link = link_of(dve, step)
                link(dve.tensor_scalar(rank[:], c["count"][0:P, 0:experts].unsqueeze(1).to_broadcast(full),
                                       float(experts), None, ALU.subtract))
                for q in range(picks):
                    link(dve.tensor_reduce(best[:, q, :], logits[:], AX.X, ALU.max))
                    link(dve.tensor_tensor(named[:], logits[:], best[:, q, :].unsqueeze(2).to_broadcast(full), ALU.is_equal))
                    link(dve.tensor_tensor(named[:], named[:], rank[:], ALU.mult))
                    link(dve.tensor_reduce(chosen[:, :, q:q + 1].rearrange("p t q -> p (t q)") if picks == 1 else chosen[:, :, q],
                                           named[:], AX.X, ALU.min))
                    if q + 1 < picks:
                        link(dve.tensor_tensor(named[:], rank[:], chosen[:, :, q].unsqueeze(2).to_broadcast(full), ALU.is_equal))
                        link(dve.scalar_tensor_tensor(logits[:], named[:], -3e38, logits[:], ALU.mult, ALU.add))
                link(dve.tensor_scalar(chosen[:], chosen[:], float(experts), None, ALU.add))
                if picks == 2:
                    dve.tensor_tensor(gap[:], best[:, 1, :], best[:, 0, :], ALU.subtract).then_inc(gapped, 1)
                    dve.wait_ge(raised, 1)
                    link(dve.tensor_scalar(total[:], e[:], 1.0, None, ALU.add))
                    link(dve.reciprocal(prob[:, :, 0], total[:]))
                    dve.tensor_tensor(prob[:, :, 1], e[:], prob[:, :, 0], ALU.mult)


def route(nc, c, experts, picks, chosen, place_i, expert_i, token_i):
    C = NT * picks
    T = slot_tiles(N * picks, experts)
    W = C // TI
    with ExitStack() as stack:
        m = Memory(nc, stack, "r_")
        member, rank = m.sb("member", [P, experts, C]), m.sb("rank", [P, experts, C])
        tally = m.sb("tally", [P, experts])
        cnt, prior = m.sb("cnt", [128, experts]), m.sb("prior", [P, experts])
        cnt_i = m.sb("cnt_i", [128, experts], I32)
        tiles, upto = m.sb("tiles", [128, experts]), m.sb("upto", [128, experts])
        base, place_f = m.sb("base", [P, experts]), m.sb("place_f", [P, C])
        past, expert_f = m.sb("past", [1, T + 2, experts]), m.sb("expert_f", [1, T + 2])
        node_i, node = m.sb("node_i", [P, NT, picks], I32), m.sb("node", [P, NT, picks])
        within_i, within = m.sb("within_i", [P, C], I32), m.sb("within", [P, C])
        tile_i, tile = m.sb("tile_i", [P, C], I32), m.sb("tile", [P, C])
        hot_within = m.sb("hot_within", [P, 2, W, 128])
        hot_tile, tile_node = m.sb("hot_tile", [P, W, T]), m.sb("tile_node", [P, 2, W, T])
        ps_cnt, ps_prior, ps_list = m.ps("ps_cnt", [128, experts]), m.ps("ps_prior", [P, experts]), m.ps("ps_list", [128, T])
        s = {n: m.sem(n) for n in "numbered step tallied summed marked listed".split()}
        with nc.Block() as block:

            @block.gpsimd
            def _(pool):
                pool.iota(node_i[:], [[P, NT], [0, picks]], base=0, channel_multiplier=1).then_inc(s["numbered"], 1)

            @block.vector
            def _(dve):
                link = link_of(dve, s["step"])
                full = [P, experts, C]
                link(dve.tensor_tensor(member[:], chosen[:].rearrange("p t q -> p (t q)").unsqueeze(1).to_broadcast(full),
                                       c["count"][0:P, 0:experts].unsqueeze(2).to_broadcast(full), ALU.is_equal))
                link(dve.tensor_reduce(tally[:], member[:], AX.X, ALU.add))
                dve.sem_inc(s["tallied"], 1)
                flat = "p b c -> p (b c)"
                link(dve.tensor_tensor_scan(rank[:].rearrange(flat), member[:].rearrange(flat),
                                            member[:].rearrange(flat), 0.0, ALU.add, ALU.bypass))
                dve.wait_ge(s["numbered"], 1)
                dve.tensor_copy(node[:], node_i[:])
                dve.wait_ge(s["summed"], 1)
                dve.tensor_copy(prior[:], ps_prior[:])
                link(dve.tensor_copy(cnt[:], ps_cnt[:]))
                link(dve.tensor_scalar(cnt_i[:], cnt[:], 127.0, None, ALU.add))
                link(dve.tensor_scalar(cnt_i[:], cnt_i[:], 7, None, ALU.arith_shift_right))
                link(dve.tensor_copy(tiles[:], cnt_i[:]))
                link(dve.tensor_tensor_scan(upto[:], tiles[:], tiles[:], 0.0, ALU.add, ALU.bypass))
                link(dve.tensor_tensor(base[:], upto[0:P, :], tiles[0:P, :], ALU.subtract))
                link(dve.tensor_scalar(base[:], base[:], 128.0, -1.0, ALU.mult, ALU.add))
                link(dve.tensor_tensor(base[:], base[:], prior[:], ALU.add))
                link(dve.tensor_tensor(base[:, 1:experts], base[:, 1:experts], rank[:, 0:experts - 1, C - 1], ALU.subtract))
                link(dve.tensor_tensor(rank[:], rank[:], base[:].unsqueeze(2).to_broadcast(full), ALU.add))
                link(dve.tensor_tensor(rank[:], rank[:], member[:], ALU.mult))
                link(dve.tensor_reduce(place_f[:], rank[:].rearrange("p b c -> p c b"), AX.X, ALU.add))
                link(dve.tensor_copy(place_i[:], place_f[:]))
                dve.tensor_scalar(within_i[:], place_i[:], 127, None, ALU.bitwise_and)
                link(dve.tensor_scalar(tile_i[:], place_i[:], 7, None, ALU.arith_shift_right))
                dve.tensor_copy(within[:], within_i[:])
                link(dve.tensor_copy(tile[:], tile_i[:]))
                for i in range(TI):
                    cols = slice(W * i, W * i + W)
                    if i >= 2:
                        dve.wait_ge(s["listed"], i - 1)
                    dve.tensor_tensor(hot_within[:, i % 2], c["count"][0:P, 0:128].unsqueeze(1).to_broadcast([P, W, 128]),
                                      within[:, cols].unsqueeze(2).to_broadcast([P, W, 128]), ALU.is_equal
                                      ).then_inc(s["marked"], 1)
                    link(dve.tensor_tensor(hot_tile[:], c["count"][0:P, 0:T].unsqueeze(1).to_broadcast([P, W, T]),
                                           tile[:, cols].unsqueeze(2).to_broadcast([P, W, T]), ALU.is_equal))
                    link(dve.tensor_tensor(tile_node[:, i % 2], hot_tile[:],
                                           node[:].rearrange("p t q -> p (t q)")[:, cols].unsqueeze(2).to_broadcast([P, W, T]),
                                           ALU.mult))
                    dve.sem_inc(s["marked"], 1)
                tall = [1, T + 2, experts]
                link(dve.tensor_tensor(past[:], upto[0:1, :].unsqueeze(1).to_broadcast(tall),
                                       c["count"][0:1, 0:T + 2].unsqueeze(2).to_broadcast(tall), ALU.is_le))
                link(dve.tensor_reduce(expert_f[:], past[:], AX.X, ALU.add))
                dve.tensor_scalar(expert_i[:], expert_f[:], float(experts - 1), None, ALU.min)
                dve.memset(token_i[:, T:T + 2], 0)
                dve.wait_ge(s["listed"], TI)
                dve.tensor_copy(token_i[:, 0:T], ps_list[:])

            @block.tensor
            def _(pe):
                pe.wait_ge(s["tallied"], 1)
                pe.matmul(ps_cnt[:], c["ones"][0:P, :], tally[:], start=True, stop=True)
                pe.matmul(ps_prior[:], c["before"][0:P, 0:P], tally[:], start=True, stop=True).then_inc(s["summed"], 1)
                for i in range(TI):
                    pe.wait_ge(s["marked"], 2 * i + 2)
                    for q in range(W):
                        last = pe.matmul(ps_list[:], hot_within[:, i % 2, q, :], tile_node[:, i % 2, q, :],
                                         start=(i + q == 0), stop=(i * W + q == C - 1))
                    last.then_inc(s["listed"], 1)


class Experts:

    def __init__(self, nc, m, w, experts, hidden):
        self.w, self.experts, self.hidden, self.hc = w, experts, hidden, max(hidden // 128, 1)
        self.w1 = m.sb("w1", [128, experts, KD, hidden])
        self.w2 = m.sb("w2", [min(hidden, 128), experts, self.hc, D])
        self.b1, self.b2 = m.sb("b1", [min(hidden, 128), experts, self.hc]), m.sb("b2", [128, experts, D])
        self.loaded = m.sem("weights_loaded")
        self.loads = 2 + (2 * self.experts if self.hc > 1 else KD + 1)

    def start_loads(self, sp):
        w = self.w
        if self.hc > 1:
            for e in range(self.experts):
                sp.dma_start(self.w1[:, e, :, :], w["w1"][e].rearrange("(k p) n -> p k n", p=128)).then_inc(self.loaded, 16)
                sp.dma_start(self.w2[:, e, :, :], w["w2"][e].rearrange("(k p) n -> p k n", p=128)).then_inc(self.loaded, 16)
        else:
            for k in range(KD):
                sp.dma_start(self.w1[:, :, k, :], w["w1"][:, 128 * k:128 * k + 128, :].rearrange("e p n -> p e n")
                             ).then_inc(self.loaded, 16)
            sp.dma_start(self.w2[:, :, 0, :], w["w2"].rearrange("e p n -> p e n")).then_inc(self.loaded, 16)
        sp.dma_start(self.b1[:], w["b1"]).then_inc(self.loaded, 16)
        sp.dma_start(self.b2[:], w["b2"].partition_broadcast(128)).then_inc(self.loaded, 16)


def gather_tokens(pool, s, gathered, got, idx, normed, token_i, t, r, ring):
    pool.wait_ge(s["x_turned"], t + 1)
    pool.tensor_copy(idx[:, r:r + 1], token_i[:, bass.ds(t, 1)]).then_inc(s["indexed"], 1)
    pool.wait_ge(s["indexed"], t + 1)
    pool.sem_inc(s["rounds"], 1)
    pool.indirect_dma_start(out=got[:, r, :], out_offset=None, in_=normed,
                            in_offset=bass.IndirectOffsetOnAxis(ap=idx[:, r:r + 1], axis=0)).then_inc(gathered[r], 16)


def experts_wide(nc, c, x, normed, token_i, expert_i, results):
    H, HC = x.hidden, x.hc
    T = slot_tiles(2 * N, x.experts)
    with ExitStack() as stack:
        m = Memory(nc, stack, "x_")
        idx = m.sb("idx", [128, 2], I32)
        got, xt = m.sb("got", [128, 2, D]), m.sb("xt", [128, D])
        hs, ht = m.sb("hs", [128, H]), m.sb("ht", [128, HC, 128])
        y, b1 = m.sb("y", [128, 2, D]), m.sb("b1", [128, 2, HC])
        ps_x, ps_h = m.ps("ps_x", [128, 512]), m.ps("ps_h", [128, 2, 512])
        ps_t, ps_y = m.ps("ps_t", [128, 2, 512]), m.ps("ps_y", [128, 2, 512])
        names = "indexed rounds x_turned xt_ready hid hs_ready h_turned ht_ready y_ready y_read b1_ready"
        s = {n: m.sem(n) for n in names.split()}
        gathered = [m.sem(f"gathered{r}") for r in range(2)]
        stored = [m.sem(f"stored{r}") for r in range(2)]

        def tile_experts(engine, i):
            if isinstance(i, int):
                return (None, *small_numbers(nc, engine, expert_i[0:1, 0:2], x.experts - 1))
            return small_numbers(nc, engine, expert_i[0:1, bass.ds(i * 2 - 1, 3)], x.experts - 1)

        with nc.Block() as block:

            @block.sync
            def _(sp):
                for r in range(2):
                    sp.sem_inc(stored[r], 16)
                with sp.Fori(0, T // 2) as i:
                    for r in range(2):
                        t = i * 2 + r
                        sp.wait_ge(s["y_read"], t + 3)
                        sp.dma_start(results[bass.ds(t * 128, 128), :], y[:, r, :]).then_inc(stored[r], 16)
                for r in range(2):
                    sp.wait_ge(stored[r], 16 * (T // 2 + 1))

            @block.gpsimd
            def _(pool):
                with pool.Fori(0, T // 2) as i:
                    for r in range(2):
                        gather_tokens(pool, s, gathered, got, idx, normed, token_i, i * 2 + r, r, 2)
                gather_tokens(pool, s, gathered, got, idx, normed, token_i, T, 0, 2)

            @block.tensor
            def _(pe):
                def turn_x(r, rows_in):
                    pe.wait_ge(gathered[r], rows_in)
                    for k in range(KD):
                        last = pe.transpose(ps_x[:, 128 * k:128 * k + 128], got[:, r, 128 * k:128 * k + 128], c["ident"][:])
                    last.then_inc(s["x_turned"], 1)

                def first_product(t, e):
                    pe.wait_ge(s["xt_ready"], t + 1)
                    for half in range(2):
                        for k in range(KD):
                            last = pe.matmul(ps_h[:, half, :], xt[:, 128 * k:128 * k + 128],
                                             x.w1[:, bass.ds(e, 1), k, 512 * half:512 * half + 512],
                                             start=(k == 0), stop=(k == KD - 1))
                        last.then_inc(s["hid"], 1)

                def turn_h(t):
                    for half in range(2):
                        pe.wait_ge(s["hs_ready"], t * 2 + half + 1)
                        for q in range(4):
                            last = pe.transpose(ps_t[:, half, 128 * q:128 * q + 128],
                                                hs[:, 512 * half + 128 * q:512 * half + 128 * q + 128], c["ident"][:])
                        last.then_inc(s["h_turned"], 1)

                def second_product(t, r, e):
                    pe.wait_ge(s["y_read"], t + 1)
                    for q in range(HC):
                        if q % 4 == 0:
                            pe.wait_ge(s["ht_ready"], t * 2 + q // 4 + 1)
                        last = pe.matmul(ps_y[:, r, 0:D], ht[:, q, :], x.w2[:, bass.ds(e, 1), q, :],
                                         start=(q == 0), stop=(q == HC - 1))
                    last.then_inc(s["y_ready"], 1)

                def turn_of_two(i):
                    numbers = tile_experts(mybir.EngineType.PE, i)
                    for r in range(2):
                        t = i * 2 + r
                        first_product(t, numbers[r + 1])
                        turn_x(1 - r, (i + r) * 16 + 16)
                        if numbers[r] is not None:
                            second_product(t - 1, 1 - r, numbers[r])
                        turn_h(t)
                    return numbers[2]

                pe.sem_inc(s["x_turned"], 2)
                pe.sem_inc(s["y_read"], 2)
                turn_x(0, 16)
                pe.wait_ge(x.loaded, 16 * x.loads)
                turn_of_two(0)
                with pe.Fori(1, T // 2) as i:
                    turn_of_two(i)
                last = small_numbers(nc, mybir.EngineType.PE, expert_i[0:1, T - 1:T], x.experts - 1)
                second_product(T - 1, 1, last[0])

            @block.scalar
            def _(act):
                def take_x(t):
                    act.wait_ge(s["x_turned"], t + 3)
                    act.copy(xt[:], ps_x[:, 0:D]).then_inc(s["xt_ready"], 1)

                take_x(0)
                with act.Fori(0, T // 2) as i:
                    for r in range(2):
                        t = i * 2 + r
                        for half in range(2):
                            act.wait_ge(s["hid"], t * 2 + half + 1)
                            act.copy(hs[:, 512 * half:512 * half + 512], ps_h[:, half, :]).then_inc(s["hs_ready"], 1)
                            if half == 0:
                                take_x(t + 1)

            @block.vector
            def _(dve):
                def stage_b1(t, r, e):
                    dve.tensor_copy(b1[:, r, :], x.b1[:, bass.ds(e, 1), :].rearrange("p e q -> p (e q)")
                                    ).then_inc(s["b1_ready"], 1)

                def take_turned(t, r):
                    dve.wait_ge(s["b1_ready"], t + 1)
                    for half in range(2):
                        dve.wait_ge(s["h_turned"], t * 2 + half + 1)
                        for q in range(4):
                            last = dve.tensor_scalar(ht[:, 4 * half + q, :], ps_t[:, half, 128 * q:128 * q + 128],
                                                     b1[:, r, 4 * half + q:4 * half + q + 1], 0.0, ALU.add, ALU.max)
                        last.then_inc(s["ht_ready"], 1)

                def add_b2(t, r, e, stores):
                    dve.wait_ge(s["y_ready"], t + 1)
                    dve.wait_ge(stored[r], stores)
                    dve.tensor_tensor(y[:, r, :], ps_y[:, r, 0:D], x.b2[:, bass.ds(e, 1), :], ALU.add).then_inc(s["y_read"], 1)

                def turn_of_two(i):
                    numbers = tile_experts(mybir.EngineType.DVE, i)
                    for r in range(2):
                        t = i * 2 + r
                        stage_b1(t, r, numbers[r + 1])
                        if numbers[r] is not None:
                            add_b2(t - 1, 1 - r, numbers[r], (i + r) * 16)
                        take_turned(t, r)

                dve.wait_ge(x.loaded, 16 * x.loads)
                turn_of_two(0)
                with dve.Fori(1, T // 2) as i:
                    turn_of_two(i)
                last = small_numbers(nc, mybir.EngineType.DVE, expert_i[0:1, T - 1:T], x.experts - 1)
                add_b2(T - 1, 1, last[0], T // 2 * 16)


def experts_narrow(nc, c, x, normed, token_i, expert_i, results):
    H = x.hidden
    T = slot_tiles(N, x.experts)
    assert T % 4 == 0
    with ExitStack() as stack:
        m = Memory(nc, stack, "x_")
        idx = m.sb("idx", [128, 4], I32)
        got, xt = m.sb("got", [128, 4, D]), m.sb("xt", [128, 2, D])
        hs, ht = m.sb("hs", [128, 2, H]), m.sb("ht", [H, 2, 128])
        b1 = m.sb("b1", [H, 2])
        sums, y = m.sb("sums", [128, 2, D]), m.sb("y", [128, 4, D])
        ps_x, ps_h = m.ps("ps_x", [128, 2, 512]), m.ps("ps_h", [128, 2, 512])
        ps_t, ps_y = m.ps("ps_t", [H, 2, 512]), m.ps("ps_y", [128, 2, 512])
        names = "indexed rounds rounds_pe x_turned xt_ready hid hs_ready h_turned ht_ready y_ready y_read y_done b1_ready"
        s = {n: m.sem(n) for n in names.split()}
        gathered = [m.sem(f"gathered{r}") for r in range(4)]
        stored = [m.sem(f"stored{r}") for r in range(4)]
        with nc.Block() as block:

            @block.sync
            def _(sp):
                for r in range(4):
                    sp.sem_inc(stored[r], 16)
                with sp.Fori(0, T // 4) as i:
                    for r in range(4):
                        t = i * 4 + r
                        sp.wait_ge(s["y_done"], t + 3)
                        sp.dma_start(results[bass.ds(t * 128, 128), :], y[:, r, :]).then_inc(stored[r], 16)
                for r in range(4):
                    sp.wait_ge(stored[r], 16 * (T // 4 + 1))

            @block.gpsimd
            def _(pool):
                with pool.Fori(0, T // 4) as i:
                    for r in range(4):
                        gather_tokens(pool, s, gathered, got, idx, normed, token_i, i * 4 + r, r, 4)
                for t in range(T, T + 2):
                    gather_tokens(pool, s, gathered, got, idx, normed, token_i, t, t % 4, 4)

            @block.tensor
            def _(pe):
                def turn_x(r, rows_in):
                    pe.wait_ge(gathered[r % 4], rows_in)
                    for k in range(KD):
                        last = pe.transpose(ps_x[:, r % 2, 128 * k:128 * k + 128], got[:, r % 4, 128 * k:128 * k + 128],
                                            c["ident"][:])
                    last.then_inc(s["x_turned"], 1)

                def hidden(t, r, e):
                    pe.wait_ge(s["xt_ready"], t + 1)
                    for k in range(KD):
                        last = pe.matmul(ps_h[:, r % 2, 0:H], xt[:, r % 2, 128 * k:128 * k + 128],
                                         x.w1[:, bass.ds(e, 1), k, :], start=(k == 0), stop=(k == KD - 1))
                    last.then_inc(s["hid"], 1)

                def turn_h(t, r):
                    pe.wait_ge(s["hs_ready"], t + 1)
                    pe.sem_inc(s["rounds_pe"], 1)
                    pe.transpose(ps_t[:, r % 2, 0:128], hs[:, r % 2, :], c["ident"][:]).then_inc(s["h_turned"], 1)

                def output(t, r, e):
                    pe.wait_ge(s["y_read"], t + 1)
                    pe.wait_ge(s["ht_ready"], t + 1)
                    pe.matmul(ps_y[:, r % 2, 0:D], ht[:, r % 2, :], x.w2[:, bass.ds(e, 1), 0, :], start=True,
                              stop=True).then_inc(s["y_ready"], 1)

                pe.sem_inc(s["x_turned"], 4)
                pe.sem_inc(s["y_read"], 2)
                turn_x(0, 16)
                turn_x(1, 16)
                pe.wait_ge(x.loaded, 16 * x.loads)
                first = small_numbers(nc, mybir.EngineType.PE, expert_i[0:1, 0:1], x.experts - 1)
                hidden(0, 0, first[0])
                turn_h(0, 0)
                with pe.Fori(0, T // 4) as i:
                    numbers = small_numbers(nc, mybir.EngineType.PE, expert_i[0:1, bass.ds(i * 4, 5)], x.experts - 1)
                    for r in range(4):
                        t = i * 4 + r
                        turn_x(r + 2, (i + (r + 2) // 4) * 16 + 16)
                        hidden(t + 1, r + 1, numbers[r + 1])
                        output(t, r, numbers[r])
                        turn_h(t + 1, r + 1)

            @block.scalar
            def _(act):
                def take_x(t, r):
                    act.wait_ge(s["x_turned"], t + 5)
                    act.copy(xt[:, r % 2, :], ps_x[:, r % 2, 0:D]).then_inc(s["xt_ready"], 1)

                def take_hidden(t, r):
                    act.wait_ge(s["hid"], t + 1)
                    act.copy(hs[:, r % 2, :], ps_h[:, r % 2, 0:H]).then_inc(s["hs_ready"], 1)

                def finish(t, r, stores):
                    act.wait_ge(s["y_read"], t + 3)
                    act.wait_ge(stored[r], stores)
                    act.activation(y[:, r, :], sums[:, r % 2, :], ACT.Relu).then_inc(s["y_done"], 1)

                take_x(0, 0)
                take_x(1, 1)
                take_hidden(0, 0)
                with act.Fori(0, T // 4) as i:
                    for r in range(4):
                        t = i * 4 + r
                        take_x(t + 2, r)
                        take_hidden(t + 1, r + 1)
                        finish(t, r, i * 16 + 16)

            @block.vector
            def _(dve):
                def take_turned(t, r, e):
                    dve.tensor_copy(b1[:, r % 2:r % 2 + 1], x.b1[:, bass.ds(e, 1), 0]).then_inc(s["b1_ready"], 1)
                    dve.wait_ge(s["h_turned"], t + 1)
                    dve.wait_ge(s["b1_ready"], t + 1)
                    dve.tensor_scalar(ht[:, r % 2, :], ps_t[:, r % 2, 0:128], b1[:, r % 2:r % 2 + 1], 0.0, ALU.add,
                                      ALU.max).then_inc(s["ht_ready"], 1)

                dve.sem_inc(s["y_done"], 2)
                dve.wait_ge(x.loaded, 16 * x.loads)
                first = small_numbers(nc, mybir.EngineType.DVE, expert_i[0:1, 0:1], x.experts - 1)
                take_turned(0, 0, first[0])
                with dve.Fori(0, T // 4) as i:
                    numbers = small_numbers(nc, mybir.EngineType.DVE, expert_i[0:1, bass.ds(i * 4, 5)], x.experts - 1)
                    for r in range(4):
                        t = i * 4 + r
                        take_turned(t + 1, r + 1, numbers[r + 1])
                        dve.wait_ge(s["y_ready"], t + 1)
                        dve.wait_ge(s["y_done"], t + 1)
                        dve.tensor_tensor(sums[:, r % 2, :], ps_y[:, r % 2, 0:D], x.b2[:, bass.ds(numbers[r], 1), :],
                                          ALU.add).then_inc(s["y_read"], 1)


def combine(nc, c, picks, results, place_i, prob, x, xn, out):
    with ExitStack() as stack:
        m = Memory(nc, stack, "o_")
        got = m.sb("got", [P, TB, picks, D])
        idx = m.sb("idx", [P, TB, picks], I32)
        indexed, rounds, added = m.sem("indexed"), m.sem("rounds"), m.sem("added")
        first_added, stored = m.sem("first_added"), m.sem("stored")
        fetched = [m.sem(f"fetched{j}") for j in range(TB)]
        norm = TurnNorm(m, c)
        with nc.Block() as block:

            @block.sync
            def _(sp):
                if out is not None:
                    with sp.Fori(0, TI) as i:
                        sp.wait_ge(added, i * TB + 2 * TB)
                        sp.dma_start(out[bass.ds(i * (TB * P), TB * P), :].rearrange("(t p) n -> p t n", p=P),
                                     x[:, bass.ds(i * TB, TB), :]).then_inc(stored, 16)
                    sp.wait_ge(stored, 16 * TI)

            @block.gpsimd
            def _(pool):
                def gather(i):
                    for j in range(TB):
                        n = i * TB + j
                        pool.wait_ge(added, n + 1)
                        pool.tensor_copy(idx[:, j, :], place_i[:, bass.ds(n * picks, picks)]).then_inc(indexed, 1)
                        pool.wait_ge(indexed, n + 1)
                        pool.sem_inc(rounds, 1)
                        for q in range(picks):
                            pool.indirect_dma_start(out=got[:, j, q, :], out_offset=None, in_=results,
                                                    in_offset=bass.IndirectOffsetOnAxis(ap=idx[:, j, q:q + 1], axis=0)
                                                    ).then_inc(fetched[j], 16)

                pool.sem_inc(norm.used, TB)
                gather(0)
                with pool.Fori(0, TI - 1) as i:
                    gather(i + 1)
                    if xn is not None:
                        norm.raise_variance(pool, i)
                if xn is not None:
                    norm.raise_variance(pool, TI - 1)

            @block.scalar
            def _(act):
                if xn is not None:
                    with act.Fori(0, TI) as i:
                        act.wait_ge(norm.shifted, i + 1)
                        for j in range(TB):
                            here = bass.ds(i * TB + j, 1)
                            act.activation(xn[:, here, :].rearrange("p t n -> p (t n)"),
                                           x[:, here, :].rearrange("p t n -> p (t n)"), ACT.Identity,
                                           bias=norm.shift[:, j:j + 1], scale=norm.scale[:, j:j + 1]
                                           ).then_inc(norm.used, 1)

            @block.vector
            def _(dve):
                def add(i):
                    for j in range(TB):
                        n = i * TB + j
                        at = x[:, bass.ds(n, 1), :]
                        dve.wait_ge(fetched[j], i * (16 * picks) + 16 * picks)
                        if picks == 1:
                            dve.tensor_tensor(at, at, got[:, j, 0:1, :], ALU.add).then_inc(added, 1)
                        else:
                            for q in range(2):
                                last = dve.scalar_tensor_tensor(at, got[:, j, q:q + 1, :], prob[:, bass.ds(n, 1), q], at,
                                                                ALU.mult, ALU.add)
                                if q == 0:
                                    last.then_inc(first_added, 1)
                                    dve.wait_ge(first_added, n + 1)
                            last.then_inc(added, 1)

                dve.sem_inc(added, TB)
                if xn is None:
                    with dve.Fori(0, TI) as i:
                        add(i)
                else:
                    add(0)
                    dve.wait_ge(added, 2 * TB)
                    norm.take_moments(dve, x, 0)
                    with dve.Fori(0, TI - 1) as i:
                        add(i + 1)
                        norm.make_shift(dve, i)
                        dve.wait_ge(added, i * TB + 3 * TB)
                        norm.take_moments(dve, x, i + 1)
                    norm.make_shift(dve, TI - 1)

WEIGHTS = {
    "L0_gnn_W": (D, D), "L0_gnn_att_src": (D,), "L0_gnn_att_dst": (D,), "L0_gnn_bias": (D,),
    "L0_mix_Wqkv": (D, 3 * D), "L0_mix_ln1_g": (D,), "L0_mix_ln1_b": (D,), "L0_mix_W1": (D, D),
    "L0_mix_b1": (128, KD), "L0_mix_W2": (D, D), "L0_mix_b2": (D,), "L0_mix_ln2_g": (D,), "L0_mix_ln2_b": (D,),
    "L0_ffn_Wg": (D, 8), "L0_ffn_bg": (8,), "L0_ffn_W1": (8, D, 1024), "L0_ffn_b1": (128, 8, 8),
    "L0_ffn_W2": (8, 1024, D), "L0_ffn_b2": (8, D),
    "L1_gnn_W": (D, D), "L1_gnn_a_src": (D,), "L1_gnn_a_dst": (D,), "L1_gnn_bias_gat": (D,),
    "L1_gnn_W_res": (D, D), "L1_gnn_b_res": (D,), "L1_gnn_gamma": (D,), "L1_gnn_beta": (D,),
    "L1_mix_Wq": (D, D), "L1_mix_Wk": (D, D), "L1_mix_Wv": (D, D), "L1_mix_Wm": (D, D),
    "L1_mix_W1": (2 * D, 2 * D), "L1_mix_W2": (2 * D, D), "L1_mix_g1": (D,), "L1_mix_b1": (D,),
    "L1_mix_g2": (D,), "L1_mix_b2": (D,),
    "L1_ffn_router_w": (D, 32), "L1_ffn_router_b": (32,), "L1_ffn_W1": (32, D, 64), "L1_ffn_b1": (64, 32, 1),
    "L1_ffn_W2": (32, 64, D), "L1_ffn_b2": (32, D),
}


def build_program(nc, x_in, src, dst, w, out):
    Memory.used.clear()
    Memory.semaphores.clear()
    edge_tiles = nc.dram_tensor("edge_tiles", (ET, 256), I32).ap()
    rows = nc.dram_tensor("source_rows", (N, ROW), F32).ap()
    normed = nc.dram_tensor("normed_rows", (N, D), F32).ap()
    T = slot_tiles(2 * N, 8)
    results = nc.dram_tensor("results", (T * 128, D), F32).ap()
    with ExitStack() as stack:
        keep = Memory(nc, stack, "")
        x = keep.sb("x", [P, NT, D])
        x_loaded = keep.sem("x_loaded")
        c = build_constants(nc, keep, x_in, x, x_loaded)
        ends = keep.sb("ends", [128, NT + 1])
        win = {"src": keep.sb("win_src", [128, WG, 128], I32), "dst": keep.sb("win_dst", [128, WG, 128]),
               "bucket": keep.sb("win_bucket", [1, WG, 128], I32)}
        place_i, prob = keep.sb("place", [P, NT * 2], I32), keep.sb("prob", [P, NT, 2])
        sort_edges(nc, c, src, dst, edge_tiles, ends)
        list_windows(nc, c, edge_tiles, ends, win)
        for layer in range(2):
            with ExitStack() as stack1:
                L = Memory(nc, stack1, f"l{layer}_")
                xn = L.sb("xn", [P, NT, D])
                qt, kv_block = L.sb("qt", [128, KD, N]), L.sb("kv_block", [128, KD, 132])
                if layer == 0:
                    layer_norm_all(nc, c, x, xn, x_loaded)
                else:
                    combine(nc, c, 2, results, place_i, prob, x, xn, None)
                with ExitStack() as stack2:
                    A = Memory(nc, stack2, f"a{layer}_")
                    scores, dst_parts = A.sb("scores", [P, NT, 16]), A.sb("dst_parts", [P, NT + 1, 48], BF16)
                    acc = A.sb("acc", [P, NT + 1, ROW])
                    if layer == 0:
                        qkv = w["L0_mix_Wqkv"]
                        weights = dict(proj=w["L0_gnn_W"], att_src=w["L0_gnn_att_src"], att_dst=w["L0_gnn_att_dst"],
                                       q=qkv[:, 0:D], k=qkv[:, D:2 * D], v=qkv[:, 2 * D:3 * D], v_scale=1.0)
                        project(nc, c, xn, weights, 8, rows, scores, qt, kv_block, acc, None)
                        with ExitStack() as stack3:
                            acc_odd = Memory(nc, stack3, f"b{layer}_").sb("acc_odd", [P, NT + 1, ROW])
                            bound_scores(nc, c, 8, scores, dst_parts, acc, acc_odd, False)
                            edges(nc, c, 8, rows, win, dst_parts, acc, acc_odd)
                        finish_gat_relu(nc, c, dict(gat_bias=w["L0_gnn_bias"]), x, acc)
                    else:
                        res = A.sb("res", [P, NT, D])
                        weights = dict(proj=w["L1_gnn_W"], att_src=w["L1_gnn_a_src"], att_dst=w["L1_gnn_a_dst"],
                                       q=w["L1_mix_Wq"], k=w["L1_mix_Wk"], v=w["L1_mix_Wv"], res=w["L1_gnn_W_res"],
                                       bias_gat=w["L1_gnn_bias_gat"], b_res=w["L1_gnn_b_res"], v_scale=1.0 / N)
                        project(nc, c, xn, weights, 4, rows, scores, qt, kv_block, acc, res)
                        with ExitStack() as stack3:
                            acc_odd = Memory(nc, stack3, f"b{layer}_").sb("acc_odd", [P, NT + 1, ROW])
                            bound_scores(nc, c, 4, scores, dst_parts, acc, acc_odd, True)
                            edges(nc, c, 4, rows, win, dst_parts, acc, acc_odd)
                        finish_gat_norm(nc, c, dict(gamma=w["L1_gnn_gamma"], beta=w["L1_gnn_beta"]), x, acc, res)
                if layer == 0:
                    mixer = dict(w1=w["L0_mix_W1"], b1=w["L0_mix_b1"], w2=w["L0_mix_W2"], b2=w["L0_mix_b2"],
                                 ln1_g=w["L0_mix_ln1_g"], ln1_b=w["L0_mix_ln1_b"],
                                 ln2_g=w["L0_mix_ln2_g"], ln2_b=w["L0_mix_ln2_b"])
                    mix_elu_gelu(nc, c, mixer, x, xn, qt, kv_block)
                else:
                    mixer = dict(wm=w["L1_mix_Wm"], w1=w["L1_mix_W1"], w2=w["L1_mix_W2"], g1=w["L1_mix_g1"],
                                 b1=w["L1_mix_b1"], g2=w["L1_mix_g2"], b2=w["L1_mix_b2"])
                    mix_concat(nc, c, mixer, x, xn, qt, kv_block)
            experts, picks = (8, 2) if layer == 0 else (32, 1)
            names = ("L0_ffn_Wg", "L0_ffn_bg", "L0_ffn_") if layer == 0 else ("L1_ffn_router_w", "L1_ffn_router_b", "L1_ffn_")
            with ExitStack() as stack1:
                F = Memory(nc, stack1, f"f{layer}_")
                expert_i, token_i = F.sb("expert", [1, T + 2], I32), F.sb("token", [128, T + 2], I32)
                parts = {n: w[names[2] + o] for n, o in (("w1", "W1"), ("b1", "b1"), ("w2", "W2"), ("b2", "b2"))}
                of_layer = Experts(nc, F, parts, experts, parts["w1"].shape[2])
                with ExitStack() as stack2:
                    G = Memory(nc, stack2, f"g{layer}_")
                    logits, chosen = G.sb("logits", [P, NT, experts]), G.sb("chosen", [P, NT, picks])
                    gate(nc, c, w[names[0]], w[names[1]], experts, x, normed, logits, of_layer)
                    choose(nc, c, experts, picks, logits, chosen, prob)
                    route(nc, c, experts, picks, chosen, place_i[:, 0:NT * picks], expert_i, token_i)
                run = experts_wide if layer == 0 else experts_narrow
                run(nc, c, of_layer, normed, token_i, expert_i, results)
            clear_semaphores(nc)
        combine(nc, c, 1, results, place_i[:, 0:NT], prob, x, None, out)


_TURNED = ("L0_mix_Wqkv", "L0_mix_W1", "L0_mix_W2", "L0_ffn_Wg", "L0_ffn_W1", "L0_ffn_W2", "L1_ffn_router_w")


def kernel(**inputs):
    import numpy as _np
    import concourse.bacc as _bacc
    from concourse import mybir as _mybir
    from concourse.bass_utils import run_bass_kernel_spmd as _run

    nc = _bacc.Bacc("TRN2", target_bir_lowering=False, num_devices=1)
    arrays, args = {}, {}
    for name in ("x", "src", "dst", *WEIGHTS):
        a = _np.asarray(inputs[name])
        if name in _TURNED:
            a = _np.swapaxes(a, -1, -2)
        if name == "L0_mix_b1":
            a = a.reshape(KD, 128).T
        elif name in ("L0_ffn_b1", "L1_ffn_b1"):
            a = a.reshape(a.shape[0], -1, WEIGHTS[name][0]).transpose(2, 0, 1)
        elif name in WEIGHTS:
            a = a.reshape(WEIGHTS[name])
        arrays[f"in_{name}"] = _np.ascontiguousarray(a)
        args[name] = nc.dram_tensor(f"in_{name}", a.shape, _mybir.dt.from_np(a.dtype), kind="ExternalInput").ap()
    out = nc.dram_tensor("out_x", (N, D), F32, kind="ExternalOutput").ap()
    build_program(nc, args["x"], args["src"], args["dst"], {n: args[n] for n in WEIGHTS}, out)
    r = _run(nc, [arrays], core_ids=[0])
    return r.results[0]["out_x"]
```
